# Optimizing a Trainium2 kernel written in Bass

```python
import numpy as np
import jax
import jax.numpy as jnp

def _softmax(x, axis=-1):
    return jax.nn.softmax(x, axis=axis)

def _gelu(x):
    return jax.nn.gelu(x, approximate=True)

def _silu(x):
    return jax.nn.silu(x)

def _sigmoid(x):
    return jax.nn.sigmoid(x)

def _layernorm(x, axis=-1, eps=1e-05):
    m = jnp.mean(x, axis=axis, keepdims=True)
    v = jnp.var(x, axis=axis, keepdims=True)
    return (x - m) / jnp.sqrt(v + eps)

def _scatter_add(tgt, idx, src, axis=0):
    return tgt.at[idx].add(src)

def _segment_sum(src, seg, n):
    return jax.ops.segment_sum(src, seg, n)
kernel_name = 'mk_decoder_preln_d2_seqx_r8_7cb2a3'

def setup_inputs(seed: int=0):
    np.random.seed(seed)
    _w = jnp.asarray

    def _rec_inputs():
        import jax
        import jax.numpy as jnp
        _rk = jax.random.key(seed)
        x = 7.22e-05 + 1 * jax.random.normal(jax.random.fold_in(_rk, 1), (32, 64, 256), jnp.float32)
        _lenS = 64 - jax.random.randint(jax.random.fold_in(_rk, 7), (32,), 0, max(1, 64 // 4) + 1, jnp.int32)
        _lenS2 = 64 - jax.random.randint(jax.random.fold_in(_rk, 8), (32,), 0, max(1, 64 // 4) + 1, jnp.int32)
        _ctx_2048P = jax.random.normal(jax.random.fold_in(_rk, 11), (32, 16, 256), jnp.float32)
        _ctx_2048c = jax.random.dirichlet(jax.random.fold_in(_rk, 511), 0.3 * jnp.ones((16,), jnp.float32), (32, 64))
        _ctx_2048t = jnp.einsum('bsk,bkd->bsd', _ctx_2048c, _ctx_2048P)
        _ctx_2048t = _ctx_2048t * jax.lax.rsqrt(jnp.mean(jnp.square(_ctx_2048t)) + 1e-12) * 0.953939
        ctx_2048 = 4.13588e-05 + 0.999923 * (_ctx_2048t + 0.3 * jax.random.normal(jax.random.fold_in(_rk, 611), (32, 64, 256), jnp.float32))
        _validS = jnp.arange(64)[None, :] < _lenS[:, None]
        _validS2 = jnp.arange(64)[None, :] < _lenS2[:, None]
        _causal = jnp.tril(jnp.ones((64, 64), dtype=bool))
        mask_BxS2_bf1 = jnp.ones((32, 64), dtype=bool)
        return (x, ctx_2048, mask_BxS2_bf1)
    x, ctx_2048, mask_BxS2_bf1 = _rec_inputs()

    def _L0_attn_setup():
        import jax, jax.numpy as jnp
        import numpy as np
        HIDDEN = 256
        NUM_HEADS = 6
        HEAD_V = 64
        VALUE_DIM = NUM_HEADS * HEAD_V
        CONV_K = 4
        PHASE_BASE = 10000.0
        EPS = 1e-05

        def _causal_depthwise_conv(x, w):
            B, T, C = x.shape
            K = w.shape[1]
            xp = jnp.pad(x, ((0, 0), (K - 1, 0), (0, 0)))
            y = jnp.zeros_like(x)
            for j in range(K):
                y = y + xp[:, j:j + T, :] * w[:, j]
            return y

        def _rotate(x, ang):
            cos = jnp.cos(ang)
            sin = jnp.sin(ang)
            xe = x[..., ::2]
            xo = x[..., 1::2]
            ye = xe * cos - xo * sin
            yo = xo * cos + xe * sin
            return jnp.stack([ye, yo], axis=-1).reshape(x.shape)

        def _forward(hidden_states, Wq, Wk, Wv, Wa, Wb, Wg, Wo, conv_q, conv_k, conv_v, rms_w):
            B, T, _ = hidden_states.shape
            H, D = (NUM_HEADS, HEAD_V)
            inv_freq = 1.0 / PHASE_BASE ** (jnp.arange(0, D, 2, dtype=jnp.float32) / D)
            q = _causal_depthwise_conv(hidden_states @ Wq, conv_q).reshape(B, T, H, D)
            k = _causal_depthwise_conv(hidden_states @ Wk, conv_k).reshape(B, T, H, D)
            v = _causal_depthwise_conv(hidden_states @ Wv, conv_v).reshape(B, T, H, D)
            theta = q[..., ::2] * inv_freq
            psi = k[..., ::2] * inv_freq
            phi = theta - jnp.concatenate([jnp.zeros_like(theta[:, :1]), theta[:, :-1]], axis=1)
            alpha = jax.nn.sigmoid(hidden_states @ Wa)
            beta = jax.nn.sigmoid(hidden_states @ Wb)
            tm = lambda a: jnp.moveaxis(a, 1, 0)
            xs = (tm(theta), tm(psi), tm(phi), tm(v), tm(alpha), tm(beta))

            def step(state, inp):
                th, ps, ph, vt, at, bt = inp
                retained = _rotate(state, ph) * at[..., None]
                write = _rotate(vt, ps)
                new_state = retained + bt[..., None] * write
                out_t = _rotate(new_state, -th)
                return (new_state, out_t)
            state0 = jnp.zeros((B, H, D), hidden_states.dtype)
            _, out = jax.lax.scan(step, state0, xs)
            out = jnp.moveaxis(out, 0, 1)
            g = (hidden_states @ Wg).reshape(B, T, H, D)
            rms = jax.lax.rsqrt(jnp.mean(jnp.square(out), axis=-1, keepdims=True) + EPS)
            o = out * rms * rms_w * jax.nn.silu(g)
            return o.reshape(B, T, VALUE_DIM) @ Wo
        key = jax.random.key(seed)
        ks = jax.random.split(key, 12)
        s = 0.02
        return {'hidden_states': jax.random.normal(ks[0], (2, 256, HIDDEN), jnp.float32), 'Wq': jax.random.normal(ks[1], (HIDDEN, VALUE_DIM), jnp.float32) * s, 'Wk': jax.random.normal(ks[2], (HIDDEN, VALUE_DIM), jnp.float32) * s, 'Wv': jax.random.normal(ks[3], (HIDDEN, VALUE_DIM), jnp.float32) * s, 'Wa': jax.random.normal(ks[4], (HIDDEN, NUM_HEADS), jnp.float32) * s, 'Wb': jax.random.normal(ks[5], (HIDDEN, NUM_HEADS), jnp.float32) * s, 'Wg': jax.random.normal(ks[6], (HIDDEN, VALUE_DIM), jnp.float32) * s, 'Wo': jax.random.normal(ks[7], (VALUE_DIM, HIDDEN), jnp.float32) * s, 'conv_q': jax.random.normal(ks[8], (VALUE_DIM, CONV_K), jnp.float32) * s, 'conv_k': jax.random.normal(ks[9], (VALUE_DIM, CONV_K), jnp.float32) * s, 'conv_v': jax.random.normal(ks[10], (VALUE_DIM, CONV_K), jnp.float32) * s, 'rms_w': jnp.ones((HEAD_V,), jnp.float32)}
    _L0_attn_all = _L0_attn_setup()
    _L0_attn_in = {k: v for k, v in _L0_attn_all.items() if k in ('Wq', 'Wk', 'Wv', 'Wa', 'Wb', 'Wg', 'Wo', 'conv_q', 'conv_k', 'conv_v', 'rms_w')}
    del _L0_attn_all

    def _L0_xattn_setup():
        import jax, jax.numpy as jnp
        import numpy as np
        import math
        D_MODEL = 256
        N_Q_HEADS = 16
        N_KV_HEADS = 4
        HEAD_DIM = D_MODEL // N_Q_HEADS
        B = 4
        S = 128

        def _alibi_slopes(num_heads):
            n = 2 ** int(math.floor(math.log2(num_heads)))
            m0 = 2.0 ** (-8.0 / n)
            return m0 ** jnp.arange(1, n + 1, dtype=jnp.float32)
        key = jax.random.key(seed)
        ks = jax.random.split(key, 8)
        xavier = lambda k, fi, fo: jax.random.normal(k, (fi, fo), jnp.float32) * math.sqrt(2.0 / (fi + fo))
        return {'query': jax.random.normal(ks[0], (B, S, D_MODEL), jnp.float32), 'key': jax.random.normal(ks[1], (B, S, D_MODEL), jnp.float32), 'value': jax.random.normal(ks[2], (B, S, D_MODEL), jnp.float32), 'mask': jnp.ones((B, S), dtype=bool), 'Wq': xavier(ks[3], D_MODEL, N_Q_HEADS * HEAD_DIM), 'Wk': xavier(ks[4], D_MODEL, N_KV_HEADS * HEAD_DIM), 'Wv': xavier(ks[5], D_MODEL, N_KV_HEADS * HEAD_DIM), 'Wo': xavier(ks[6], D_MODEL, D_MODEL)}
    _L0_xattn_all = _L0_xattn_setup()
    _L0_xattn_in = {k: v for k, v in _L0_xattn_all.items() if k in ('Wq', 'Wk', 'Wv', 'Wo')}
    del _L0_xattn_all

    def _L0_ffn_setup():
        import jax, jax.numpy as jnp
        import numpy as np
        B, S, D, F, E, SH, K = (2, 256, 256, 128, 16, 2, 2)

        def _experts_all(x, g, gb, w1, b1, w2, b2):
            y = jax.nn.gelu(jnp.einsum('bsd,edf->bsef', x, g) + gb, approximate=False)
            y = y * (jnp.einsum('bsd,edf->bsef', x, w1) + b1)
            return jnp.einsum('bsef,efd->bsed', y, w2) + b2
        key = jax.random.key(seed)
        ks = jax.random.split(key, 8)
        std = 0.02
        mk = lambda k, sh: jax.random.normal(k, sh, jnp.float32) * std
        return {'x': jax.random.normal(ks[0], (B, S, D), jnp.float32), 'wa': mk(ks[1], (D, E)), 'rg': mk(ks[2], (E, D, F)), 'rgb': jnp.zeros((E, F), jnp.float32), 'rw1': mk(ks[3], (E, D, F)), 'rb1': jnp.zeros((E, F), jnp.float32), 'rw2': mk(ks[4], (E, F, D)), 'rb2': jnp.zeros((E, D), jnp.float32), 'sg': mk(ks[5], (SH, D, F)), 'sgb': jnp.zeros((SH, F), jnp.float32), 'sw1': mk(ks[6], (SH, D, F)), 'sb1': jnp.zeros((SH, F), jnp.float32), 'sw2': mk(ks[7], (SH, F, D)), 'sb2': jnp.zeros((SH, D), jnp.float32)}
    _L0_ffn_all = _L0_ffn_setup()
    _L0_ffn_in = {k: v for k, v in _L0_ffn_all.items() if k in ('wa', 'rg', 'rgb', 'rw1', 'rb1', 'rw2', 'rb2', 'sg', 'sgb', 'sw1', 'sb1', 'sw2', 'sb2')}
    del _L0_ffn_all

    def _L1_attn_setup():
        import jax, jax.numpy as jnp
        import numpy as np
        B, N, H = (2, 512, 256)
        NH, HD = (16, 128)
        BLK = 32
        EPS = 1e-06

        def _lightning_attn(x, slope_rate, w_qkv, w_gate, w_out, norm_w):
            b, n, _ = x.shape
            h, d = (NH, HD)
            nb = n // BLK
            qkv = jax.nn.silu(jnp.einsum('bnf,of->bno', x, w_qkv))
            qkv = qkv.reshape(b, n, h, 3 * d)
            q, k, v = jnp.split(qkv, 3, axis=-1)
            q = q.transpose(0, 2, 1, 3)
            k = k.transpose(0, 2, 1, 3)
            v = v.transpose(0, 2, 1, 3)
            s = slope_rate.astype(jnp.float32)
            arr = jnp.arange(1, BLK + 1, dtype=jnp.float32)
            q_decay = jnp.exp(-s * arr[:, None])
            k_decay = jnp.exp(-s * (BLK - arr)[:, None])
            idx = arr[:, None] - arr[None, :]
            diag_decay = jnp.where(idx >= 0, jnp.exp(-s * idx), 0.0)
            block_decay = jnp.exp(-s * BLK)
            qb = q.reshape(b, h, nb, BLK, d).transpose(2, 0, 1, 3, 4)
            kb = k.reshape(b, h, nb, BLK, d).transpose(2, 0, 1, 3, 4)
            vb = v.reshape(b, h, nb, BLK, d).transpose(2, 0, 1, 3, 4)

            def step(kv, blk):
                qi, ki, vi = blk
                o_inter = jnp.einsum('bhmd,bhde->bhme', qi * q_decay, kv)
                qk = jnp.einsum('bhmd,bhnd->bhmn', qi, ki) * diag_decay
                o_intra = jnp.einsum('bhmn,bhne->bhme', qk, vi)
                kv_new = block_decay * kv + jnp.einsum('bhmd,bhme->bhde', ki * k_decay, vi)
                return (kv_new, o_inter + o_intra)
            kv0 = jnp.zeros((b, h, d, d), dtype=jnp.float32)
            _, out = jax.lax.scan(step, kv0, (qb, kb, vb))
            out = out.transpose(1, 2, 0, 3, 4).reshape(b, h, n, d)
            out = out.transpose(0, 2, 1, 3).reshape(b, n, h * d)
            var = jnp.mean(out * out, axis=-1, keepdims=True)
            out = norm_w * (out * jax.lax.rsqrt(var + EPS))
            gate = jax.nn.sigmoid(jnp.einsum('bnf,of->bno', x, w_gate))
            return jnp.einsum('bno,fo->bnf', gate * out, w_out)
        key = jax.random.key(seed)
        ks = jax.random.split(key, 5)
        scale = 0.02
        x = jax.random.normal(ks[0], (B, N, H), dtype=jnp.float32)
        slopes = (1.0 / 2.0 ** (8.0 * np.arange(1, NH + 1) / NH)).astype(np.float32)
        slope_rate = jnp.asarray(slopes).reshape(NH, 1, 1)
        w_qkv = jax.random.normal(ks[1], (3 * NH * HD, H), dtype=jnp.float32) * scale
        w_gate = jax.random.normal(ks[2], (NH * HD, H), dtype=jnp.float32) * scale
        w_out = jax.random.normal(ks[3], (H, NH * HD), dtype=jnp.float32) * scale
        norm_w = jnp.ones((NH * HD,), dtype=jnp.float32)
        return {'hidden_states': x, 'slope_rate': slope_rate, 'w_qkv': w_qkv, 'w_gate': w_gate, 'w_out': w_out, 'norm_w': norm_w}
    _L1_attn_all = _L1_attn_setup()
    _L1_attn_in = {k: v for k, v in _L1_attn_all.items() if k in ('slope_rate', 'w_qkv', 'w_gate', 'w_out', 'norm_w')}
    del _L1_attn_all

    def _L1_xattn_setup():
        import jax, jax.numpy as jnp
        import numpy as np
        D_MODEL = 256
        NUM_HEADS = 16
        HEAD_DIM = D_MODEL // NUM_HEADS

        def _fq_sym(x, axis):
            s = jnp.max(jnp.abs(x), axis=axis, keepdims=True) / 127.0
            s = jnp.maximum(s, 1e-08)
            q = jnp.clip(jnp.round(x / s), -127.0, 127.0) * s
            return x + jax.lax.stop_gradient(q - x)

        def _fq_unsigned(x, axis):
            s = jnp.max(x, axis=axis, keepdims=True) / 255.0
            s = jnp.maximum(s, 1e-08)
            q = jnp.clip(jnp.round(x / s), 0.0, 255.0) * s
            return x + jax.lax.stop_gradient(q - x)
        key = jax.random.key(seed)
        ks = jax.random.split(key, 8)
        B, N, M, C = (2, 256, 64, D_MODEL)
        return {'x': jax.random.normal(ks[0], (B, N, C), jnp.float32), 'cond': jax.random.normal(ks[1], (B, M, C), jnp.float32), 'Wq': jax.random.normal(ks[2], (C, C), jnp.float32) * 0.02, 'bq': jnp.zeros((C,), jnp.float32), 'Wkv': jax.random.normal(ks[3], (C, 2 * C), jnp.float32) * 0.02, 'bkv': jnp.zeros((2 * C,), jnp.float32), 'Wp': jax.random.normal(ks[4], (C, C), jnp.float32) * 0.02, 'bp': jnp.zeros((C,), jnp.float32)}
    _L1_xattn_all = _L1_xattn_setup()
    _L1_xattn_in = {k: v for k, v in _L1_xattn_all.items() if k in ('Wq', 'bq', 'Wkv', 'bkv', 'Wp', 'bp')}
    del _L1_xattn_all

    def _L1_ffn_setup():
        import jax, jax.numpy as jnp
        import numpy as np
        TOP_K = 4
        key = jax.random.key(seed)
        ks = jax.random.split(key, 9)
        B, T, D, H, NE = (2, 128, 256, 176, 16)
        s = 0.02
        return {'x': jax.random.normal(ks[0], (B, T, D), jnp.float32), 'gate_w': jax.random.normal(ks[1], (NE, D), jnp.float32) * s, 'gate_b': jax.random.normal(ks[2], (NE,), jnp.float32) * s, 'w1_shared': jax.random.normal(ks[3], (D, H), jnp.float32) * s, 'w2_shared': jax.random.normal(ks[4], (H, D), jnp.float32) * s, 'w3_shared': jax.random.normal(ks[5], (D, H), jnp.float32) * s, 'w1_routed': jax.random.normal(ks[6], (NE, D, H), jnp.float32) * s, 'w2_routed': jax.random.normal(ks[7], (NE, H, D), jnp.float32) * s, 'w3_routed': jax.random.normal(ks[8], (NE, D, H), jnp.float32) * s}
    _L1_ffn_all = _L1_ffn_setup()
    _L1_ffn_in = {k: v for k, v in _L1_ffn_all.items() if k in ('gate_w', 'gate_b', 'w1_shared', 'w2_shared', 'w3_shared', 'w1_routed', 'w2_routed', 'w3_routed')}
    del _L1_ffn_all
    return {'x': x, 'ctx_2048': ctx_2048, 'mask_BxS2_bf1': mask_BxS2_bf1, 'L0_attn_Wq': _L0_attn_in['Wq'], 'L0_attn_Wk': _L0_attn_in['Wk'], 'L0_attn_Wv': _L0_attn_in['Wv'], 'L0_attn_Wa': _L0_attn_in['Wa'], 'L0_attn_Wb': _L0_attn_in['Wb'], 'L0_attn_Wg': _L0_attn_in['Wg'], 'L0_attn_Wo': _L0_attn_in['Wo'], 'L0_attn_conv_q': _L0_attn_in['conv_q'], 'L0_attn_conv_k': _L0_attn_in['conv_k'], 'L0_attn_conv_v': _L0_attn_in['conv_v'], 'L0_attn_rms_w': _L0_attn_in['rms_w'], 'L0_xattn_Wq': _L0_xattn_in['Wq'], 'L0_xattn_Wk': _L0_xattn_in['Wk'], 'L0_xattn_Wv': _L0_xattn_in['Wv'], 'L0_xattn_Wo': _L0_xattn_in['Wo'], 'L0_ffn_wa': _L0_ffn_in['wa'], 'L0_ffn_rg': _L0_ffn_in['rg'], 'L0_ffn_rgb': _L0_ffn_in['rgb'], 'L0_ffn_rw1': _L0_ffn_in['rw1'], 'L0_ffn_rb1': _L0_ffn_in['rb1'], 'L0_ffn_rw2': _L0_ffn_in['rw2'], 'L0_ffn_rb2': _L0_ffn_in['rb2'], 'L0_ffn_sg': _L0_ffn_in['sg'], 'L0_ffn_sgb': _L0_ffn_in['sgb'], 'L0_ffn_sw1': _L0_ffn_in['sw1'], 'L0_ffn_sb1': _L0_ffn_in['sb1'], 'L0_ffn_sw2': _L0_ffn_in['sw2'], 'L0_ffn_sb2': _L0_ffn_in['sb2'], 'L1_attn_slope_rate': _L1_attn_in['slope_rate'], 'L1_attn_w_qkv': _L1_attn_in['w_qkv'], 'L1_attn_w_gate': _L1_attn_in['w_gate'], 'L1_attn_w_out': _L1_attn_in['w_out'], 'L1_attn_norm_w': _L1_attn_in['norm_w'], 'L1_xattn_Wq': _L1_xattn_in['Wq'], 'L1_xattn_bq': _L1_xattn_in['bq'], 'L1_xattn_Wkv': _L1_xattn_in['Wkv'], 'L1_xattn_bkv': _L1_xattn_in['bkv'], 'L1_xattn_Wp': _L1_xattn_in['Wp'], 'L1_xattn_bp': _L1_xattn_in['bp'], 'L1_ffn_gate_w': _L1_ffn_in['gate_w'], 'L1_ffn_gate_b': _L1_ffn_in['gate_b'], 'L1_ffn_w1_shared': _L1_ffn_in['w1_shared'], 'L1_ffn_w2_shared': _L1_ffn_in['w2_shared'], 'L1_ffn_w3_shared': _L1_ffn_in['w3_shared'], 'L1_ffn_w1_routed': _L1_ffn_in['w1_routed'], 'L1_ffn_w2_routed': _L1_ffn_in['w2_routed'], 'L1_ffn_w3_routed': _L1_ffn_in['w3_routed']}

def reference(x, ctx_2048, mask_BxS2_bf1, L0_attn_Wq, L0_attn_Wk, L0_attn_Wv, L0_attn_Wa, L0_attn_Wb, L0_attn_Wg, L0_attn_Wo, L0_attn_conv_q, L0_attn_conv_k, L0_attn_conv_v, L0_attn_rms_w, L0_xattn_Wq, L0_xattn_Wk, L0_xattn_Wv, L0_xattn_Wo, L0_ffn_wa, L0_ffn_rg, L0_ffn_rgb, L0_ffn_rw1, L0_ffn_rb1, L0_ffn_rw2, L0_ffn_rb2, L0_ffn_sg, L0_ffn_sgb, L0_ffn_sw1, L0_ffn_sb1, L0_ffn_sw2, L0_ffn_sb2, L1_attn_slope_rate, L1_attn_w_qkv, L1_attn_w_gate, L1_attn_w_out, L1_attn_norm_w, L1_xattn_Wq, L1_xattn_bq, L1_xattn_Wkv, L1_xattn_bkv, L1_xattn_Wp, L1_xattn_bp, L1_ffn_gate_w, L1_ffn_gate_b, L1_ffn_w1_shared, L1_ffn_w2_shared, L1_ffn_w3_shared, L1_ffn_w1_routed, L1_ffn_w2_routed, L1_ffn_w3_routed):
    import jax
    import jax.numpy as jnp

    def _L0_attn_ref(hidden_states, Wq, Wk, Wv, Wa, Wb, Wg, Wo, conv_q, conv_k, conv_v, rms_w):
        import jax, jax.numpy as jnp
        import numpy as np
        HIDDEN = 256
        NUM_HEADS = 6
        HEAD_V = 64
        VALUE_DIM = NUM_HEADS * HEAD_V
        CONV_K = 4
        PHASE_BASE = 10000.0
        EPS = 1e-05

        def _causal_depthwise_conv(x, w):
            B, T, C = x.shape
            K = w.shape[1]
            xp = jnp.pad(x, ((0, 0), (K - 1, 0), (0, 0)))
            y = jnp.zeros_like(x)
            for j in range(K):
                y = y + xp[:, j:j + T, :] * w[:, j]
            return y

        def _rotate(x, ang):
            cos = jnp.cos(ang)
            sin = jnp.sin(ang)
            xe = x[..., ::2]
            xo = x[..., 1::2]
            ye = xe * cos - xo * sin
            yo = xo * cos + xe * sin
            return jnp.stack([ye, yo], axis=-1).reshape(x.shape)

        def _forward(hidden_states, Wq, Wk, Wv, Wa, Wb, Wg, Wo, conv_q, conv_k, conv_v, rms_w):
            B, T, _ = hidden_states.shape
            H, D = (NUM_HEADS, HEAD_V)
            inv_freq = 1.0 / PHASE_BASE ** (jnp.arange(0, D, 2, dtype=jnp.float32) / D)
            q = _causal_depthwise_conv(hidden_states @ Wq, conv_q).reshape(B, T, H, D)
            k = _causal_depthwise_conv(hidden_states @ Wk, conv_k).reshape(B, T, H, D)
            v = _causal_depthwise_conv(hidden_states @ Wv, conv_v).reshape(B, T, H, D)
            theta = q[..., ::2] * inv_freq
            psi = k[..., ::2] * inv_freq
            phi = theta - jnp.concatenate([jnp.zeros_like(theta[:, :1]), theta[:, :-1]], axis=1)
            alpha = jax.nn.sigmoid(hidden_states @ Wa)
            beta = jax.nn.sigmoid(hidden_states @ Wb)
            tm = lambda a: jnp.moveaxis(a, 1, 0)
            xs = (tm(theta), tm(psi), tm(phi), tm(v), tm(alpha), tm(beta))

            def step(state, inp):
                th, ps, ph, vt, at, bt = inp
                retained = _rotate(state, ph) * at[..., None]
                write = _rotate(vt, ps)
                new_state = retained + bt[..., None] * write
                out_t = _rotate(new_state, -th)
                return (new_state, out_t)
            state0 = jnp.zeros((B, H, D), hidden_states.dtype)
            _, out = jax.lax.scan(step, state0, xs)
            out = jnp.moveaxis(out, 0, 1)
            g = (hidden_states @ Wg).reshape(B, T, H, D)
            rms = jax.lax.rsqrt(jnp.mean(jnp.square(out), axis=-1, keepdims=True) + EPS)
            o = out * rms * rms_w * jax.nn.silu(g)
            return o.reshape(B, T, VALUE_DIM) @ Wo
        return _forward(hidden_states, Wq, Wk, Wv, Wa, Wb, Wg, Wo, conv_q, conv_k, conv_v, rms_w)

    def _L0_xattn_ref(query, key, value, mask, Wq, Wk, Wv, Wo):
        import jax, jax.numpy as jnp
        import numpy as np
        import math
        D_MODEL = 256
        N_Q_HEADS = 16
        N_KV_HEADS = 4
        HEAD_DIM = D_MODEL // N_Q_HEADS
        B = 4
        S = 128

        def _alibi_slopes(num_heads):
            n = 2 ** int(math.floor(math.log2(num_heads)))
            m0 = 2.0 ** (-8.0 / n)
            return m0 ** jnp.arange(1, n + 1, dtype=jnp.float32)
        b, q_len, d = query.shape
        kv_len = key.shape[1]
        G = N_KV_HEADS
        Hpg = N_Q_HEADS // G
        dh = HEAD_DIM
        Q = (query @ Wq).reshape(b, q_len, G, Hpg, dh)
        K = (key @ Wk).reshape(b, kv_len, G, dh)
        V = (value @ Wv).reshape(b, kv_len, G, dh)
        Q = Q / math.sqrt(dh)
        scores = jnp.einsum('bqghd,bkgd->bghqk', Q, K)
        rel = jnp.arange(kv_len, dtype=jnp.float32)[None, :] - jnp.arange(q_len, dtype=jnp.float32)[:, None]
        m = _alibi_slopes(N_Q_HEADS).reshape(1, G, Hpg, 1, 1)
        scores = scores + m * rel[None, None, None]
        neg = jnp.finfo(scores.dtype).min
        scores = jnp.where(mask[:, None, None, None, :], scores, neg)
        w = jax.nn.softmax(scores, axis=-1)
        out = jnp.einsum('bghqk,bkgd->bqghd', w, V)
        out = out.reshape(b, q_len, G * Hpg * dh)
        return out @ Wo

    def _L0_ffn_ref(x, wa, rg, rgb, rw1, rb1, rw2, rb2, sg, sgb, sw1, sb1, sw2, sb2):
        import jax, jax.numpy as jnp
        import numpy as np
        B, S, D, F, E, SH, K = (2, 256, 256, 128, 16, 2, 2)

        def _experts_all(x, g, gb, w1, b1, w2, b2):
            y = jax.nn.gelu(jnp.einsum('bsd,edf->bsef', x, g) + gb, approximate=False)
            y = y * (jnp.einsum('bsd,edf->bsef', x, w1) + b1)
            return jnp.einsum('bsef,efd->bsed', y, w2) + b2
        aff = jax.nn.sigmoid(jnp.einsum('bsd,de->bse', x, wa))
        topk_p, topk_i = jax.lax.top_k(aff, K)
        topk_p = topk_p / jnp.sum(topk_p, axis=-1, keepdims=True)
        combine = jnp.sum(jax.nn.one_hot(topk_i, E, dtype=x.dtype) * topk_p[..., None], axis=2)
        routed = jnp.einsum('bsed,bse->bsd', _experts_all(x, rg, rgb, rw1, rb1, rw2, rb2), combine)
        shared = jnp.sum(_experts_all(x, sg, sgb, sw1, sb1, sw2, sb2), axis=2)
        return x + shared + routed

    def _L1_attn_ref(hidden_states, slope_rate, w_qkv, w_gate, w_out, norm_w):
        import jax, jax.numpy as jnp
        import numpy as np
        B, N, H = (2, 512, 256)
        NH, HD = (16, 128)
        BLK = 32
        EPS = 1e-06

        def _lightning_attn(x, slope_rate, w_qkv, w_gate, w_out, norm_w):
            b, n, _ = x.shape
            h, d = (NH, HD)
            nb = n // BLK
            qkv = jax.nn.silu(jnp.einsum('bnf,of->bno', x, w_qkv))
            qkv = qkv.reshape(b, n, h, 3 * d)
            q, k, v = jnp.split(qkv, 3, axis=-1)
            q = q.transpose(0, 2, 1, 3)
            k = k.transpose(0, 2, 1, 3)
            v = v.transpose(0, 2, 1, 3)
            s = slope_rate.astype(jnp.float32)
            arr = jnp.arange(1, BLK + 1, dtype=jnp.float32)
            q_decay = jnp.exp(-s * arr[:, None])
            k_decay = jnp.exp(-s * (BLK - arr)[:, None])
            idx = arr[:, None] - arr[None, :]
            diag_decay = jnp.where(idx >= 0, jnp.exp(-s * idx), 0.0)
            block_decay = jnp.exp(-s * BLK)
            qb = q.reshape(b, h, nb, BLK, d).transpose(2, 0, 1, 3, 4)
            kb = k.reshape(b, h, nb, BLK, d).transpose(2, 0, 1, 3, 4)
            vb = v.reshape(b, h, nb, BLK, d).transpose(2, 0, 1, 3, 4)

            def step(kv, blk):
                qi, ki, vi = blk
                o_inter = jnp.einsum('bhmd,bhde->bhme', qi * q_decay, kv)
                qk = jnp.einsum('bhmd,bhnd->bhmn', qi, ki) * diag_decay
                o_intra = jnp.einsum('bhmn,bhne->bhme', qk, vi)
                kv_new = block_decay * kv + jnp.einsum('bhmd,bhme->bhde', ki * k_decay, vi)
                return (kv_new, o_inter + o_intra)
            kv0 = jnp.zeros((b, h, d, d), dtype=jnp.float32)
            _, out = jax.lax.scan(step, kv0, (qb, kb, vb))
            out = out.transpose(1, 2, 0, 3, 4).reshape(b, h, n, d)
            out = out.transpose(0, 2, 1, 3).reshape(b, n, h * d)
            var = jnp.mean(out * out, axis=-1, keepdims=True)
            out = norm_w * (out * jax.lax.rsqrt(var + EPS))
            gate = jax.nn.sigmoid(jnp.einsum('bnf,of->bno', x, w_gate))
            return jnp.einsum('bno,fo->bnf', gate * out, w_out)
        return _lightning_attn(hidden_states, slope_rate, w_qkv, w_gate, w_out, norm_w)

    def _L1_xattn_ref(x, cond, Wq, bq, Wkv, bkv, Wp, bp):
        import jax, jax.numpy as jnp
        import numpy as np
        D_MODEL = 256
        NUM_HEADS = 16
        HEAD_DIM = D_MODEL // NUM_HEADS

        def _fq_sym(x, axis):
            s = jnp.max(jnp.abs(x), axis=axis, keepdims=True) / 127.0
            s = jnp.maximum(s, 1e-08)
            q = jnp.clip(jnp.round(x / s), -127.0, 127.0) * s
            return x + jax.lax.stop_gradient(q - x)

        def _fq_unsigned(x, axis):
            s = jnp.max(x, axis=axis, keepdims=True) / 255.0
            s = jnp.maximum(s, 1e-08)
            q = jnp.clip(jnp.round(x / s), 0.0, 255.0) * s
            return x + jax.lax.stop_gradient(q - x)
        B, N, C = x.shape
        H, hd = (NUM_HEADS, HEAD_DIM)
        q = (x @ Wq + bq).reshape(1, B * N, H, hd)
        kv = (cond @ Wkv + bkv).reshape(1, -1, 2, H, hd)
        k, v = (kv[:, :, 0], kv[:, :, 1])
        scale = 1.0 / np.sqrt(hd).astype(np.float32)
        q = jnp.transpose(q * scale, (0, 2, 1, 3))
        k = jnp.transpose(k, (0, 2, 1, 3))
        v = jnp.transpose(v, (0, 2, 1, 3))
        q = _fq_sym(q, axis=-1)
        k = _fq_sym(k, axis=-1)
        v = _fq_sym(v, axis=2)
        attn = jnp.einsum('bhqd,bhkd->bhqk', q, k)
        attn = jax.nn.softmax(attn.astype(jnp.float32), axis=-1)
        attn = _fq_unsigned(attn, axis=-1)
        out = jnp.einsum('bhqk,bhkd->bhqd', attn, v)
        out = jnp.transpose(out, (0, 2, 1, 3)).reshape(B, N, C)
        return out @ Wp + bp

    def _L1_ffn_ref(x, gate_w, gate_b, w1_shared, w2_shared, w3_shared, w1_routed, w2_routed, w3_routed):
        import jax, jax.numpy as jnp
        import numpy as np
        TOP_K = 4
        n_experts = w1_routed.shape[0]
        logits = jnp.einsum('ed,btd->bte', gate_w, x)
        scores = jax.nn.sigmoid(logits) + gate_b
        weights, indices = jax.lax.top_k(scores, TOP_K)
        weights = weights / weights.sum(-1, keepdims=True)
        shared_out = jax.nn.silu(x @ w1_shared) * (x @ w3_shared) @ w2_shared
        one_hot = jax.nn.one_hot(indices, n_experts, dtype=x.dtype)
        router_probs = (weights[..., None] * one_hot).sum(-2)
        h1 = jnp.einsum('btd,edc->btec', x, w1_routed)
        h2 = jnp.einsum('btd,edc->btec', x, w3_routed)
        h3 = jax.nn.silu(h1 * h2)
        experts_out = jnp.einsum('btec,ecd->bted', h3, w2_routed)
        routed_out = jnp.einsum('bted,bte->btd', experts_out, router_probs)
        return shared_out + routed_out
    x = x + _L0_attn_ref(_layernorm(x, axis=-1), L0_attn_Wq, L0_attn_Wk, L0_attn_Wv, L0_attn_Wa, L0_attn_Wb, L0_attn_Wg, L0_attn_Wo, L0_attn_conv_q, L0_attn_conv_k, L0_attn_conv_v, L0_attn_rms_w)
    x = x + _L0_xattn_ref(_layernorm(x, axis=-1), ctx_2048, ctx_2048, mask_BxS2_bf1, L0_xattn_Wq, L0_xattn_Wk, L0_xattn_Wv, L0_xattn_Wo)
    x = x + _L0_ffn_ref(_layernorm(x, axis=-1), L0_ffn_wa, L0_ffn_rg, L0_ffn_rgb, L0_ffn_rw1, L0_ffn_rb1, L0_ffn_rw2, L0_ffn_rb2, L0_ffn_sg, L0_ffn_sgb, L0_ffn_sw1, L0_ffn_sb1, L0_ffn_sw2, L0_ffn_sb2)
    x = x + _L1_attn_ref(_layernorm(x, axis=-1), L1_attn_slope_rate, L1_attn_w_qkv, L1_attn_w_gate, L1_attn_w_out, L1_attn_norm_w)
    x = x + _L1_xattn_ref(_layernorm(x, axis=-1), ctx_2048, L1_xattn_Wq, L1_xattn_bq, L1_xattn_Wkv, L1_xattn_bkv, L1_xattn_Wp, L1_xattn_bp)
    x = x + _L1_ffn_ref(_layernorm(x, axis=-1), L1_ffn_gate_w, L1_ffn_gate_b, L1_ffn_w1_shared, L1_ffn_w2_shared, L1_ffn_w3_shared, L1_ffn_w1_routed, L1_ffn_w2_routed, L1_ffn_w3_routed)
    return x

_drawn_inputs = setup_inputs


def setup_inputs(seed=0):
    import zlib

    import numpy as np

    out = dict(_drawn_inputs(seed))
    spreads = {'L0_attn_rms_w': (1.0, 0.6),
     'L0_ffn_rgb': (0.0, 0.8),
     'L0_ffn_rb1': (0.0, 0.8),
     'L0_ffn_rb2': (0.0, 0.1),
     'L0_ffn_sgb': (0.0, 0.8),
     'L0_ffn_sb1': (0.0, 0.8),
     'L0_ffn_sb2': (0.0, 0.1),
     'L1_attn_norm_w': (1.0, 0.2),
     'L1_xattn_bq': (0.0, 0.8),
     'L1_xattn_bkv': (0.0, 0.64),
     'L1_xattn_bp': (0.0, 0.1)}
    factors = {'L0_attn_Wq': 8.0,
     'L0_attn_Wk': 8.0,
     'L0_attn_Wa': 8.0,
     'L0_attn_Wb': 8.0,
     'L0_attn_conv_q': 8.0,
     'L0_attn_conv_k': 8.0,
     'L0_ffn_rg': 8.0,
     'L0_ffn_rw1': 8.0,
     'L0_ffn_rw2': 8.0,
     'L0_ffn_sg': 6.929,
     'L0_ffn_sw1': 6.665,
     'L0_ffn_sw2': 6.395,
     'L1_xattn_Wq': 8.0,
     'L1_xattn_Wkv': 8.0,
     'L1_xattn_Wp': 4.299,
     'L1_ffn_gate_w': 8.0,
     'L1_ffn_gate_b': 8.0,
     'L1_ffn_w1_shared': 8.0,
     'L1_ffn_w2_shared': 8.0,
     'L1_ffn_w3_shared': 8.0,
     'L1_ffn_w1_routed': 8.0,
     'L1_ffn_w2_routed': 8.0,
     'L1_ffn_w3_routed': 8.0}
    for name, (base, spread) in spreads.items():
        noise = np.random.default_rng([zlib.crc32(name.encode()), seed]).standard_normal(out[name].shape)
        drawn = base * np.exp(spread * noise) if base else spread * noise
        out[name] = jnp.asarray(drawn.astype(out[name].dtype))
    for name, factor in factors.items():
        out[name] = (out[name] * factor).astype(out[name].dtype)
    return out
```

```python
from contextlib import ExitStack

import numpy as np
import concourse.bass as bass
from concourse import mybir

F32 = mybir.dt.float32
BF16 = mybir.dt.bfloat16
U8 = mybir.dt.uint8
U32 = mybir.dt.uint32
ALU = mybir.AluOpType
ACT = mybir.ActivationFunctionType
AX = mybir.AxisListType.X
ds = bass.ds

BATCH, SEQ, D = 32, 64, 256
TOK = BATCH * SEQ
P = 128
NT = TOK // P
KC = D // P
BLK = 512
NBLK = TOK // BLK
TPB = BLK // P
BPB = BLK // SEQ
MAGIC = 12582912.0
FLT_MAX = 3.4028234663852886e38


class Mem:

    def __init__(self, nc, ctx):
        self.nc, self.ctx = nc, ctx
        self.X = self.sb("X", [P, NT, D])
        self.xnT = self.sb("xnT", [P, KC, TOK])
        self.ctxT = self.sb("ctxT", [P, KC, TOK])
        self.ident = self.sb("ident", [P, P])
        self.psum = ctx.enter_context(nc.psum_tensor("psum", [P, 8, 512], F32))
        self.bank = [self.psum[:, i, :] for i in range(8)]

        self.apart = self.sem("apart")
        self.norms = 0
        self.norm_sems = [self.sem(f"ln_{n}") for n in "stats moments sd rstd xn turned bank_free added".split()]

    def wait_apart(self, eng, sem, value):
        eng.wait_ge(sem, value)
        eng.sem_inc(self.apart, 1)

    def sb(self, name, shape, dt=F32, ctx=None):
        return (ctx or self.ctx).enter_context(self.nc.sbuf_tensor(name, shape, dt))

    def sem(self, name):
        return self.ctx.enter_context(self.nc.semaphore(name))


class Chain:

    def __init__(self, eng, sem):
        self.eng, self.sem, self.n, self.base = eng, sem, 0, 0

    def enter(self, i, per):
        self.base = i * per

    def do(self, ins):
        self.n += 1
        ins.then_inc(self.sem, 1)
        self.eng.wait_ge(self.sem, self.base + self.n)


def load_inputs(nc, m, x, ctx_tokens, c_ident, x_ready):
    tile_in, turned, ctx_free, bank_free = (m.sem(n) for n in ("ld_tile", "ld_turned", "ld_free", "ld_bank_free"))
    ready = m.sem("ld_consts")
    with ExitStack() as own:
        C = m.sb("ctx_rows", [P, NT, D], ctx=own)
        with nc.Block() as block:
            @block.sync
            def _(sp):
                sp.dma_start(m.ident[:, :], c_ident).then_inc(ready, 16)
                sp.dma_start(C[:, :, :], ctx_tokens.rearrange("(t p) d -> p t d", p=P)).then_inc(tile_in, 16)
                sp.dma_start(m.X[:, :, :], x.rearrange("(t p) d -> p t d", p=P)).then_inc(x_ready, 16)

            @block.tensor
            def _(pe):
                pe.wait_ge(ready, 16)
                pe.wait_ge(tile_in, 16)
                for g in range(NBLK * KC):
                    b, c = divmod(g, KC)
                    if g >= 4:
                        pe.wait_ge(bank_free, g - 3)
                    for j in range(TPB):
                        last = pe.transpose(m.bank[g % 4][:, j * P:(j + 1) * P],
                                            C[:, b * TPB + j, c * P:(c + 1) * P], m.ident[:, :])
                    last.then_inc(turned, 1)

            @block.scalar
            def _(act):
                for g in range(NBLK * KC):
                    b, c = divmod(g, KC)
                    act.wait_ge(turned, g + 1)
                    act.activation(m.ctxT[:, c, b * BLK:(b + 1) * BLK], m.bank[g % 4][:, :],
                                   ACT.Copy).then_inc(bank_free, 1)
            @block.vector
            def _(dve):
                dve.wait_ge(x_ready, 16)


def layernorm(nc, m, add_to_x=False):
    stats_done, moments_done, sd_done, rstd_done, xn_ready, turned, bank_free, added = m.norm_sems
    r = m.norms
    m.norms += 1
    tag, tiles, turns, frees = f"ln{r}", r * NT, r * (NBLK * KC + 1), r * (NBLK + 1)
    with ExitStack() as own:
        stats = m.sb(f"{tag}_stats", [P, NT, 6], ctx=own)
        mom = m.sb(f"{tag}_mom", [P, NT, 2], ctx=own)
        sd = m.sb(f"{tag}_sd", [P, NT], ctx=own)
        rstd = m.sb(f"{tag}_rstd", [P, NT], ctx=own)
        eps = m.sb(f"{tag}_eps", [P, 1], ctx=own)
        xn = m.sb(f"{tag}_xn", [P, TPB, D], ctx=own)
        with nc.Block() as block:
            @block.vector
            def _(dve):
                dve.memset(eps[:, :], 1e-5).then_inc(moments_done, 1)
                with dve.Fori(0, NT) as t:
                    dve.bn_stats(stats[:, t, :], m.X[:, t, :]).then_inc(stats_done, 1)
                dve.wait_ge(stats_done, tiles + NT)
                for t in range(NT):
                    dve.bn_aggr(mom[:, t, :], stats[:, t, :]).then_inc(moments_done, 1)
                dve.wait_ge(sd_done, r + 1)
                dve.reciprocal(rstd[:, :], sd[:, :]).then_inc(rstd_done, 1)
                dve.wait_ge(rstd_done, r + 1)
                with dve.Fori(0, NBLK) as i:
                    dve.wait_ge(turned, turns + i * KC + 1)
                    for j in range(TPB):
                        t = i * TPB + j
                        dve.tensor_scalar(xn[:, j, :], m.X[:, t, :], mom[:, t, 0:1], rstd[:, ds(t, 1)],
                                          ALU.subtract, ALU.mult).then_inc(xn_ready, 1)
                        if add_to_x:
                            dve.wait_ge(xn_ready, tiles + t + 1)
                            dve.tensor_tensor(m.X[:, t, :], m.X[:, t, :], xn[:, j, :], ALU.add).then_inc(added, 1)
                    if add_to_x:
                        dve.wait_ge(added, i * TPB + TPB)

            @block.scalar
            def _(act):
                act.wait_ge(moments_done, (r + 1) * (NT + 1))
                act.activation(sd[:, :], mom[:, :, 1], ACT.Sqrt, bias=eps[:, :]).then_inc(sd_done, 1)
                act.sem_inc(bank_free, 1)
                with act.Fori(0, NBLK) as i:
                    for c in range(KC):
                        act.wait_ge(turned, turns + i * KC + c + 2)
                        last = act.activation(m.xnT[:, c, ds(i * BLK, BLK)], m.bank[c][:, :], ACT.Copy)
                    last.then_inc(bank_free, 1)

            @block.tensor
            def _(pe):
                pe.sem_inc(turned, 1)
                with pe.Fori(0, NBLK) as i:
                    pe.wait_ge(xn_ready, tiles + i * TPB + TPB)
                    pe.wait_ge(bank_free, frees + i + 1)
                    for c in range(KC):
                        for j in range(TPB):
                            last = pe.transpose(m.bank[c][:, j * P:(j + 1) * P], xn[:, j, c * P:(c + 1) * P],
                                                m.ident[:, :])
                        last.then_inc(turned, 1)


def rotary_recurrence(nc, m, w):
    NH, HD, HU = 6, 64, 3
    J = HD // 2
    U = NH // HU
    M = HU * J
    VD = NH * HD
    K, Q, VE, VO, AL, BE, GE, GO = range(8)
    NG = 8
    CONVK = 4
    TWO_PI = 6.283185307179586
    TWO_PI_HI = 6.28125
    TWO_PI_LO = TWO_PI - TWO_PI_HI
    PI_IN = 3.1415925
    loaded, prep, proj, evac, chain_s = (m.sem(f"a_{n}") for n in ("loaded", "prep", "proj", "evac", "chain"))
    angle, sincos, scanned, squares, meansq, sd_ready, gated, gates_used, outp, added = (m.sem(f"a_{n}") for n in (
        "angle", "sincos", "scanned", "squares", "meansq", "sd", "gated", "gates_used", "outp", "added"))
    with ExitStack() as own:
        def sb(n, s, dt=F32):
            return m.sb("a_" + n, s, dt, own)

        Wq, Wk, Wv, Wg = (sb(n, [P, KC, VD]) for n in ("Wq", "Wk", "Wv", "Wg"))
        Wab = sb("Wab", [P, KC, 2, NH])
        WabX = sb("WabX", [P, KC, 2, NH, J])
        Wo = sb("Wo", [M, U, 2, D])
        cw = sb("cw", [M, U, 4, CONVK])
        cwr = sb("cwr", [M, U, 2, CONVK])
        freq = sb("freq", [M, 2])
        rw = sb("rw", [M, 2])
        half_pi = sb("half_pi", [M, 1])
        eps = sb("eps", [M, 1])
        mean_w = sb("mean_w", [M, M])
        pad = sb("pad", [M, U, 4, BPB, SEQ + CONVK - 1])
        tab = sb("tab", [M, U, 2, BLK])
        gs = sb("gs", [M, U, 2, BLK])
        ang, n1, tmp = (sb(n, [M, BLK]) for n in ("ang", "n1", "tmp"))
        absang = sb("absang", [M, U, BLK])
        sc = sb("sc", [M, U, 2, BLK])
        v = sb("v", [M, 2, BLK])
        u = sb("u", [M, 2, BLK])
        t4 = sb("t4", [M, 4, BLK])
        al = sb("al", [M, BPB, SEQ])
        o = sb("o", [M, U, 2, BLK])
        sq = sb("sq", [M, U, 2, BLK])
        rstd = sb("rstd", [M, BLK])
        sdv = sb("sdv", [M, U, BLK])
        og = sb("og", [M, U, 2, BLK])

        def wcols(g, unit, c):
            if g in (AL, BE):
                return WabX[:, c, g - AL, unit * HU:(unit + 1) * HU, :].rearrange("p h j -> p (h j)")
            W, odd = {K: (Wk, 0), Q: (Wq, 0), VE: (Wv, 0), VO: (Wv, 1), GE: (Wg, 0), GO: (Wg, 1)}[g]
            return W[:, c, unit * HU * HD:(unit + 1) * HU * HD].rearrange("p (n two) -> p n two", two=2)[:, :, odd]

        NLOAD = 4 + 2 + 2 * U + U * 4 + 1 + 2 * HU + 1
        with nc.Block() as block:
            @block.sync
            def _(sp):
                with nc.allow_non_contiguous_dma("small, strided weights"):
                    for W, src in ((Wk, w["Wk"]), (Wq, w["Wq"]), (Wv, w["Wv"]), (Wg, w["Wg"])):
                        sp.dma_start(W[:, :, :], src.rearrange("(c p) n -> p c n", p=P)).then_inc(loaded, 16)
                    for n, src in enumerate((w["Wa"], w["Wb"])):
                        sp.dma_start(Wab[:, :, n, :], src.rearrange("(c p) n -> p c n", p=P)).then_inc(loaded, 16)
                    for unit in range(U):
                        rows = slice(unit * HU * HD, (unit + 1) * HU * HD)
                        for odd in range(2):
                            src = w["Wo"][rows, :].rearrange("(n two) d -> n two d", two=2)[:, odd, :]
                            sp.dma_start(Wo[:, unit, odd, :], src).then_inc(loaded, 16)
                        for n, (src, odd) in enumerate((("conv_k", 0), ("conv_q", 0), ("conv_v", 0), ("conv_v", 1))):
                            s = w[src][rows, :].rearrange("(n two) d -> n two d", two=2)[:, odd, :]
                            sp.dma_start(cw[:, unit, n, :], s).then_inc(loaded, 16)
                    sp.dma_start(freq[:, :], w["freq"]).then_inc(loaded, 16)
                    sp.dma_start(mean_w[:, :], w["mean_w"]).then_inc(loaded, 16)
                    for h in range(HU):
                        for odd in range(2):
                            s = w["rms_w"].rearrange("(j two) -> j two", two=2)[:, odd:odd + 1]
                            sp.dma_start(rw[h * J:(h + 1) * J, odd:odd + 1], s).then_inc(loaded, 16)

            @block.vector
            def _(dve):
                dve.memset(pad[:, :, :, :, 0:CONVK - 1].rearrange("p a b c d -> p (a b) c d"), 0.0).then_inc(prep, 1)
                dve.memset(half_pi[:, :], TWO_PI / 4).then_inc(prep, 1)
                dve.memset(eps[:, :], 1e-5).then_inc(prep, 1)
                dve.wait_ge(loaded, 16 * NLOAD)
                dve.tensor_copy(WabX[:, :, :, :, :].rearrange("p c w h j -> p (c w h) j"),
                                Wab[:, :, :, :].rearrange("p c w (h o) -> p (c w h) o", o=1)
                                .broadcast_to((P, KC * 2 * NH, J))).then_inc(prep, 1)
                for n in range(2):
                    dve.tensor_scalar(cwr[:, :, n, :], cw[:, :, n, :], freq[:, n:n + 1], None, ALU.mult).then_inc(prep, 1)
                dve.tensor_scalar(rw[:, :], rw[:, :], 0.5, None, ALU.mult).then_inc(prep, 1)
                dve.wait_ge(prep, 7)
                dve.sem_inc(gated, 3)

                def conv(c, unit, n, out, wt, first=True):
                    for j in range(CONVK):
                        src = pad[:, unit, n, :, j:j + SEQ]
                        dst = out.rearrange("p (b t) -> p b t", b=BPB)
                        if first and j == 0:
                            c.do(dve.tensor_scalar(dst, src, wt[:, j:j + 1], None, ALU.mult))
                        else:
                            c.do(dve.scalar_tensor_tensor(dst, src, wt[:, j:j + 1], dst, ALU.mult, ALU.add))

                STEPS = 30
                with dve.Fori(0, NBLK) as i:
                    c = Chain(dve, chain_s)
                    c.enter(i, STEPS * U)
                    for unit in range(U):
                        k = i * U + unit
                        dve.wait_ge(evac, k * NG + K + 1 + 4)
                        conv(c, unit, 0, ang[:, :], cwr[:, unit, 0, :])
                        dve.wait_ge(evac, k * NG + Q + 1 + 4)
                        conv(c, unit, 1, ang[:, :], cwr[:, unit, 1, :], first=False)
                        c.do(dve.tensor_scalar(n1[:, :], ang[:, :], 1 / TWO_PI, MAGIC, ALU.mult, ALU.add))
                        c.do(dve.tensor_scalar(n1[:, :], n1[:, :], MAGIC, None, ALU.subtract))
                        c.do(dve.scalar_tensor_tensor(ang[:, :], n1[:, :], -TWO_PI_HI, ang[:, :], ALU.mult, ALU.add))
                        c.do(dve.scalar_tensor_tensor(ang[:, :], n1[:, :], -TWO_PI_LO, ang[:, :], ALU.mult, ALU.add))
                        dve.tensor_scalar(absang[:, unit, :], ang[:, :], PI_IN, -PI_IN, ALU.min, ALU.max).then_inc(angle, 1)
                        dve.wait_ge(evac, k * NG + VO + 1 + 4)
                        conv(c, unit, 2, v[:, 0, :], cw[:, unit, 2, :])
                        conv(c, unit, 3, v[:, 1, :], cw[:, unit, 3, :])
                        dve.wait_ge(sincos, 2 * (k + 1))
                        s_, c_ = sc[:, unit, 0, :], sc[:, unit, 1, :]
                        ve, vo = v[:, 0, :], v[:, 1, :]
                        dve.tensor_tensor(t4[:, 0, :], ve, c_, ALU.mult)
                        dve.tensor_tensor(t4[:, 1, :], vo, s_, ALU.mult)
                        dve.tensor_tensor(t4[:, 2, :], vo, c_, ALU.mult)
                        c.do(dve.tensor_tensor(t4[:, 3, :], ve, s_, ALU.mult))
                        c.do(dve.tensor_tensor(u[:, 0, :], t4[:, 0, :], t4[:, 1, :], ALU.subtract))
                        c.do(dve.tensor_tensor(u[:, 1, :], t4[:, 2, :], t4[:, 3, :], ALU.add))
                        dve.wait_ge(evac, k * NG + BE + 1 + 4)
                        tb = tab[:, unit, 1, :]
                        c.do(dve.scalar_tensor_tensor(u[:, 0, :], tb, 1.0, u[:, 0, :], ALU.add, ALU.mult))
                        c.do(dve.scalar_tensor_tensor(u[:, 1, :], tb, 1.0, u[:, 1, :], ALU.add, ALU.mult))
                        alf = al[:, :, :].rearrange("p b t -> p (b t)")
                        c.do(dve.tensor_scalar(alf, tab[:, unit, 0, :], 0.5, 0.5, ALU.mult, ALU.add))
                        c.do(dve.memset(al[:, :, 0:1], 0.0))
                        for par in range(2):
                            dve.tensor_tensor_scan(o[:, unit, par, :], alf, u[:, par, :], 0.0,
                                                   ALU.mult, ALU.add).then_inc(scanned, 1)
                        dve.wait_ge(sd_ready, k + 2)
                        c.do(dve.reciprocal(rstd[:, :], sdv[:, unit, :]))
                        dve.wait_ge(evac, k * NG + GO + 1 + 4)
                        dve.wait_ge(outp, i * 2 + 1)
                        for par in range(2):
                            c.do(dve.scalar_tensor_tensor(t4[:, par, :], o[:, unit, par, :], rw[:, par:par + 1],
                                                          rstd[:, :], ALU.mult, ALU.mult))
                        for par in range(2):
                            dve.tensor_tensor(og[:, unit, par, :], t4[:, par, :], gs[:, unit, par, :],
                                              ALU.mult).then_inc(gated, 1)
                    assert c.n == STEPS * U, c.n
                    for half in range(2):
                        dve.wait_ge(outp, i * 2 + half + 2)
                        t = i * TPB + 2 * half
                        x2 = m.X[:, ds(t, 2), :].rearrange("p t d -> p (t d)")
                        dve.tensor_tensor(x2, m.bank[5 + half][:, :], x2, ALU.add).then_inc(added, 1)

            @block.scalar
            def _(act):
                act.sem_inc(evac, 4)
                act.sem_inc(sd_ready, 1)
                act.wait_ge(prep, 6)
                with act.Fori(0, NBLK) as i:
                    for unit in range(U):
                        k = i * U + unit
                        for g in range(NG):
                            act.wait_ge(proj, k * NG + g + 1)
                            if g == 0:
                                act.wait_ge(gated, k * 2 + 1)
                            src = m.bank[g % 4][0:M, :]
                            if g in (K, Q, VE, VO):
                                ins = act.activation(pad[:, unit, g, :, CONVK - 1:],
                                                     src.rearrange("p (b t) -> p b t", b=BPB), ACT.Copy)
                            elif g in (AL, BE):
                                ins = act.activation(tab[:, unit, g - AL, :], src, ACT.Tanh, scale=0.5)
                            else:
                                ins = act.activation(gs[:, unit, g - GE, :], src, ACT.Silu)
                            ins.then_inc(evac, 1)
                        act.wait_ge(angle, k + 1)
                        act.activation(sc[:, unit, 0, :], absang[:, unit, :], ACT.Sin).then_inc(sincos, 1)
                        act.activation(sdv[:, unit, :], absang[:, unit, :], ACT.Abs).then_inc(squares, 1)
                        act.wait_ge(squares, k * 3 + 1)
                        act.activation(sc[:, unit, 1, :], sdv[:, unit, :], ACT.Sin, scale=-1.0,
                                       bias=half_pi[:, :]).then_inc(sincos, 1)
                        act.wait_ge(scanned, 2 * (k + 1))
                        for par in range(2):
                            act.activation(sq[:, unit, par, :], o[:, unit, par, :], ACT.Square).then_inc(squares, 1)
                        act.wait_ge(meansq, k + 1)
                        act.wait_ge(sincos, 2 * (k + 1))
                        act.activation(sdv[:, unit, :], m.bank[4][0:M, :], ACT.Sqrt, bias=eps[:, :]).then_inc(sd_ready, 1)

            @block.tensor
            def _(pe):
                pe.wait_ge(prep, 6)
                pe.sem_inc(outp, 1)
                with pe.Fori(0, NBLK) as i:
                    for unit in range(U):
                        k = i * U + unit
                        for g in range(NG):
                            pe.wait_ge(evac, k * NG + g + 1)
                            for c in range(KC):
                                mm = pe.matmul(m.bank[g % 4][0:M, :], wcols(g, unit, c),
                                               m.xnT[:, c, ds(i * BLK, BLK)], start=(c == 0), stop=(c == KC - 1))
                            mm.then_inc(proj, 1)
                        for par in range(2):
                            pe.wait_ge(squares, k * 3 + 2 + par)
                            if par == 0:
                                pe.wait_ge(sd_ready, k + 1)
                            mm = pe.matmul(m.bank[4][0:M, :], mean_w[:, :], sq[:, unit, par, :],
                                           start=(par == 0), stop=(par == 1))
                        mm.then_inc(meansq, 1)
                    pe.wait_ge(gated, 3 + (i + 1) * U * 2)
                    for half in range(2):
                        for j in range(2):
                            tok = slice((2 * half + j) * P, (2 * half + j + 1) * P)
                            for n in range(2 * U):
                                mm = pe.matmul(m.bank[5 + half][:, j * D:(j + 1) * D], og[:, n // 2, n % 2, tok],
                                               Wo[:, n // 2, n % 2, :], start=(n == 0), stop=(n == 2 * U - 1))
                        mm.then_inc(outp, 1)


def gqa_cross_attention(nc, m, w):
    G, C, HD = 4, 4, 16
    NH = G * C
    GD = G * HD
    COLS = NH * SEQ
    loaded, prep, ctx_copied, proj, evac = (m.sem(f"b_{n}") for n in ("loaded", "prep", "ctx", "proj", "evac"))
    bias_ready, scores, biased, shifted, exped = (m.sem(f"b_{n}") for n in ("bias", "scores", "biased", "shifted", "exped"))
    turned, pt_ready, mixed, ao_ready, ao_turned, aot_ready, outp, added, chain_s = (m.sem(f"b_{n}") for n in (
        "turned", "pt", "mixed", "ao", "ao_turned", "aot", "outp", "added", "chain"))
    with ExitStack() as own:
        def sb(n, s, dt=F32):
            return m.sb("b_" + n, s, dt, own)

        WqR = sb("WqR", [P, KC, G, C, HD])
        Wq = sb("Wq", [P, KC, C, G, HD])
        Wk = sb("Wk", [P, KC, 2, GD])
        Wv = sb("Wv", [P, KC, GD])
        Wo = sb("Wo", [P, KC, D])
        alibi = sb("alibi", [P, NH, SEQ])
        gmask = sb("gmask", [P, G])
        hmask = sb("hmask", [P, 2])
        mask8 = sb("mask8", [P, NT, SEQ], U8)
        neg = sb("neg", [P, NT, SEQ])
        ctxS = sb("ctxS", [P, KC, BLK])
        QT = sb("QT", [P, 2, BLK])
        Kbd = sb("Kbd", [P, BPB, G, SEQ])
        Vbd = sb("Vbd", [P, BPB * 2, 2, HD])
        bias = sb("bias", [P, 2, NH, SEQ])
        S = sb("S", [P, 2, NH, SEQ])
        mx, tot, rtot = (sb(n, [P, NH]) for n in ("mx", "tot", "rtot"))
        PT = sb("PT", [P, 2 * C, P])
        ao = sb("ao", [P, G, C, HD])
        aoT = sb("aoT", [P, KC, P])
        NLOAD = 1 + 2 + 1 + 1 + 3 + 2
        with nc.Block() as block:
            @block.sync
            def _(sp):
                def load(dst, src):
                    sp.dma_start(dst, src).then_inc(loaded, 16)
                with nc.allow_non_contiguous_dma("small weights, mask rows"):
                    load(WqR[:, :, :, :, :].rearrange("p k g c d -> p k (g c d)"),
                         w["L0_xattn_Wq"].rearrange("(k p) n -> p k n", p=P))
                    for half in range(2):
                        load(Wk[:, :, half, :], w["L0_xattn_Wk"].rearrange("(k p) n -> p k n", p=P))
                    load(Wv[:, :, :], w["L0_xattn_Wv"].rearrange("(k p) n -> p k n", p=P))
                    load(Wo[:, :, :], w["L0_xattn_Wo"].rearrange("(k p) n -> p k n", p=P))
                    load(alibi[:, :, :].rearrange("p h k -> p (h k)"), w["alibi"])
                    load(gmask[:, :], w["gmask"])
                    load(hmask[:, :], w["hmask"])
                    for b in range(2):
                        src = w["mask_BxS2_bf1"].rearrange("(t b) k -> b t k", b=2)[b]
                        load(mask8[b * SEQ:(b + 1) * SEQ, :, :], src.partition_broadcast(SEQ))

            @block.gpsimd
            def _(pool):
                pool.wait_ge(prep, 1 + KC * C)
                with pool.Fori(0, NBLK) as i:
                    pool.wait_ge(proj, i * 4 + 4)
                    pool.tensor_copy(ctxS[:, :, :], m.ctxT[:, :, ds(i * BLK, BLK)]).then_inc(ctx_copied, 1)
                    for tt in range(TPB):
                        n = i * TPB + tt
                        pool.wait_ge(biased, n + 1)
                        pool.tensor_tensor(bias[:, tt % 2, :, :], alibi[:, :, :],
                                           neg[:, ds(n, 1), :].broadcast_to((P, NH, SEQ)), ALU.add).then_inc(bias_ready, 1)

            @block.scalar
            def _(act):
                act.wait_ge(prep, 1 + KC * C)
                with act.Fori(0, NBLK) as i:
                    for c in range(2):
                        act.wait_ge(proj, i * 4 + 4 + c + 1)
                        act.activation(QT[:, c, :], m.bank[c][:, :], ACT.Copy).then_inc(evac, 1)
                    act.wait_ge(proj, i * 4 + 4 + 3)
                    for g in range(G):
                        last = act.activation(Kbd[:, :, g, :], m.bank[2][:, :].rearrange("p (b k) -> p b k", k=SEQ),
                                              ACT.Copy, scale=gmask[:, g:g + 1])
                    last.then_inc(evac, 1)
                    act.wait_ge(proj, i * 4 + 4 + 4)
                    for h in range(2):
                        src = m.bank[3][:, :].rearrange("p (a h d) -> p a h d", h=2, d=HD)[:, :, h, :]
                        last = act.activation(Vbd[:, :, h, :], src, ACT.Copy, scale=hmask[:, h:h + 1])
                    last.then_inc(evac, 1)
                    for tt in range(TPB):
                        n = i * TPB + tt
                        act.wait_ge(shifted, n + 1)
                        act.activation(S[:, tt % 2, :, :], S[:, tt % 2, :, :], ACT.Exp).then_inc(exped, 1)
                        for h in range(2):
                            act.wait_ge(turned, 2 * n + h + 1)
                            act.activation(PT[:, 4 * h:4 * h + 4, :].rearrange("p a b -> p (a b)"), m.bank[6 + h][:, :],
                                           ACT.Copy).then_inc(pt_ready, 1)
                        act.wait_ge(ao_turned, n + 1)
                        act.activation(aoT[:, :, :].rearrange("p a b -> p (a b)"), m.bank[1][:, 0:KC * P],
                                       ACT.Copy).then_inc(aot_ready, 1)

            @block.vector
            def _(dve):
                dve.wait_ge(loaded, 16 * NLOAD)
                dve.tensor_scalar(neg[:, :, :], mask8[:, :, :], 1.0, FLT_MAX, ALU.subtract, ALU.mult).then_inc(prep, 1)
                for k in range(KC):
                    for c in range(C):
                        slot = 2 * (c % 2) + c // 2
                        dve.tensor_copy(Wq[:, k, slot, :, :], WqR[:, k, :, c, :]).then_inc(prep, 1)
                dve.sem_inc(biased, 2)
                dve.sem_inc(added, 1)

                def front(c, n, tt):
                    s = S[:, tt % 2, :, :]
                    dve.wait_ge(scores, n + 1)
                    dve.wait_ge(bias_ready, n + 1)
                    for h in range(2):
                        sl = slice(h * NH // 2, (h + 1) * NH // 2)
                        dve.scalar_tensor_tensor(s[:, sl, :].rearrange("p a b -> p (a b)"), m.bank[4 + h][:, :], HD ** -0.5,
                                                 bias[:, tt % 2, sl, :].rearrange("p a b -> p (a b)"), ALU.mult,
                                                 ALU.add).then_inc(*((biased, 1) if h else (chain_s, 1)))
                    c.n += 1
                    dve.wait_ge(biased, n + 3)
                    c.do(dve.tensor_reduce(mx[:, :], s, AX, ALU.max))
                    dve.tensor_tensor(s, s, mx[:, :].unsqueeze(2).broadcast_to((P, NH, SEQ)),
                                      ALU.subtract).then_inc(shifted, 1)

                STEPS = TPB * 4
                with dve.Fori(0, NBLK) as i:
                    c = Chain(dve, chain_s)
                    c.enter(i, STEPS)
                    front(c, i * TPB, 0)
                    for tt in range(TPB):
                        n = i * TPB + tt
                        dve.wait_ge(exped, n + 1)
                        c.do(dve.tensor_reduce(tot[:, :], S[:, tt % 2, :, :], AX, ALU.add))
                        c.do(dve.reciprocal(rtot[:, :], tot[:, :]))
                        dve.wait_ge(mixed, n + 1)
                        dve.tensor_tensor(ao[:, :, :, :].rearrange("p g c d -> p c g d"),
                                          m.bank[0][:, 0:D].rearrange("p (c g d) -> p c g d", c=C, g=G),
                                          rtot[:, :].rearrange("p (c g o) -> p c g o", c=C, o=1)
                                          .broadcast_to((P, C, G, HD)), ALU.mult).then_inc(ao_ready, 1)
                        if tt < TPB - 1:
                            front(c, n + 1, tt + 1)
                        dve.wait_ge(outp, n + 1)
                        dve.tensor_tensor(m.X[:, n, :], m.bank[3][:, 0:D], m.X[:, n, :], ALU.add).then_inc(added, 1)
                    assert c.n == STEPS, c.n

            @block.tensor
            def _(pe):
                pe.wait_ge(prep, 1 + KC * C)
                pe.sem_inc(proj, 4)

                def score(i, n, tt):
                    m.wait_apart(pe, biased, n + 2)
                    for b in range(2):
                        for c in range(C):
                            half = slice(64 * (c // 2), 64 * (c // 2) + 64)
                            tok = slice(tt * P + b * SEQ, tt * P + (b + 1) * SEQ)
                            mm = pe.matmul(m.bank[4 + c // 2][b * SEQ:(b + 1) * SEQ, (c % 2) * 256:(c % 2) * 256 + 256],
                                           QT[half, c % 2, tok],
                                           Kbd[half, 2 * tt + b, :, :].rearrange("p g k -> p (g k)"),
                                           start=True, stop=True)
                    mm.then_inc(scores, 1)

                with pe.Fori(0, NBLK) as i:
                    for c in range(2):
                        for k in range(KC):
                            mm = pe.matmul(m.bank[c][:, :], Wq[:, k, 2 * c:2 * c + 2, :, :].rearrange("p c g d -> p (c g d)"),
                                           m.xnT[:, k, ds(i * BLK, BLK)], start=(k == 0), stop=(k == KC - 1))
                        mm.then_inc(proj, 1)
                    for k in range(KC):
                        mm = pe.matmul(m.bank[2][:, :], Wk[:, k, :, :].rearrange("p a b -> p (a b)"),
                                       m.ctxT[:, k, ds(i * BLK, BLK)], start=(k == 0), stop=(k == KC - 1))
                    mm.then_inc(proj, 1)
                    pe.wait_ge(ctx_copied, i + 1)
                    pe.wait_ge(added, i * TPB + 1)
                    for b in range(BPB):
                        for half in range(2):
                            for k in range(KC):
                                mm = pe.matmul(m.bank[3][half * 64:half * 64 + 64, b * GD:(b + 1) * GD],
                                               ctxS[:, k, b * SEQ:(b + 1) * SEQ], Wv[:, k, :],
                                               start=(k == 0), stop=(k == KC - 1))
                    mm.then_inc(proj, 1)
                    pe.wait_ge(evac, i * 4 + 4)
                    score(i, i * TPB, 0)
                    for tt in range(TPB):
                        n = i * TPB + tt
                        if tt < TPB - 1:
                            score(i, n + 1, tt + 1)
                        pe.wait_ge(exped, n + 1)
                        for pr in range(2 * C):
                            mm = pe.transpose(m.bank[6 + pr // 4][:, (pr % 4) * P:(pr % 4 + 1) * P],
                                              S[:, tt % 2, 2 * pr:2 * pr + 2, :].rearrange("p a b -> p (a b)"),
                                              m.ident[:, :])
                            if pr % 4 == 3:
                                mm.then_inc(turned, 1)
                        pe.wait_ge(pt_ready, 2 * n + 2)
                        for b in range(2):
                            for pr in range(2 * C):
                                mm = pe.matmul(m.bank[0][b * SEQ:(b + 1) * SEQ, pr * 32:pr * 32 + 32],
                                               PT[:, pr, b * SEQ:(b + 1) * SEQ],
                                               Vbd[:, (2 * tt + b) * 2 + pr % 2, :, :].rearrange("p a b -> p (a b)"),
                                               start=True, stop=True)
                        mm.then_inc(mixed, 1)
                        pe.wait_ge(ao_ready, n + 1)
                        for k in range(KC):
                            mm = pe.transpose(m.bank[1][:, k * P:(k + 1) * P],
                                              ao[:, 2 * k:2 * k + 2, :, :].rearrange("p g c d -> p (g c d)"), m.ident[:, :])
                        mm.then_inc(ao_turned, 1)
                        pe.wait_ge(aot_ready, n + 1)
                        pe.wait_ge(added, n + 1)
                        for k in range(KC):
                            mm = pe.matmul(m.bank[3][:, 0:D], aoT[:, k, :], Wo[:, k, :], start=(k == 0), stop=(k == KC - 1))
                        mm.then_inc(outp, 1)


class Router:
    NE = 16

    def __init__(self, m, tag, own, top, shared):
        self.m, self.top, self.ne = m, top, self.NE + shared

        def sb(n, s, dt=F32):
            return m.sb(f"{tag}_{n}", s, dt, own)
        self.route = sb("route", [P, NT, self.ne])
        self.score = sb("score", [P, NT, self.NE])
        self.iota = sb("iota", [P, self.NE])
        self.val = sb("val", [P, NT, 8])
        self.idx = sb("idx", [P, NT, 8], U32)
        self.idxf = sb("idxf", [P, NT, 8])
        self.tot = sb("tot", [P, NT])
        self.oh = sb("oh", [P, NT, self.NE])
        self.logits, self.scored, self.chain, self.done = (m.sem(f"{tag}_{n}") for n in (
            "logits", "scored", "rchain", "routed"))

    def tensor(self, pe, wa, bank):
        for t in range(NT):
            for k in range(KC):
                mm = pe.matmul(bank[:, t * self.NE:(t + 1) * self.NE], self.m.xnT[:, k, t * P:(t + 1) * P], wa[:, k, :],
                               start=(k == 0), stop=(k == KC - 1))
        mm.then_inc(self.logits, 1)

    def scalar(self, act, bank):
        act.wait_ge(self.logits, 1)
        act.activation(self.score[:, :, :].rearrange("p t e -> p (t e)"), bank[:, 0:NT * self.NE],
                       ACT.Sigmoid).then_inc(self.scored, 1)

    def vector(self, dve, bias=None):
        c = Chain(dve, self.chain)
        shape = (P, NT, self.NE)
        dve.wait_ge(self.scored, 1)
        if bias is not None:
            c.do(dve.tensor_tensor(self.score[:, :, :], self.score[:, :, :],
                                   bias.unsqueeze(1).broadcast_to(shape), ALU.add))
        c.do(dve.memset(self.route[:, :, :], 1.0))
        for t in range(NT):
            last = dve.max(self.val[:, t, :], self.score[:, t, :])
        c.do(last)
        for t in range(NT):
            last = dve.max_index(self.idx[:, t, :], self.val[:, t, :], self.score[:, t, :])
        c.do(last)
        c.do(dve.tensor_copy(self.idxf[:, :, :], self.idx[:, :, :]))
        c.do(dve.tensor_reduce(self.tot[:, :], self.val[:, :, 0:self.top], AX, ALU.add))
        c.do(dve.reciprocal(self.tot[:, :], self.tot[:, :]))
        c.do(dve.tensor_tensor(self.val[:, :, :], self.val[:, :, :],
                               self.tot[:, :].unsqueeze(2).broadcast_to((P, NT, 8)), ALU.mult))
        r = self.route[:, :, 0:self.NE]
        for j in range(self.top):
            out = r if j == 0 else self.oh[:, :, :]
            c.do(dve.tensor_tensor(out, self.iota[:, :].unsqueeze(1).broadcast_to(shape),
                                   self.idxf[:, :, j:j + 1].broadcast_to(shape), ALU.is_equal))
            c.do(dve.tensor_tensor(out, out, self.val[:, :, j:j + 1].broadcast_to(shape), ALU.mult))
            if j:
                c.do(dve.tensor_tensor(r, r, self.oh[:, :, :], ALU.add))
        dve.sem_inc(self.done, 1)


def experts_top2(nc, m, w):
    NE, SH, F = 16, 2, 128
    PAIRS = NE // 2
    (loaded, w_in0, w_in1, gate_up, gated, hready, downs, summed, routed_T, rt_ready, biased) = (
        m.sem(f"c_{n}") for n in ("loaded", "w0", "w1", "gate_up", "gelu", "h", "downs", "summed", "rT", "rTs", "b2"))
    w_in = (w_in0, w_in1)
    with ExitStack() as own:
        def sb(n, s, dt=F32):
            return m.sb("c_" + n, s, dt, own)

        wa = sb("wa", [P, KC, NE])
        Wg, Wu = (sb(n, [P, 2, KC, F]) for n in ("Wg", "Wu"))
        Wd = sb("Wd", [F, 2, D])
        gb, ub = (sb(n, [F, NE + SH]) for n in ("gb", "ub"))
        b2 = sb("b2", [NE + SH, D])
        gelu = sb("gelu", [F, 2, BLK])
        h = sb("h", [F, 2, BLK])
        rT = sb("rT", [NE + SH, TPB, P])
        R = Router(m, "c", own, 2, SH)
        src_r = {"Wg": w["L0_ffn_rg"], "Wu": w["L0_ffn_rw1"], "Wd": w["L0_ffn_rw2"]}
        src_s = {"Wg": w["L0_ffn_sg"], "Wu": w["L0_ffn_sw1"], "Wd": w["L0_ffn_sw2"]}
        with nc.Block() as block:
            @block.sync
            def _(sp):
                def load(dst, src):
                    sp.dma_start(dst, src).then_inc(loaded, 16)

                def weights(src, e, slot):
                    for W, n in ((Wg, "Wg"), (Wu, "Wu")):
                        sp.dma_start(W[:, slot, :, :], src[n][e].rearrange("(k p) f -> p k f", p=P)).then_inc(w_in[slot], 16)
                    sp.dma_start(Wd[:, slot, :], src["Wd"][e]).then_inc(w_in[slot], 16)

                with nc.allow_non_contiguous_dma("biases to partitions"):
                    load(wa[:, :, :], w["L0_ffn_wa"].rearrange("(k p) e -> p k e", p=P))
                    load(R.iota[:, :], w["iota16"].partition_broadcast(P))
                    for dst, r, s in ((gb, "rgb", "sgb"), (ub, "rb1", "sb1")):
                        load(dst[:, 0:NE], w["L0_ffn_" + r].rearrange("e f -> f e"))
                        load(dst[:, NE:], w["L0_ffn_" + s].rearrange("e f -> f e"))
                    load(b2[0:NE, :], w["L0_ffn_rb2"])
                    load(b2[NE:, :], w["L0_ffn_sb2"])
                with sp.Fori(0, PAIRS) as i:
                    for slot in range(2):
                        sp.wait_ge(downs, i * 8 + 4 * (slot + 1))
                        weights(src_r, i * 2 + slot, slot)
                for slot in range(2):
                    sp.wait_ge(downs, PAIRS * 8 + 4 * (slot + 1))
                    weights(src_s, slot, slot)

            @block.scalar
            def _(act):
                R.scalar(act, m.bank[0])
                for q in range(NBLK):
                    act.wait_ge(routed_T, q + 1)
                    act.activation(rT[:, :, :].rearrange("p a b -> p (a b)"), m.bank[1][0:NE + SH, :],
                                   ACT.Copy).then_inc(rt_ready, 1)

                def pair(i, e0):
                    for st in range(8):
                        slot, q = divmod(st, NBLK)
                        m.wait_apart(act, gate_up, i * 8 + st + 1)
                        act.activation(gelu[:, q % 2, :], m.bank[q % 2][:, :], ACT.Gelu,
                                       bias=gb[:, ds(e0 + slot, 1)]).then_inc(gated, 1)

                with act.Fori(0, PAIRS) as i:
                    pair(i, i * 2)
                pair(PAIRS, NE)

            @block.vector
            def _(dve):
                dve.wait_ge(loaded, 16 * 8)
                R.vector(dve)
                for q in range(NBLK):
                    dve.wait_ge(biased, 2 * q + 2)
                    for half in range(2):
                        t = q * TPB + 2 * half
                        x2 = m.X[:, t:t + 2, :].rearrange("p t d -> p (t d)")
                        dve.tensor_tensor(x2, m.bank[2 + half][:, :], x2, ALU.add).then_inc(summed, 1)
                dve.sem_inc(hready, 2)

                def hidden(i, e0, st):
                    slot, q = divmod(st, NBLK)
                    dve.wait_ge(gated, i * 8 + st + 1)
                    dve.scalar_tensor_tensor(h[:, q % 2, :], m.bank[2 + q % 2][:, :], ub[:, ds(e0 + slot, 1)],
                                             gelu[:, q % 2, :], ALU.add, ALU.mult).then_inc(hready, 1)

                def add(i, e0, st):
                    slot, q = divmod(st, NBLK)
                    dve.wait_ge(downs, 8 + i * 8 + st + 1)
                    for j in range(TPB):
                        t = q * TPB + j
                        last = dve.scalar_tensor_tensor(
                            m.X[:, t, :], m.bank[4 + 2 * (q % 2) + j // 2][:, (j % 2) * D:(j % 2 + 1) * D],
                            R.route[:, t, ds(e0 + slot, 1)], m.X[:, t, :], ALU.mult, ALU.add)
                    last.then_inc(summed, 1)

                def pair(i, e0):
                    hidden(i, e0, 0)
                    for st in range(8):
                        if st < 7:
                            hidden(i, e0, st + 1)
                        add(i, e0, st)

                with dve.Fori(0, PAIRS) as i:
                    pair(i, i * 2)
                pair(PAIRS, NE)

            @block.tensor
            def _(pe):
                pe.sem_inc(downs, 8)
                pe.wait_ge(loaded, 16 * 8)
                R.tensor(pe, wa, m.bank[0])
                pe.wait_ge(R.done, 1)
                for q in range(NBLK):
                    if q:
                        pe.wait_ge(summed, 2 * q)
                    for j in range(TPB):
                        mm = pe.transpose(m.bank[1][0:NE + SH, j * P:(j + 1) * P], R.route[:, q * TPB + j, :], m.ident[:, :])
                    mm.then_inc(routed_T, 1)
                    pe.wait_ge(rt_ready, q + 1)
                    for j in range(TPB):
                        mm = pe.matmul(m.bank[2 + j // 2][:, (j % 2) * D:(j % 2 + 1) * D], rT[:, j, :], b2[:, :],
                                       start=True, stop=True)
                        if j % 2:
                            mm.then_inc(biased, 1)
                pe.wait_ge(summed, 2 * NBLK)

                def gate_and_up(i, st):
                    slot, q = divmod(st, NBLK)
                    if q == 0:
                        pe.wait_ge(w_in[slot], i * 48 + 48)
                    pe.wait_ge(hready, i * 8 + st + 1)
                    for W, bank in ((Wg, q % 2), (Wu, 2 + q % 2)):
                        for k in range(KC):
                            mm = pe.matmul(m.bank[bank][:, :], W[:, slot, k, :], m.xnT[:, k, q * BLK:(q + 1) * BLK],
                                           start=(k == 0), stop=(k == KC - 1))
                    mm.then_inc(gate_up, 1)

                def down(i, st):
                    slot, q = divmod(st, NBLK)
                    pe.wait_ge(hready, 2 + i * 8 + st + 1)
                    pe.wait_ge(summed, 2 * NBLK - 2 + i * 8 + st + 1)
                    for j in range(TPB):
                        mm = pe.matmul(m.bank[4 + 2 * (q % 2) + j // 2][:, (j % 2) * D:(j % 2 + 1) * D],
                                       h[:, q % 2, j * P:(j + 1) * P], Wd[:, slot, :], start=True, stop=True)
                    mm.then_inc(downs, 1)

                def pair(i):
                    gate_and_up(i, 0)
                    for st in range(8):
                        if st < 7:
                            gate_and_up(i, st + 1)
                        down(i, st)

                with pe.Fori(0, PAIRS) as i:
                    pair(i)
                pair(PAIRS)


def lightning_attention(nc, m, w):
    NH, HD = 16, 128
    Q, K, V, GT = range(4)
    PAIRS = NH // 2
    SPH = NBLK
    SPP = 2 * SPH
    (loaded, prep, decays, wload, wturned, wt_ready, proj, evac, scored, masked, mixed, ocopied, squared, yready, outs,
     summed, ssq, sd_ready, chain_s) = (m.sem(f"d_{n}") for n in (
        "loaded", "prep", "decays", "wload", "wturned", "wt_ready", "proj", "evac", "scored", "masked", "mixed",
        "ocopied", "squared", "y", "outs", "summed", "ssq", "sd", "chain"))
    with ExitStack() as own:
        def sb(n, s, dt=F32):
            return m.sb("d_" + n, s, dt, own)

        Wn = sb("Wn", [P, 4, D])
        Won = sb("Won", [P, KC, HD])
        WT = sb("WT", [P, 2, KC, 4, HD])
        WoT = sb("WoT", [HD, 2, D])
        nw = sb("nw", [HD, NH])
        slope = sb("slope", [P, NH])
        rel = sb("rel", [P, P])
        tri = sb("tri", [P, P])
        decay = sb("decay", [P, NH, P])
        qT, kT, gt, vS, oS = (sb(n, [P, 2, BLK]) for n in ("qT", "kT", "gt", "vS", "oS"))
        A = sb("A", [P, TPB, P])
        y = sb("y", [P, BLK])
        sq = sb("sq", [P, BLK])
        SQ = sb("SQ", [P, TOK])
        ACC = sb("ACC", [P, NT, D])
        ones = sb("ones", [P, 1])
        eps = sb("eps", [P, 1])
        sd = sb("sd", [P, NT])
        rstd = sb("rstd", [P, NT])
        NPREP = 6
        with nc.Block() as block:
            @block.sync
            def _(sp):
                def load(dst, src):
                    sp.dma_start(dst, src).then_inc(loaded, 16)

                with nc.allow_non_contiguous_dma("norm_w to partitions"):
                    load(nw[:, :], w["L1_attn_norm_w"].rearrange("(h d) -> d h", d=HD))
                load(slope[:, :], w["L1_attn_slope_rate"].rearrange("h a b -> (h a b)").partition_broadcast(P))
                load(rel[:, :], w["rel"])
                load(tri[:, :], w["tri"])
                with sp.Fori(0, NH) as h:
                    sp.wait_ge(wturned, h + 1)
                    sp.dma_start(Wn[:, 0:3, :], w["L1_attn_w_qkv"][ds(h * 3 * HD, 3 * HD), :]
                                 .rearrange("(m o) f -> o m f", o=HD)).then_inc(wload, 16)
                    sp.dma_start(Wn[:, 3, :], w["L1_attn_w_gate"][ds(h * HD, HD), :]).then_inc(wload, 16)
                    sp.dma_start(Won[:, :, :], w["L1_attn_w_out"][:, ds(h * HD, HD)]
                                 .rearrange("(k p) o -> p k o", p=P)).then_inc(wload, 16)

            @block.gpsimd
            def _(pool):
                pool.memset(SQ[:, :], 0.0).then_inc(squared, 4)
                with pool.Fori(0, NH) as h:
                    for q in range(SPH):
                        s = h * SPH + q
                        pool.wait_ge(ocopied, s + 2)
                        pool.wait_ge(squared, 2 * s + 4)
                        o = oS[:, q % 2, :]
                        pool.tensor_tensor(sq[:, :], o, o, ALU.mult).then_inc(squared, 1)
                        pool.wait_ge(squared, 2 * s + 5)
                        acc = SQ[:, q * BLK:(q + 1) * BLK]
                        pool.tensor_tensor(acc, acc, sq[:, :], ALU.add).then_inc(squared, 1)

            @block.scalar
            def _(act):
                act.wait_ge(prep, NPREP)
                for h in range(NH):
                    act.activation(decay[:, h, :], rel[:, :], ACT.Exp, scale=slope[:, h:h + 1]).then_inc(decays, 1)
                act.sem_inc(evac, 4)
                act.sem_inc(ocopied, 1)

                def turn(h, slot):
                    m.wait_apart(act, wturned, h + 2)
                    for k in range(KC):
                        act.activation(WT[:, slot, k, :, :].rearrange("p a b -> p (a b)"), m.bank[6 + k][:, :],
                                       ACT.Copy).then_inc(wt_ready, 1)
                    act.activation(WoT[:, slot, :], m.bank[4][:, 0:D], ACT.Copy,
                                   scale=nw[:, ds(h, 1)]).then_inc(wt_ready, 1)

                def qkg(s, q):
                    for n, dst in enumerate((qT, kT, gt)):
                        act.wait_ge(proj, 4 * s + n + 1)
                        if n == 2:
                            ins = act.activation(dst[:, q % 2, :], m.bank[n][:, :], ACT.Tanh, scale=0.5)
                        else:
                            ins = act.activation(dst[:, q % 2, :], m.bank[n][:, :], ACT.Silu)
                        ins.then_inc(evac, 1)

                def values(s, q):
                    act.wait_ge(proj, 4 * s + 4)
                    act.activation(vS[:, q % 2, :], m.bank[3][:, :], ACT.Silu).then_inc(evac, 1)

                def pair(i, last):
                    for st in range(SPP):
                        u, q = divmod(st, SPH)
                        s, h = i * SPP + st, i * 2 + u
                        end = last and st == SPP - 1
                        if not end:
                            qkg(s + 1, q + 1)
                        act.wait_ge(squared, 2 * s + 2)
                        act.wait_ge(mixed, s + 1)
                        act.activation(oS[:, q % 2, :], m.bank[5][:, :], ACT.Copy).then_inc(ocopied, 1)
                        if not end:
                            values(s + 1, q + 1)
                        if q == 1 and not (last and u == 1):
                            turn(h + 1, 1 - u)

                turn(0, 0)
                qkg(0, 0)
                values(0, 0)
                with act.Fori(0, PAIRS - 1) as i:
                    pair(i, False)
                pair(PAIRS - 1, True)
                act.wait_ge(ssq, 1)
                act.activation(sd[:, :], m.bank[0][:, 0:NT], ACT.Sqrt, scale=1.0 / (NH * HD),
                               bias=eps[:, :]).then_inc(sd_ready, 1)

            @block.vector
            def _(dve):
                dve.memset(ACC[:, :, :], 0.0).then_inc(prep, 1)
                dve.memset(ones[:, :], 1.0).then_inc(prep, 1)
                dve.memset(eps[:, :], 1e-6).then_inc(prep, 1)
                dve.wait_ge(loaded, 16 * 4)
                dve.tensor_scalar(nw[:, :], nw[:, :], 0.5, None, ALU.mult).then_inc(prep, 1)
                dve.tensor_scalar(slope[:, :], slope[:, :], -1.0, None, ALU.mult).then_inc(prep, 2)
                dve.wait_ge(decays, NH)
                dve.tensor_tensor(decay[:, :, :], decay[:, :, :], tri[:, :].unsqueeze(1).broadcast_to((P, NH, P)),
                                  ALU.mult).then_inc(prep, 1)
                dve.wait_ge(prep, NPREP + 1)
                dve.sem_inc(masked, 1)
                dve.sem_inc(summed, 1)
                with dve.Fori(0, NH) as h:
                    for q in range(SPH):
                        s = h * SPH + q
                        dve.wait_ge(scored, s + 1)
                        dve.tensor_tensor(A[:, :, :], m.bank[4][:, :].rearrange("p (a b) -> p a b", a=TPB),
                                          decay[:, ds(h, 1), :].broadcast_to((P, TPB, P)), ALU.mult).then_inc(masked, 1)
                        dve.wait_ge(ocopied, s + 2)
                        dve.wait_ge(evac, 4 + 4 * s + 3)
                        dve.scalar_tensor_tensor(y[:, :], gt[:, q % 2, :], 1.0, oS[:, q % 2, :], ALU.add,
                                                 ALU.mult).then_inc(yready, 1)
                        dve.wait_ge(outs, s + 1)
                        for half in range(2):
                            t = q * TPB + 2 * half
                            a2 = ACC[:, t:t + 2, :].rearrange("p t d -> p (t d)")
                            last = dve.tensor_tensor(a2, m.bank[6 + half][:, :], a2, ALU.add)
                        last.then_inc(summed, 1)
                dve.wait_ge(sd_ready, 1)
                dve.reciprocal(rstd[:, :], sd[:, :]).then_inc(chain_s, 1)
                dve.wait_ge(chain_s, 1)
                dve.wait_ge(summed, 1 + NH * SPH)
                for t in range(NT):
                    dve.scalar_tensor_tensor(m.X[:, t, :], ACC[:, t, :], rstd[:, t:t + 1], m.X[:, t, :], ALU.mult, ALU.add)

            @block.tensor
            def _(pe):
                pe.sem_inc(wturned, 1)
                pe.wait_ge(prep, NPREP)

                def turn(h):
                    pe.wait_ge(wload, 48 * h + 48)
                    for k in range(KC):
                        for n in range(4):
                            pe.transpose(m.bank[6 + k][:, n * HD:(n + 1) * HD], Wn[:, n, k * P:(k + 1) * P], m.ident[:, :])
                    for k in range(KC):
                        mm = pe.transpose(m.bank[4][:, k * P:(k + 1) * P], Won[:, k, :], m.ident[:, :])
                    mm.then_inc(wturned, 1)

                def wide(s, q, slot, n):
                    b = {Q: 0, K: 1, GT: 2}[n]
                    pe.wait_ge(evac, 4 * s + b + 1)
                    for k in range(KC):
                        mm = pe.matmul(m.bank[b][:, :], WT[:, slot, k, n, :], m.xnT[:, k, q * BLK:(q + 1) * BLK],
                                       start=(k == 0), stop=(k == KC - 1))
                    mm.then_inc(proj, 1)

                def values(s, q, slot):
                    pe.wait_ge(evac, 4 * s + 4)
                    for j in range(TPB):
                        t = q * TPB + j
                        for k in range(KC):
                            mm = pe.matmul(m.bank[3][:, j * HD:(j + 1) * HD], m.xnT[:, k, t * P:(t + 1) * P],
                                           WT[:, slot, k, V, :], start=(k == 0), stop=(k == KC - 1))
                    mm.then_inc(proj, 1)

                def pair(i, last):
                    for st in range(SPP):
                        u, q = divmod(st, SPH)
                        s, h = i * SPP + st, i * 2 + u
                        end = last and st == SPP - 1
                        nslot, nq = ((st + 1) // SPH) % 2, (q + 1) % SPH
                        if not end:
                            wide(s + 1, nq, nslot, Q)
                            wide(s + 1, nq, nslot, K)
                        pe.wait_ge(evac, 4 + 4 * s + 2)
                        pe.wait_ge(masked, s + 1)
                        for j in range(TPB):
                            tok = slice(j * P, (j + 1) * P)
                            mm = pe.matmul(m.bank[4][:, tok], kT[:, q % 2, tok], qT[:, q % 2, tok], start=True, stop=True)
                        mm.then_inc(scored, 1)
                        if not end:
                            wide(s + 1, nq, nslot, GT)
                        pe.wait_ge(masked, s + 2)
                        pe.wait_ge(evac, 4 + 4 * s + 4)
                        pe.wait_ge(ocopied, s + 1)
                        for j in range(TPB):
                            tok = slice(j * P, (j + 1) * P)
                            mm = pe.matmul(m.bank[5][:, tok], vS[:, q % 2, tok], A[:, j, :], start=True, stop=True)
                        mm.then_inc(mixed, 1)
                        if not end:
                            values(s + 1, nq, nslot)
                        pe.wait_ge(yready, s + 1)
                        pe.wait_ge(summed, s + 1)
                        for j in range(TPB):
                            mm = pe.matmul(m.bank[6 + j // 2][:, (j % 2) * D:(j % 2 + 1) * D], y[:, j * P:(j + 1) * P],
                                           WoT[:, u, :], start=True, stop=True)
                        mm.then_inc(outs, 1)
                        if q == 1 and not (last and u == 1):
                            pe.wait_ge(summed, s + 2)
                            turn(h + 1)
                            pe.wait_ge(wt_ready, 3 * h + 6)

                turn(0)
                pe.wait_ge(wt_ready, 3)
                wide(0, 0, 0, Q)
                wide(0, 0, 0, K)
                wide(0, 0, 0, GT)
                values(0, 0, 0)
                with pe.Fori(0, PAIRS - 1) as i:
                    pair(i, False)
                pair(PAIRS - 1, True)
                pe.wait_ge(squared, 4 + 2 * NH * SPH)
                for t in range(NT):
                    mm = pe.matmul(m.bank[0][:, t:t + 1], SQ[:, t * P:(t + 1) * P], ones[:, :], start=True, stop=True)
                mm.then_inc(ssq, 1)


def quantised_attention(nc, m, w):
    H, HD = 16, 16
    PR = H // 2
    U16 = mybir.dt.uint16
    KT = TOK // P
    HALF = TOK // 2
    LN255 = float(np.log(255.0))
    names = "loaded prep copied proj taken packed turned stored".split()
    loaded, prep, copied, proj, taken, packed, turned, stored = (m.sem(f"e_{n}") for n in names)
    chain_s, vmaxed, vall, v_ready = (m.sem(f"e_{n}") for n in ("chain", "vmax", "vall", "v"))
    q_here, scored, biased, exped, tturned, evac0, evac1, mixed, normed, chain2 = (m.sem(f"e_{n}") for n in (
        "q_here", "scored", "biased", "exped", "tturned", "evac0", "evac1", "mixed", "normed", "chain2"))
    xb, o_ready, o_turned, ot_ready, outp, added, chain3 = (m.sem(f"e_{n}") for n in (
        "xb", "o", "o_turned", "oT", "outp", "added", "chain3"))
    with ExitStack() as own:
        def sb(n, s, dt=F32, ctx=own):
            return m.sb("e_" + n, s, dt, ctx)

        QT = sb("QT", [P, NT * PR, P], BF16)
        KTt = sb("KT", [P, PR, TOK], BF16)
        Vi = sb("Vi", [P, KT, H, HD], BF16)
        sq = sb("sq", [P, NT * H])
        nsq = sb("nsq", [P, NT * H])
        sv = sb("sv", [P, D])
        identb = sb("identb", [P, P], BF16)
        bp = sb("bp", [P, D])
        Wp = sb("Wp", [P, KC, D])
        with ExitStack() as first:
            def sb1(n, s, dt=F32):
                return m.sb("e_" + n, s, dt, first)

            Wq = sb1("Wq", [P, KC, D])
            Wkv = sb1("Wkv", [P, KC, 2, D])
            bias = sb1("bias", [P, 3, D])
            xs, cs = sb1("xs", [P, KC, BLK]), sb1("cs", [P, KC, BLK])
            V32 = sb1("V32", [P, NT, D])
            z = sb1("z", [P, 2, H, HD])
            am, s_, rs = (sb1(n, [P, 2, H]) for n in ("am", "s", "rs"))
            k32, r32 = sb1("k32", [P, H, HD]), sb1("r32", [P, H, HD])
            Tq, Tk = (sb1(n, [P, 2, H, 4, HD], BF16) for n in ("Tq", "Tk"))
            vm, vma, rv = (sb1(n, [P, D]) for n in ("vm", "vma", "rv"))
            with nc.Block() as block:
                @block.sync
                def _(sp):
                    def load(dst, src):
                        sp.dma_start(dst, src).then_inc(loaded, 16)
                    load(Wq[:, :, :], w["L1_xattn_Wq"].rearrange("(k p) n -> p k n", p=P))
                    load(Wkv[:, :, :, :].rearrange("p k a n -> p k (a n)"), w["L1_xattn_Wkv"].rearrange("(k p) n -> p k n", p=P))
                    load(Wp[:, :, :], w["L1_xattn_Wp"].rearrange("(k p) n -> p k n", p=P))
                    load(bias[:, 0, :], w["L1_xattn_bq"].partition_broadcast(P))
                    load(bias[:, 1:3, :].rearrange("p a n -> p (a n)"), w["L1_xattn_bkv"].partition_broadcast(P))
                    load(bp[:, :], w["L1_xattn_bp"].partition_broadcast(P))

                @block.gpsimd
                def _(pool):
                    pool.wait_ge(vmaxed, 1)
                    pool.partition_all_reduce(vma[:, :], vm[:, :], P, bass.bass_isa.ReduceOp.max).then_inc(vall, 1)
                    pool.wait_ge(loaded, 16 * 6)
                    pool.tensor_tensor(m.X[:, :, :], m.X[:, :, :], bp[:, :].unsqueeze(1).broadcast_to((P, NT, D)),
                                       ALU.add).then_inc(xb, 1)

                @block.scalar
                def _(act):
                    act.sem_inc(stored, 2)
                    with act.Fori(0, NBLK) as i:
                        act.wait_ge(proj, i * TPB + 1)
                        act.activation(xs[:, :, :], m.xnT[:, :, ds(i * BLK, BLK)], ACT.Copy).then_inc(copied, 1)
                        act.activation(cs[:, :, :], m.ctxT[:, :, ds(i * BLK, BLK)], ACT.Copy).then_inc(copied, 1)
                        for tt in range(TPB):
                            t = i * TPB + tt
                            m.wait_apart(act, turned, t + 3)
                            b = 4 + 2 * (tt % 2)
                            act.activation(QT[:, ds(t * PR, PR), :].rearrange("p a b -> p (a b)"),
                                           m.bank[b].bitcast(BF16), ACT.Copy)
                            act.activation(KTt[:, :, ds(t * P, P)], m.bank[b + 1].bitcast(BF16)
                                           .rearrange("p (a b) -> p a b", a=PR), ACT.Copy).then_inc(stored, 1)

                @block.vector
                def _(dve):
                    dve.tensor_copy(identb[:, :], m.ident[:, :]).then_inc(prep, 1)
                    dve.memset(Tq[:, :, :, :, :].rearrange("p a b c d -> p (a b c d)"), 0.0).then_inc(prep, 1)
                    dve.memset(Tk[:, :, :, :, :].rearrange("p a b c d -> p (a b c d)"), 0.0).then_inc(prep, 1)
                    dve.wait_ge(loaded, 16 * 6)
                    dve.tensor_scalar(bias[:, 0, :], bias[:, 0, :], HD ** -0.5, None, ALU.mult).then_inc(prep, 1)
                    dve.wait_ge(prep, 4)
                    dve.sem_inc(taken, 2)
                    STEPS = 10
                    with dve.Fori(0, NBLK) as i:
                        c = Chain(dve, chain_s)
                        c.enter(i, STEPS * TPB)
                        for tt in range(TPB):
                            t = i * TPB + tt
                            sl = tt % 2
                            dve.wait_ge(proj, t + 2)
                            A, B = m.bank[sl], m.bank[2 + sl]
                            for n, sc in ((0, HD ** -0.5), (1, 1.0)):
                                last = dve.scalar_tensor_tensor(z[:, n, :, :].rearrange("p h d -> p (h d)"),
                                                                A[:, n * D:(n + 1) * D], sc, bias[:, n, :], ALU.mult, ALU.add)
                            c.do(last)
                            dve.tensor_tensor(V32[:, t, :], B[:, 0:D], bias[:, 2, :], ALU.add).then_inc(taken, 1)
                            zf = z[:, :, :, :].rearrange("p a h d -> p (a h) d")
                            amf, sf, rf = (x[:, :, :].rearrange("p a h -> p (a h)") for x in (am, s_, rs))
                            c.do(dve.tensor_reduce(amf, zf, AX, ALU.max, apply_absolute_value=True))
                            c.do(dve.tensor_scalar(sf, amf, 1.0 / 127.0, 1e-8, ALU.mult, ALU.max))
                            dve.tensor_copy(sq[:, ds(t * H, H)], s_[:, 0, :])
                            c.do(dve.reciprocal(rf, sf))
                            c.do(dve.tensor_tensor(zf, zf, rf.unsqueeze(2).broadcast_to((P, 2 * H, HD)), ALU.mult))
                            dve.wait_ge(turned, t + 1)
                            for cp in range(3):
                                last = dve.tensor_scalar(Tq[:, sl, :, cp, :], z[:, 0, :, :], MAGIC, MAGIC, ALU.add, ALU.subtract)
                            c.do(dve.tensor_scalar(k32[:, :, :], z[:, 1, :, :], MAGIC, MAGIC, ALU.add, ALU.subtract))
                            c.do(dve.tensor_tensor(k32[:, :, :], k32[:, :, :],
                                                   s_[:, 1, :].unsqueeze(2).broadcast_to((P, H, HD)), ALU.mult))
                            c.do(dve.tensor_copy(Tk[:, sl, :, 0, :], k32[:, :, :]))
                            c.do(dve.tensor_tensor(r32[:, :, :], k32[:, :, :], Tk[:, sl, :, 0, :], ALU.subtract))
                            c.do(dve.tensor_copy(Tk[:, sl, :, 1, :], r32[:, :, :]))
                            dve.tensor_tensor(Tk[:, sl, :, 2, :], r32[:, :, :], Tk[:, sl, :, 1, :],
                                              ALU.subtract).then_inc(packed, 1)
                        assert c.n == STEPS * TPB, c.n
                    c = Chain(dve, chain2)
                    dve.wait_ge(taken, 2 + NT)
                    dve.tensor_reduce(vm[:, :], V32[:, :, :].rearrange("p t c -> p c t"), AX, ALU.max,
                                      apply_absolute_value=True).then_inc(vmaxed, 1)
                    c.do(dve.tensor_scalar(nsq[:, :], sq[:, :], -1.0, None, ALU.mult))
                    dve.wait_ge(vall, 1)
                    c.do(dve.tensor_scalar(sv[:, :], vma[:, :], 1.0 / 127.0, 1e-8, ALU.mult, ALU.max))
                    c.do(dve.reciprocal(rv[:, :], sv[:, :]))
                    c.do(dve.tensor_tensor(V32[:, :, :], V32[:, :, :], rv[:, :].unsqueeze(1).broadcast_to((P, NT, D)), ALU.mult))
                    c.do(dve.tensor_scalar(Vi[:, :, :, :].rearrange("p t h d -> p (t h d)"),
                                           V32[:, :, :].rearrange("p t c -> p (t c)"), MAGIC, MAGIC, ALU.add, ALU.subtract))

                @block.tensor
                def _(pe):
                    pe.sem_inc(proj, 1)
                    pe.sem_inc(turned, 2)
                    pe.wait_ge(prep, 4)

                    def project(i, tt):
                        t = i * TPB + tt
                        sl = tt % 2
                        tok = slice(tt * P, (tt + 1) * P)
                        pe.wait_ge(taken, t + 1)
                        for out, src, W in ((m.bank[sl][:, 0:D], xs, lambda k: Wq[:, k, :]),
                                            (m.bank[sl][:, D:], cs, lambda k: Wkv[:, k, 0, :]),
                                            (m.bank[2 + sl][:, 0:D], cs, lambda k: Wkv[:, k, 1, :])):
                            for k in range(KC):
                                mm = pe.matmul(out, src[:, k, tok], W(k), start=(k == 0), stop=(k == KC - 1))
                        mm.then_inc(proj, 1)

                    with pe.Fori(0, NBLK) as i:
                        pe.wait_ge(copied, 2 * i + 2)
                        project(i, 0)
                        for tt in range(TPB):
                            t = i * TPB + tt
                            sl = tt % 2
                            if tt < TPB - 1:
                                project(i, tt + 1)
                            pe.wait_ge(packed, t + 1)
                            pe.wait_ge(stored, t + 1)
                            for src, b in ((Tq, 4 + 2 * sl), (Tk, 5 + 2 * sl)):
                                for pr in range(PR):
                                    mm = pe.transpose(m.bank[b].bitcast(BF16)[:, pr * P:(pr + 1) * P],
                                                      src[:, sl, 2 * pr:2 * pr + 2, :, :].rearrange("p h c d -> p (h c d)"),
                                                      identb[:, :])
                            mm.then_inc(turned, 1)

        N = NT * H
        Qs = sb("Qs", [P, 4, P], BF16)
        e16 = sb("e16", [P, 2, TOK], U16)
        PT = sb("PT", [P, 2, KT // 2, P], BF16)
        mx = sb("mx", [P, 2, 3])
        ebias = sb("ebias", [P, 2])
        esum = sb("esum", [P, 2, N])
        Osb = sb("Osb", [P, N, HD])
        SC = 16
        slot = [m.psum[:, 2 * k:2 * k + 2, :].rearrange("p a b -> p (a b)") for k in range(3)]
        turn_bank, out_bank = m.bank[6].bitcast(BF16), m.bank[7]

        def loop(eng, step):
            def tile(t):
                for j in range(H):
                    step(t * H + j, j)
            tile(0)
            with eng.Fori(1, NT - 1) as i:
                tile(i)
            tile(NT - 1)

        def first(n):
            return isinstance(n, int) and n == 0

        def last(n):
            return isinstance(n, int) and n == N - 1

        def halves(n, j):
            return [(hf, n * 2 + hf, (2 * j + hf) % 3) for hf in range(2)]

        with nc.Block() as block:
            @block.gpsimd
            def _(pool):
                with pool.Fori(0, NT) as i:
                    for jp in range(PR):
                        pair = i * PR + jp
                        m.wait_apart(pool, scored, 4 * pair + 4)
                        pool.tensor_copy(Qs[:, jp % 4, :], QT[:, ds(pair, 1), :].rearrange("p a b -> p (a b)")).then_inc(q_here, 1)

            @block.tensor
            def _(pe):
                pe.sem_inc(scored, SC)

                def score(n, j):
                    rows = slice(64 * (j % 2), 64 * (j % 2) + 48)
                    for hf, g, sl in halves(n, j):
                        m.wait_apart(pe, exped, g + (2 if j == 0 and not first(n) else 1))
                        if hf == 0 and j % 2 == 0:
                            m.wait_apart(pe, q_here, (n // 2) + 1)
                        for b in range(2):
                            col = hf * HALF + b * BLK
                            mm = pe.matmul(slot[sl][:, b * BLK:(b + 1) * BLK], Qs[rows, j // 2 % 4, :],
                                           KTt[rows, j // 2, col:col + BLK],
                                           start=True, stop=True)
                        mm.then_inc(scored, 1)

                def turn(n, j, hf):
                    g = 2 * n + hf
                    m.wait_apart(pe, exped, 3 + g + 1)
                    if hf == 0:
                        m.wait_apart(pe, evac1, n + 1)
                    else:
                        m.wait_apart(pe, evac0, n + 1)
                    for k in range(KT // 2):
                        col = hf * HALF + k * P
                        mm = pe.transpose(turn_bank[:, k * P:(k + 1) * P], e16[:, j % 2, col:col + P].bitcast(BF16), identb[:, :])
                    mm.then_inc(tturned, 1)

                def mix(n, j, hf):
                    m.wait_apart(pe, *((evac1, n + 2) if hf else (normed, n + 1)))
                    for k in range(KT // 2):
                        kt = hf * (KT // 2) + k
                        mm = pe.matmul(out_bank[:, 0:HD], PT[:, hf, k, :], Vi[:, kt, j, :],
                                       start=(kt == 0), stop=(kt == KT - 1))
                    if hf:
                        mm.then_inc(mixed, 1)

                score(0, 0)

                def step(n, j):
                    if not last(n):
                        score(n + 1, (j + 1) % H)
                    turn(n, j, 0)
                    if not first(n):
                        mix(n - 1, (j - 1) % H, 1)
                    turn(n, j, 1)
                    mix(n, j, 0)
                loop(pe, step)
                mix(N - 1, H - 1, 1)

            @block.vector
            def _(dve):
                dve.sem_inc(normed, 1)

                def maxima(n, j, c):
                    for hf, g, sl in halves(n, j):
                        dve.wait_ge(scored, SC + g + 1)
                        red = dve.tensor_reduce(mx[:, j % 2, hf:hf + 1], slot[sl], AX, ALU.max)
                    c.do(red)
                    c.do(dve.tensor_tensor(mx[:, j % 2, 2:3], mx[:, j % 2, 0:1], mx[:, j % 2, 1:2], ALU.max))
                    dve.tensor_scalar(ebias[:, j % 2:j % 2 + 1], mx[:, j % 2, 2:3], nsq[:, ds(n, 1)], LN255,
                                      ALU.mult, ALU.add).then_inc(biased, 1)

                def take(n, j):
                    dve.wait_ge(tturned, 2 * n + 1)
                    dve.tensor_copy(PT[:, 0, :, :].rearrange("p a b -> p (a b)"), turn_bank.bitcast(U16)).then_inc(evac0, 1)

                def output(n, j):
                    dve.wait_ge(mixed, n + 1)
                    dve.tensor_copy(Osb[:, ds(n, 1), :].rearrange("p a b -> p (a b)"), out_bank[:, 0:HD]).then_inc(normed, 1)

                PER = 2

                def step(n, j):
                    if not last(n):
                        c = Chain(dve, chain3)
                        c.base = n * PER + PER
                        maxima(n + 1, (j + 1) % H, c)
                    take(n, j)
                    if not first(n):
                        output(n - 1, (j - 1) % H)
                c0 = Chain(dve, chain3)
                maxima(0, 0, c0)
                loop(dve, step)
                output(N - 1, 0)

            @block.scalar
            def _(act):
                act.sem_inc(exped, 3)
                act.sem_inc(evac1, 1)

                def exp(n, j, hf, sl):
                    m.wait_apart(act, biased, n + 1)
                    act.activation(e16[:, j % 2, hf * HALF:(hf + 1) * HALF], slot[sl], ACT.Exp, bias=ebias[:, j % 2:j % 2 + 1],
                                   scale=sq[:, ds(n, 1)], accum_out=esum[:, hf, ds(n, 1)]).then_inc(exped, 1)

                def take(n):
                    act.wait_ge(tturned, 2 * n + 2)
                    act.activation(PT[:, 1, :, :].rearrange("p a b -> p (a b)"), turn_bank.bitcast(U16), ACT.Copy).then_inc(evac1, 1)

                def step(n, j):
                    (_, _, s0), (_, _, s1) = halves(n, j)
                    exp(n, j, 0, s0)
                    if not first(n):
                        take(n - 1)
                    exp(n, j, 1, s1)
                loop(act, step)
                take(N - 1)

        rsum = sb("rsum", [P, N])
        on = sb("on", [P, TPB, H, HD])
        onT = sb("onT", [P, KC, BLK])
        with nc.Block() as block:
            @block.vector
            def _(dve):
                c = Chain(dve, o_ready)
                c.do(dve.tensor_tensor(rsum[:, :], esum[:, 0, :], esum[:, 1, :], ALU.add))
                c.do(dve.reciprocal(rsum[:, :], rsum[:, :]))
                dve.sem_inc(outp, 1)
                with dve.Fori(0, NBLK) as i:
                    nn = TPB * H
                    dve.wait_ge(o_turned, KC * i + 1)
                    of = on[:, :, :, :].rearrange("p t h d -> p (t h) d")
                    dve.tensor_tensor(on[:, :, :, :].rearrange("p t h d -> p t (h d)"),
                                      Osb[:, ds(i * nn, nn), :].rearrange("p (t h) d -> p t (h d)", t=TPB),
                                      sv[:, :].unsqueeze(1).broadcast_to((P, TPB, D)), ALU.mult).then_inc(o_ready, 1)
                    dve.wait_ge(o_ready, 2 + 2 * i + 1)
                    dve.tensor_tensor(of, of, rsum[:, ds(i * nn, nn)].unsqueeze(2).broadcast_to((P, nn, HD)),
                                      ALU.mult).then_inc(o_ready, 1)
                    for half in range(2):
                        dve.wait_ge(outp, i * 2 + half + 2)
                        x2 = m.X[:, ds(i * TPB + 2 * half, 2), :].rearrange("p t d -> p (t d)")
                        dve.tensor_tensor(x2, m.bank[2 + half], x2, ALU.add).then_inc(added, 1)

            @block.scalar
            def _(act):
                with act.Fori(0, NBLK) as i:
                    for k in range(KC):
                        act.wait_ge(o_turned, KC * i + k + 2)
                        act.activation(onT[:, k, :], m.bank[k], ACT.Copy).then_inc(ot_ready, 1)

            @block.tensor
            def _(pe):
                pe.sem_inc(o_turned, 1)
                with pe.Fori(0, NBLK) as i:
                    pe.wait_ge(o_ready, 2 + 2 * i + 2)
                    for k in range(KC):
                        for j in range(TPB):
                            mm = pe.transpose(m.bank[k][:, j * P:(j + 1) * P],
                                              on[:, j, k * H // 2:(k + 1) * H // 2, :].rearrange("p h d -> p (h d)"), m.ident[:, :])
                        mm.then_inc(o_turned, 1)
                    pe.wait_ge(ot_ready, KC * i + KC)
                    for j in range(TPB):
                        for k in range(KC):
                            mm = pe.matmul(m.bank[2 + j // 2][:, (j % 2) * D:(j % 2 + 1) * D], onT[:, k, j * P:(j + 1) * P],
                                           Wp[:, k, :], start=(k == 0), stop=(k == KC - 1))
                        if j % 2:
                            mm.then_inc(outp, 1)


def experts_top4(nc, m, w):
    NE, F, FB = 16, 176, 48
    PAIRS = NE // 2
    ROWS = (P, FB)
    names = "loaded gate_w wa w0 w1 up copied product h downs summed"
    (loaded, gate_turned, wa_ready, w_in0, w_in1, up, copied, product, hready, downs, summed) = (
        m.sem(f"f_{n}") for n in names.split())
    w_in = (w_in0, w_in1)
    with ExitStack() as own:
        def sb(n, s, dt=F32):
            return m.sb("f_" + n, s, dt, own)

        gw, wa, gb = sb("gw", [NE, D]), sb("wa", [P, KC, NE]), sb("gb", [P, NE])
        W1, W3 = (sb(n, [P, 2, KC, F]) for n in ("W1", "W3"))
        W2 = sb("W2", [P, 2, 2, D])
        h1, pr, h = (sb(n, [P, 2, 2, BLK]) for n in ("h1", "pr", "h"))
        R = Router(m, "f", own, 4, 1)
        with nc.Block() as block:
            @block.sync
            def _(sp):
                def load(dst, src):
                    sp.dma_start(dst, src).then_inc(loaded, 16)

                def weights(w1, w3, w2, slot):
                    for W, src in ((W1, w1), (W3, w3)):
                        sp.dma_start(W[:, slot, :, :], src.rearrange("(k p) f -> p k f", p=P)).then_inc(w_in[slot], 16)
                    sp.dma_start(W2[:, slot, 0, :], w2[0:P, :]).then_inc(w_in[slot], 16)
                    sp.dma_start(W2[0:FB, slot, 1, :], w2[P:F, :]).then_inc(w_in[slot], 16)

                load(gw[:, :], w["L1_ffn_gate_w"])
                load(gb[:, :], w["L1_ffn_gate_b"].partition_broadcast(P))
                load(R.iota[:, :], w["iota16"].partition_broadcast(P))
                w1, w3, w2 = (w[f"L1_ffn_w{n}_routed"] for n in (1, 3, 2))
                with sp.Fori(0, PAIRS) as i:
                    for slot in range(2):
                        e = i * 2 + slot
                        sp.wait_ge(downs, i * 8 + 4 * (slot + 1))
                        weights(w1[e], w3[e], w2[e], slot)
                sp.wait_ge(downs, PAIRS * 8 + 4)
                weights(*(w[f"L1_ffn_w{n}_shared"] for n in (1, 3, 2)), 0)

            @block.scalar
            def _(act):
                act.wait_ge(gate_turned, 1)
                act.activation(wa[:, :, :].rearrange("p k e -> p (k e)"), m.bank[1][:, 0:KC * NE], ACT.Copy).then_inc(wa_ready, 1)
                R.scalar(act, m.bank[0])

                def steps(i, n, first, second):
                    for st in range(n):
                        q = st % NBLK
                        act.wait_ge(up, i * 8 + st + 1)
                        for part, r in enumerate(ROWS):
                            last = act.activation(h1[0:r, q % 2, part, :], m.bank[2 * part][0:r, :], first)
                        last.then_inc(copied, 1)
                        act.wait_ge(product, i * 8 + st + 2)
                        for part, r in enumerate(ROWS):
                            last = act.activation(h[0:r, q % 2, part, :], pr[0:r, q % 2, part, :], second)
                        last.then_inc(hready, 1)

                with act.Fori(0, PAIRS) as i:
                    steps(i, 8, ACT.Copy, ACT.Silu)
                steps(PAIRS, 4, ACT.Silu, ACT.Copy)

            @block.vector
            def _(dve):
                dve.wait_ge(loaded, 16 * 3)
                R.vector(dve, gb[:, :])
                dve.sem_inc(product, 1)
                dve.sem_inc(summed, 2)

                def multiply(i, st):
                    dve.wait_ge(copied, i * 8 + st + 1)
                    for part, r in enumerate(ROWS):
                        last = dve.tensor_tensor(pr[0:r, st % 2, part, :], m.bank[2 * part + 1][0:r, :],
                                                 h1[0:r, st % 2, part, :], ALU.mult)
                    last.then_inc(product, 1)

                def add(i, e, st):
                    q = st % NBLK
                    dve.wait_ge(downs, 8 + i * 8 + st + 1)
                    for j in range(TPB):
                        t = q * TPB + j
                        last = dve.scalar_tensor_tensor(
                            m.X[:, t, :], m.bank[4 + 2 * (q % 2) + j // 2][:, (j % 2) * D:(j % 2 + 1) * D],
                            R.route[:, t, ds(e, 1)], m.X[:, t, :], ALU.mult, ALU.add)
                    last.then_inc(summed, 1)

                def steps(i, n, e0):
                    multiply(i, 0)
                    for st in range(n):
                        if st < n - 1:
                            multiply(i, st + 1)
                        add(i, e0 + st // NBLK, st)

                with dve.Fori(0, PAIRS) as i:
                    steps(i, 8, i * 2)
                steps(PAIRS, 4, NE)

            @block.tensor
            def _(pe):
                pe.sem_inc(downs, 8)
                pe.wait_ge(loaded, 16 * 3)
                for k in range(KC):
                    mm = pe.transpose(m.bank[1][:, k * NE:(k + 1) * NE], gw[:, k * P:(k + 1) * P], m.ident[0:NE, 0:NE])
                mm.then_inc(gate_turned, 1)
                pe.wait_ge(wa_ready, 1)
                R.tensor(pe, wa, m.bank[0])
                pe.wait_ge(R.done, 1)

                def hidden(i, st):
                    slot, q = divmod(st, NBLK)
                    if q == 0:
                        pe.wait_ge(w_in[slot], i * 64 + 64)
                    pe.wait_ge(product, i * 8 + st + 1)
                    for part, r in enumerate(ROWS):
                        for n, W in enumerate((W1, W3)):
                            for k in range(KC):
                                mm = pe.matmul(m.bank[2 * part + n][0:r, :], W[:, slot, k, part * P:part * P + r],
                                               m.xnT[:, k, q * BLK:(q + 1) * BLK], start=(k == 0), stop=(k == KC - 1))
                    mm.then_inc(up, 1)

                def down(i, st):
                    slot, q = divmod(st, NBLK)
                    pe.wait_ge(hready, i * 8 + st + 1)
                    pe.wait_ge(summed, i * 8 + st + 1)
                    for j in range(TPB):
                        for part, r in enumerate(ROWS):
                            mm = pe.matmul(m.bank[4 + 2 * (q % 2) + j // 2][:, (j % 2) * D:(j % 2 + 1) * D],
                                           h[0:r, q % 2, part, j * P:(j + 1) * P], W2[0:r, slot, part, :],
                                           start=(part == 0), stop=(part == 1))
                    mm.then_inc(downs, 1)

                def steps(i, n):
                    hidden(i, 0)
                    for st in range(n):
                        if st < n - 1:
                            hidden(i, st + 1)
                        down(i, st)

                with pe.Fori(0, PAIRS) as i:
                    steps(i, 8)
                steps(PAIRS, 4)


def constants():
    J, M, HU = 32, 96, 3
    inv_freq = (1.0 / 10000.0 ** (np.arange(0, 64, 2, dtype=np.float32) / np.float32(64))).astype(np.float32)
    col = np.tile(inv_freq, HU)
    head = np.arange(M) // J
    slopes = (np.float32(2.0 ** -0.5) ** np.arange(1, 17, dtype=np.float32)).reshape(4, 4).T
    q, k = np.arange(P) % SEQ, np.arange(SEQ)
    rel = (k[None, :] - q[:, None]).astype(np.float32)
    row = np.arange(P)
    ahead = ((row[None, :] - row[:, None])).astype(np.float32)
    same = (row[None, :] // SEQ == row[:, None] // SEQ) & (ahead >= 0)
    return {
        "rel": np.where(same, ahead, 0).astype(np.float32),
        "tri": same.astype(np.float32),
        "alibi": (slopes.reshape(1, 16, 1) * rel[:, None, :]).astype(np.float32).reshape(P, 16 * SEQ),
        "gmask": ((row[:, None] % 64) // 16 == np.arange(4)).astype(np.float32),
        "hmask": (row[:, None] // 64 == np.arange(2)).astype(np.float32),
        "iota16": np.arange(16, dtype=np.float32),
        "ident": np.eye(P, dtype=np.float32),
        "freq": np.stack([col, -col], 1).astype(np.float32),
        "mean_w": ((head[:, None] == head[None, :]) / np.float32(64 * 4)).astype(np.float32),
    }


def build(nc, w, out):
    with ExitStack() as ctx:
        m = Mem(nc, ctx)
        x_ready, stored = m.sem("x_ready"), m.sem("stored")
        load_inputs(nc, m, w["x"], w["ctx_2048"], w["ident"], x_ready)
        layernorm(nc, m)
        own = {k[len("L0_attn_"):]: v for k, v in w.items() if k.startswith("L0_attn_")}
        rotary_recurrence(nc, m, {**own, "freq": w["freq"], "mean_w": w["mean_w"]})
        layernorm(nc, m)
        gqa_cross_attention(nc, m, w)
        layernorm(nc, m, add_to_x=True)
        experts_top2(nc, m, w)
        layernorm(nc, m)
        lightning_attention(nc, m, w)
        layernorm(nc, m)
        quantised_attention(nc, m, w)
        layernorm(nc, m)
        experts_top4(nc, m, w)
        with nc.Block() as block:
            @block.sync
            def _(sp):
                sp.dma_start(out.rearrange("(t p) d -> p t d", p=P), m.X[:, :, :]).then_inc(stored, 16)
                sp.wait_ge(stored, 16)


def kernel(**inputs):
    import concourse.bacc as bacc
    from concourse.bass_utils import run_bass_kernel_spmd

    nc = bacc.Bacc("TRN2", target_bir_lowering=False, num_devices=1)
    arrays = {k: np.ascontiguousarray(v) for k, v in inputs.items()}
    for name in ("x", "ctx_2048"):
        arrays[name] = arrays[name].reshape(TOK, D)
    arrays.update(constants())
    arrays["mask_BxS2_bf1"] = arrays["mask_BxS2_bf1"].view(np.uint8)
    aps = {k: nc.dram_tensor("in_" + k, a.shape, mybir.dt.from_np(a.dtype), kind="ExternalInput").ap()
           for k, a in arrays.items()}
    out = nc.dram_tensor("out_0", (TOK, D), F32, kind="ExternalOutput").ap()
    build(nc, aps, out)
    r = run_bass_kernel_spmd(nc, [{"in_" + k: a for k, a in arrays.items()}], core_ids=[0])
    return r.results[0]["out_0"].reshape(BATCH, SEQ, D)
```

```python
from contextlib import ExitStack

import numpy as np
import concourse.bass as bass
from concourse import mybir

F32 = mybir.dt.float32
BF16 = mybir.dt.bfloat16
F16 = mybir.dt.float16
U8 = mybir.dt.uint8
U32 = mybir.dt.uint32
ALU = mybir.AluOpType
ACT = mybir.ActivationFunctionType
AX = mybir.AxisListType.X
ds = bass.ds

BATCH, SEQ, D = 32, 64, 256
TOK = BATCH * SEQ
P = 128
NT = TOK // P
KC = D // P
BLK = 512
NBLK = TOK // BLK
TPB = BLK // P
BPB = BLK // SEQ
MAGIC = 12582912.0
SPLIT = 1024.0
UNSPLIT = SPLIT ** -2
FLT_MAX = 3.4028234663852886e38


class Mem:

    def __init__(self, nc, ctx):
        self.nc, self.ctx = nc, ctx
        self.X = self.sb("X", [P, NT, D])
        self.xnT = self.sb("xnT", [P, KC, TOK])
        self.xh, self.xl = (self.sb(n, [P, KC, TOK], F16) for n in ("xh", "xl"))
        self.ctxT = self.sb("ctxT", [P, KC, TOK])
        self.ident = self.sb("ident", [P, P])
        self.psum = ctx.enter_context(nc.psum_tensor("psum", [P, 8, 512], F32))
        self.bank = [self.psum[:, i, :] for i in range(8)]

        self.apart = self.sem("apart")
        self.norms = 0
        self.norm_sems = [self.sem(f"ln_{n}") for n in "stats moments sd rstd xn turned bank_free added split".split()]
        self.splits = 0

    def wait_apart(self, eng, sem, value):
        eng.wait_ge(sem, value)
        eng.sem_inc(self.apart, 1)

    def sb(self, name, shape, dt=F32, ctx=None):
        return (ctx or self.ctx).enter_context(self.nc.sbuf_tensor(name, shape, dt))

    def sem(self, name):
        return self.ctx.enter_context(self.nc.semaphore(name))


class Chain:

    def __init__(self, eng, sem):
        self.eng, self.sem, self.n, self.base = eng, sem, 0, 0

    def enter(self, i, per):
        self.base = i * per

    def do(self, ins):
        self.n += 1
        ins.then_inc(self.sem, 1)
        self.eng.wait_ge(self.sem, self.base + self.n)


def split_product(pe, out, lhsT, rhs):
    terms = [(a, b, k) for a, b in ((0, 0), (0, 1), (1, 0)) for k in range(KC)]
    for n, (a, b, k) in enumerate(terms):
        mm = pe.matmul(out, lhsT(a, k), rhs(b, k), start=(n == 0), stop=(n == len(terms) - 1))
    return mm


def load_inputs(nc, m, x, ctx_tokens, c_ident, x_ready):
    tile_in, turned, ctx_free, bank_free = (m.sem(n) for n in ("ld_tile", "ld_turned", "ld_free", "ld_bank_free"))
    ready = m.sem("ld_consts")
    with ExitStack() as own:
        C = m.sb("ctx_rows", [P, NT, D], ctx=own)
        with nc.Block() as block:
            @block.sync
            def _(sp):
                sp.dma_start(m.ident[:, :], c_ident).then_inc(ready, 16)
                sp.dma_start(C[:, :, :], ctx_tokens.rearrange("(t p) d -> p t d", p=P)).then_inc(tile_in, 16)
                sp.dma_start(m.X[:, :, :], x.rearrange("(t p) d -> p t d", p=P)).then_inc(x_ready, 16)

            @block.tensor
            def _(pe):
                pe.wait_ge(ready, 16)
                pe.wait_ge(tile_in, 16)
                for g in range(NBLK * KC):
                    b, c = divmod(g, KC)
                    if g >= 4:
                        pe.wait_ge(bank_free, g - 3)
                    for j in range(TPB):
                        last = pe.transpose(m.bank[g % 4][:, j * P:(j + 1) * P],
                                            C[:, b * TPB + j, c * P:(c + 1) * P], m.ident[:, :])
                    last.then_inc(turned, 1)

            @block.scalar
            def _(act):
                for g in range(NBLK * KC):
                    b, c = divmod(g, KC)
                    act.wait_ge(turned, g + 1)
                    act.activation(m.ctxT[:, c, b * BLK:(b + 1) * BLK], m.bank[g % 4][:, :],
                                   ACT.Copy).then_inc(bank_free, 1)
            @block.vector
            def _(dve):
                dve.wait_ge(x_ready, 16)


def layernorm(nc, m, add_to_x=False, split=False):
    stats_done, moments_done, sd_done, rstd_done, xn_ready, turned, bank_free, added, split_done = m.norm_sems
    splits = m.splits * NBLK
    m.splits += int(split)
    r = m.norms
    m.norms += 1
    tag, tiles, turns, frees = f"ln{r}", r * NT, r * (NBLK * KC + 1), r * (NBLK + 1)
    with ExitStack() as own:
        stats = m.sb(f"{tag}_stats", [P, NT, 6], ctx=own)
        mom = m.sb(f"{tag}_mom", [P, NT, 2], ctx=own)
        sd = m.sb(f"{tag}_sd", [P, NT], ctx=own)
        rstd = m.sb(f"{tag}_rstd", [P, NT], ctx=own)
        eps = m.sb(f"{tag}_eps", [P, 1], ctx=own)
        xn = m.sb(f"{tag}_xn", [P, TPB, D], ctx=own)
        with nc.Block() as block:
            @block.vector
            def _(dve):
                dve.memset(eps[:, :], 1e-5).then_inc(moments_done, 1)
                with dve.Fori(0, NT) as t:
                    dve.bn_stats(stats[:, t, :], m.X[:, t, :]).then_inc(stats_done, 1)
                dve.wait_ge(stats_done, tiles + NT)
                for t in range(NT):
                    dve.bn_aggr(mom[:, t, :], stats[:, t, :]).then_inc(moments_done, 1)
                dve.wait_ge(sd_done, r + 1)
                dve.reciprocal(rstd[:, :], sd[:, :]).then_inc(rstd_done, 1)
                dve.wait_ge(rstd_done, r + 1)
                with dve.Fori(0, NBLK) as i:
                    dve.wait_ge(turned, turns + i * KC + 1)
                    for j in range(TPB):
                        t = i * TPB + j
                        dve.tensor_scalar(xn[:, j, :], m.X[:, t, :], mom[:, t, 0:1], rstd[:, ds(t, 1)],
                                          ALU.subtract, ALU.mult).then_inc(xn_ready, 1)
                        if add_to_x:
                            dve.wait_ge(xn_ready, tiles + t + 1)
                            dve.tensor_tensor(m.X[:, t, :], m.X[:, t, :], xn[:, j, :], ALU.add).then_inc(added, 1)
                    if add_to_x:
                        dve.wait_ge(added, i * TPB + TPB)
                if split:
                    with dve.Fori(0, NBLK) as i:
                        dve.wait_ge(split_done, splits + i + 1)
                        tok = ds(i * BLK, BLK)
                        dve.scalar_tensor_tensor(m.xl[:, :, tok], m.xnT[:, :, tok], SPLIT, m.xh[:, :, tok],
                                                 ALU.mult, ALU.subtract)

            @block.scalar
            def _(act):
                act.wait_ge(moments_done, (r + 1) * (NT + 1))
                act.activation(sd[:, :], mom[:, :, 1], ACT.Sqrt, bias=eps[:, :]).then_inc(sd_done, 1)
                act.sem_inc(bank_free, 1)
                with act.Fori(0, NBLK) as i:
                    for c in range(KC):
                        act.wait_ge(turned, turns + i * KC + c + 2)
                        last = act.activation(m.xnT[:, c, ds(i * BLK, BLK)], m.bank[c][:, :], ACT.Copy)
                        if split:
                            high = act.activation(m.xh[:, c, ds(i * BLK, BLK)], m.bank[c][:, :], ACT.Copy, scale=SPLIT)
                    if split:
                        high.then_inc(split_done, 1)
                        act.wait_ge(split_done, splits + i + 1)
                        act.sem_inc(bank_free, 1)
                    else:
                        last.then_inc(bank_free, 1)

            @block.tensor
            def _(pe):
                pe.sem_inc(turned, 1)
                with pe.Fori(0, NBLK) as i:
                    pe.wait_ge(xn_ready, tiles + i * TPB + TPB)
                    pe.wait_ge(bank_free, frees + i + 1)
                    for c in range(KC):
                        for j in range(TPB):
                            last = pe.transpose(m.bank[c][:, j * P:(j + 1) * P], xn[:, j, c * P:(c + 1) * P],
                                                m.ident[:, :])
                        last.then_inc(turned, 1)


def rotary_recurrence(nc, m, w):
    NH, HD, HU = 6, 64, 3
    J = HD // 2
    U = NH // HU
    M = HU * J
    VD = NH * HD
    K, Q, VE, VO, AL, BE, GE, GO = range(8)
    NG = 8
    CONVK = 4
    TWO_PI = 6.283185307179586
    TWO_PI_HI = 6.28125
    TWO_PI_LO = TWO_PI - TWO_PI_HI
    PI_IN = 3.1415925
    loaded, prep, proj, evac, chain_s = (m.sem(f"a_{n}") for n in ("loaded", "prep", "proj", "evac", "chain"))
    angle, sincos, scanned, squares, meansq, sd_ready, gated, gates_used, outp, added = (m.sem(f"a_{n}") for n in (
        "angle", "sincos", "scanned", "squares", "meansq", "sd", "gated", "gates_used", "outp", "added"))
    with ExitStack() as own:
        def sb(n, s, dt=F32):
            return m.sb("a_" + n, s, dt, own)

        Wq, Wk, Wv, Wg = (sb(n, [P, KC, VD]) for n in ("Wq", "Wk", "Wv", "Wg"))
        Wab = sb("Wab", [P, KC, 2, NH])
        WabX = sb("WabX", [P, KC, 2, NH, J])
        Wo = sb("Wo", [M, U, 2, D])
        cw = sb("cw", [M, U, 4, CONVK])
        cwr = sb("cwr", [M, U, 2, CONVK])
        freq = sb("freq", [M, 2])
        rw = sb("rw", [M, 2])
        half_pi = sb("half_pi", [M, 1])
        eps = sb("eps", [M, 1])
        mean_w = sb("mean_w", [M, M])
        pad = sb("pad", [M, U, 4, BPB, SEQ + CONVK - 1])
        tab = sb("tab", [M, U, 2, BLK])
        gs = sb("gs", [M, U, 2, BLK])
        ang, n1, tmp = (sb(n, [M, BLK]) for n in ("ang", "n1", "tmp"))
        absang = sb("absang", [M, U, BLK])
        sc = sb("sc", [M, U, 2, BLK])
        v = sb("v", [M, 2, BLK])
        u = sb("u", [M, 2, BLK])
        t4 = sb("t4", [M, 4, BLK])
        al = sb("al", [M, BPB, SEQ])
        o = sb("o", [M, U, 2, BLK])
        sq = sb("sq", [M, U, 2, BLK])
        rstd = sb("rstd", [M, BLK])
        sdv = sb("sdv", [M, U, BLK])
        og = sb("og", [M, U, 2, BLK])

        def wcols(g, unit, c):
            if g in (AL, BE):
                return WabX[:, c, g - AL, unit * HU:(unit + 1) * HU, :].rearrange("p h j -> p (h j)")
            W, odd = {K: (Wk, 0), Q: (Wq, 0), VE: (Wv, 0), VO: (Wv, 1), GE: (Wg, 0), GO: (Wg, 1)}[g]
            return W[:, c, unit * HU * HD:(unit + 1) * HU * HD].rearrange("p (n two) -> p n two", two=2)[:, :, odd]

        NLOAD = 4 + 2 + 2 * U + U * 4 + 1 + 2 * HU + 1
        with nc.Block() as block:
            @block.sync
            def _(sp):
                with nc.allow_non_contiguous_dma("small, strided weights"):
                    for W, src in ((Wk, w["Wk"]), (Wq, w["Wq"]), (Wv, w["Wv"]), (Wg, w["Wg"])):
                        sp.dma_start(W[:, :, :], src.rearrange("(c p) n -> p c n", p=P)).then_inc(loaded, 16)
                    for n, src in enumerate((w["Wa"], w["Wb"])):
                        sp.dma_start(Wab[:, :, n, :], src.rearrange("(c p) n -> p c n", p=P)).then_inc(loaded, 16)
                    for unit in range(U):
                        rows = slice(unit * HU * HD, (unit + 1) * HU * HD)
                        for odd in range(2):
                            src = w["Wo"][rows, :].rearrange("(n two) d -> n two d", two=2)[:, odd, :]
                            sp.dma_start(Wo[:, unit, odd, :], src).then_inc(loaded, 16)
                        for n, (src, odd) in enumerate((("conv_k", 0), ("conv_q", 0), ("conv_v", 0), ("conv_v", 1))):
                            s = w[src][rows, :].rearrange("(n two) d -> n two d", two=2)[:, odd, :]
                            sp.dma_start(cw[:, unit, n, :], s).then_inc(loaded, 16)
                    sp.dma_start(freq[:, :], w["freq"]).then_inc(loaded, 16)
                    sp.dma_start(mean_w[:, :], w["mean_w"]).then_inc(loaded, 16)
                    for h in range(HU):
                        for odd in range(2):
                            s = w["rms_w"].rearrange("(j two) -> j two", two=2)[:, odd:odd + 1]
                            sp.dma_start(rw[h * J:(h + 1) * J, odd:odd + 1], s).then_inc(loaded, 16)

            @block.vector
            def _(dve):
                dve.memset(pad[:, :, :, :, 0:CONVK - 1].rearrange("p a b c d -> p (a b) c d"), 0.0).then_inc(prep, 1)
                dve.memset(half_pi[:, :], TWO_PI / 4).then_inc(prep, 1)
                dve.memset(eps[:, :], 1e-5).then_inc(prep, 1)
                dve.wait_ge(loaded, 16 * NLOAD)
                dve.tensor_copy(WabX[:, :, :, :, :].rearrange("p c w h j -> p (c w h) j"),
                                Wab[:, :, :, :].rearrange("p c w (h o) -> p (c w h) o", o=1)
                                .broadcast_to((P, KC * 2 * NH, J))).then_inc(prep, 1)
                for n in range(2):
                    dve.tensor_scalar(cwr[:, :, n, :], cw[:, :, n, :], freq[:, n:n + 1], None, ALU.mult).then_inc(prep, 1)
                dve.tensor_scalar(rw[:, :], rw[:, :], 0.5, None, ALU.mult).then_inc(prep, 1)
                dve.wait_ge(prep, 7)
                dve.sem_inc(gated, 3)

                def conv(c, unit, n, out, wt, first=True):
                    for j in range(CONVK):
                        src = pad[:, unit, n, :, j:j + SEQ]
                        dst = out.rearrange("p (b t) -> p b t", b=BPB)
                        if first and j == 0:
                            c.do(dve.tensor_scalar(dst, src, wt[:, j:j + 1], None, ALU.mult))
                        else:
                            c.do(dve.scalar_tensor_tensor(dst, src, wt[:, j:j + 1], dst, ALU.mult, ALU.add))

                STEPS = 30
                with dve.Fori(0, NBLK) as i:
                    c = Chain(dve, chain_s)
                    c.enter(i, STEPS * U)
                    for unit in range(U):
                        k = i * U + unit
                        dve.wait_ge(evac, k * NG + K + 1 + 4)
                        conv(c, unit, 0, ang[:, :], cwr[:, unit, 0, :])
                        dve.wait_ge(evac, k * NG + Q + 1 + 4)
                        conv(c, unit, 1, ang[:, :], cwr[:, unit, 1, :], first=False)
                        c.do(dve.tensor_scalar(n1[:, :], ang[:, :], 1 / TWO_PI, MAGIC, ALU.mult, ALU.add))
                        c.do(dve.tensor_scalar(n1[:, :], n1[:, :], MAGIC, None, ALU.subtract))
                        c.do(dve.scalar_tensor_tensor(ang[:, :], n1[:, :], -TWO_PI_HI, ang[:, :], ALU.mult, ALU.add))
                        c.do(dve.scalar_tensor_tensor(ang[:, :], n1[:, :], -TWO_PI_LO, ang[:, :], ALU.mult, ALU.add))
                        dve.tensor_scalar(absang[:, unit, :], ang[:, :], PI_IN, -PI_IN, ALU.min, ALU.max).then_inc(angle, 1)
                        dve.wait_ge(evac, k * NG + VO + 1 + 4)
                        conv(c, unit, 2, v[:, 0, :], cw[:, unit, 2, :])
                        conv(c, unit, 3, v[:, 1, :], cw[:, unit, 3, :])
                        dve.wait_ge(sincos, 2 * (k + 1))
                        s_, c_ = sc[:, unit, 0, :], sc[:, unit, 1, :]
                        ve, vo = v[:, 0, :], v[:, 1, :]
                        dve.tensor_tensor(t4[:, 0, :], ve, c_, ALU.mult)
                        dve.tensor_tensor(t4[:, 1, :], vo, s_, ALU.mult)
                        dve.tensor_tensor(t4[:, 2, :], vo, c_, ALU.mult)
                        c.do(dve.tensor_tensor(t4[:, 3, :], ve, s_, ALU.mult))
                        c.do(dve.tensor_tensor(u[:, 0, :], t4[:, 0, :], t4[:, 1, :], ALU.subtract))
                        c.do(dve.tensor_tensor(u[:, 1, :], t4[:, 2, :], t4[:, 3, :], ALU.add))
                        dve.wait_ge(evac, k * NG + BE + 1 + 4)
                        tb = tab[:, unit, 1, :]
                        c.do(dve.scalar_tensor_tensor(u[:, 0, :], tb, 1.0, u[:, 0, :], ALU.add, ALU.mult))
                        c.do(dve.scalar_tensor_tensor(u[:, 1, :], tb, 1.0, u[:, 1, :], ALU.add, ALU.mult))
                        alf = al[:, :, :].rearrange("p b t -> p (b t)")
                        c.do(dve.tensor_scalar(alf, tab[:, unit, 0, :], 0.5, 0.5, ALU.mult, ALU.add))
                        c.do(dve.memset(al[:, :, 0:1], 0.0))
                        for par in range(2):
                            dve.tensor_tensor_scan(o[:, unit, par, :], alf, u[:, par, :], 0.0,
                                                   ALU.mult, ALU.add).then_inc(scanned, 1)
                        dve.wait_ge(sd_ready, k + 2)
                        c.do(dve.reciprocal(rstd[:, :], sdv[:, unit, :]))
                        dve.wait_ge(evac, k * NG + GO + 1 + 4)
                        dve.wait_ge(outp, i * 2 + 1)
                        for par in range(2):
                            c.do(dve.scalar_tensor_tensor(t4[:, par, :], o[:, unit, par, :], rw[:, par:par + 1],
                                                          rstd[:, :], ALU.mult, ALU.mult))
                        for par in range(2):
                            dve.tensor_tensor(og[:, unit, par, :], t4[:, par, :], gs[:, unit, par, :],
                                              ALU.mult).then_inc(gated, 1)
                    assert c.n == STEPS * U, c.n
                    for half in range(2):
                        dve.wait_ge(outp, i * 2 + half + 2)
                        t = i * TPB + 2 * half
                        x2 = m.X[:, ds(t, 2), :].rearrange("p t d -> p (t d)")
                        dve.tensor_tensor(x2, m.bank[5 + half][:, :], x2, ALU.add).then_inc(added, 1)

            @block.scalar
            def _(act):
                act.sem_inc(evac, 4)
                act.sem_inc(sd_ready, 1)
                act.wait_ge(prep, 6)
                with act.Fori(0, NBLK) as i:
                    for unit in range(U):
                        k = i * U + unit
                        for g in range(NG):
                            act.wait_ge(proj, k * NG + g + 1)
                            if g == 0:
                                act.wait_ge(gated, k * 2 + 1)
                            src = m.bank[g % 4][0:M, :]
                            if g in (K, Q, VE, VO):
                                ins = act.activation(pad[:, unit, g, :, CONVK - 1:],
                                                     src.rearrange("p (b t) -> p b t", b=BPB), ACT.Copy)
                            elif g in (AL, BE):
                                ins = act.activation(tab[:, unit, g - AL, :], src, ACT.Tanh, scale=0.5)
                            else:
                                ins = act.activation(gs[:, unit, g - GE, :], src, ACT.Silu)
                            ins.then_inc(evac, 1)
                        act.wait_ge(angle, k + 1)
                        act.activation(sc[:, unit, 0, :], absang[:, unit, :], ACT.Sin).then_inc(sincos, 1)
                        act.activation(sdv[:, unit, :], absang[:, unit, :], ACT.Abs).then_inc(squares, 1)
                        act.wait_ge(squares, k * 3 + 1)
                        act.activation(sc[:, unit, 1, :], sdv[:, unit, :], ACT.Sin, scale=-1.0,
                                       bias=half_pi[:, :]).then_inc(sincos, 1)
                        act.wait_ge(scanned, 2 * (k + 1))
                        for par in range(2):
                            act.activation(sq[:, unit, par, :], o[:, unit, par, :], ACT.Square).then_inc(squares, 1)
                        act.wait_ge(meansq, k + 1)
                        act.wait_ge(sincos, 2 * (k + 1))
                        act.activation(sdv[:, unit, :], m.bank[4][0:M, :], ACT.Sqrt, bias=eps[:, :]).then_inc(sd_ready, 1)

            @block.tensor
            def _(pe):
                pe.wait_ge(prep, 6)
                pe.sem_inc(outp, 1)
                with pe.Fori(0, NBLK) as i:
                    for unit in range(U):
                        k = i * U + unit
                        for g in range(NG):
                            pe.wait_ge(evac, k * NG + g + 1)
                            for c in range(KC):
                                mm = pe.matmul(m.bank[g % 4][0:M, :], wcols(g, unit, c),
                                               m.xnT[:, c, ds(i * BLK, BLK)], start=(c == 0), stop=(c == KC - 1))
                            mm.then_inc(proj, 1)
                        for par in range(2):
                            pe.wait_ge(squares, k * 3 + 2 + par)
                            if par == 0:
                                pe.wait_ge(sd_ready, k + 1)
                            mm = pe.matmul(m.bank[4][0:M, :], mean_w[:, :], sq[:, unit, par, :],
                                           start=(par == 0), stop=(par == 1))
                        mm.then_inc(meansq, 1)
                    pe.wait_ge(gated, 3 + (i + 1) * U * 2)
                    for half in range(2):
                        for j in range(2):
                            tok = slice((2 * half + j) * P, (2 * half + j + 1) * P)
                            for n in range(2 * U):
                                mm = pe.matmul(m.bank[5 + half][:, j * D:(j + 1) * D], og[:, n // 2, n % 2, tok],
                                               Wo[:, n // 2, n % 2, :], start=(n == 0), stop=(n == 2 * U - 1))
                        mm.then_inc(outp, 1)


def gqa_cross_attention(nc, m, w):
    G, C, HD = 4, 4, 16
    NH = G * C
    GD = G * HD
    COLS = NH * SEQ
    loaded, prep, ctx_copied, proj, evac = (m.sem(f"b_{n}") for n in ("loaded", "prep", "ctx", "proj", "evac"))
    bias_ready, scores, biased, shifted, exped = (m.sem(f"b_{n}") for n in ("bias", "scores", "biased", "shifted", "exped"))
    turned, pt_ready, mixed, ao_ready, ao_turned, aot_ready, outp, added, chain_s = (m.sem(f"b_{n}") for n in (
        "turned", "pt", "mixed", "ao", "ao_turned", "aot", "outp", "added", "chain"))
    with ExitStack() as own:
        def sb(n, s, dt=F32):
            return m.sb("b_" + n, s, dt, own)

        WqR = sb("WqR", [P, KC, G, C, HD])
        Wq = sb("Wq", [P, KC, C, G, HD])
        Wk = sb("Wk", [P, KC, 2, GD])
        Wv = sb("Wv", [P, KC, GD])
        Wo = sb("Wo", [P, KC, D])
        alibi = sb("alibi", [P, NH, SEQ])
        gmask = sb("gmask", [P, G])
        hmask = sb("hmask", [P, 2])
        mask8 = sb("mask8", [P, NT, SEQ], U8)
        neg = sb("neg", [P, NT, SEQ])
        ctxS = sb("ctxS", [P, KC, BLK])
        QT = sb("QT", [P, 2, BLK])
        Kbd = sb("Kbd", [P, BPB, G, SEQ])
        Vbd = sb("Vbd", [P, BPB * 2, 2, HD])
        bias = sb("bias", [P, 2, NH, SEQ])
        S = sb("S", [P, 2, NH, SEQ])
        mx, tot, rtot = (sb(n, [P, NH]) for n in ("mx", "tot", "rtot"))
        PT = sb("PT", [P, 2 * C, P])
        ao = sb("ao", [P, G, C, HD])
        aoT = sb("aoT", [P, KC, P])
        NLOAD = 1 + 2 + 1 + 1 + 3 + 2
        with nc.Block() as block:
            @block.sync
            def _(sp):
                def load(dst, src):
                    sp.dma_start(dst, src).then_inc(loaded, 16)
                with nc.allow_non_contiguous_dma("small weights, mask rows"):
                    load(WqR[:, :, :, :, :].rearrange("p k g c d -> p k (g c d)"),
                         w["L0_xattn_Wq"].rearrange("(k p) n -> p k n", p=P))
                    for half in range(2):
                        load(Wk[:, :, half, :], w["L0_xattn_Wk"].rearrange("(k p) n -> p k n", p=P))
                    load(Wv[:, :, :], w["L0_xattn_Wv"].rearrange("(k p) n -> p k n", p=P))
                    load(Wo[:, :, :], w["L0_xattn_Wo"].rearrange("(k p) n -> p k n", p=P))
                    load(alibi[:, :, :].rearrange("p h k -> p (h k)"), w["alibi"])
                    load(gmask[:, :], w["gmask"])
                    load(hmask[:, :], w["hmask"])
                    for b in range(2):
                        src = w["mask_BxS2_bf1"].rearrange("(t b) k -> b t k", b=2)[b]
                        load(mask8[b * SEQ:(b + 1) * SEQ, :, :], src.partition_broadcast(SEQ))

            @block.gpsimd
            def _(pool):
                pool.wait_ge(prep, 1 + KC * C)
                with pool.Fori(0, NBLK) as i:
                    pool.wait_ge(proj, i * 4 + 4)
                    pool.tensor_copy(ctxS[:, :, :], m.ctxT[:, :, ds(i * BLK, BLK)]).then_inc(ctx_copied, 1)
                    for tt in range(TPB):
                        n = i * TPB + tt
                        pool.wait_ge(biased, n + 1)
                        pool.tensor_tensor(bias[:, tt % 2, :, :], alibi[:, :, :],
                                           neg[:, ds(n, 1), :].broadcast_to((P, NH, SEQ)), ALU.add).then_inc(bias_ready, 1)

            @block.scalar
            def _(act):
                act.wait_ge(prep, 1 + KC * C)
                with act.Fori(0, NBLK) as i:
                    for c in range(2):
                        act.wait_ge(proj, i * 4 + 4 + c + 1)
                        act.activation(QT[:, c, :], m.bank[c][:, :], ACT.Copy).then_inc(evac, 1)
                    act.wait_ge(proj, i * 4 + 4 + 3)
                    for g in range(G):
                        last = act.activation(Kbd[:, :, g, :], m.bank[2][:, :].rearrange("p (b k) -> p b k", k=SEQ),
                                              ACT.Copy, scale=gmask[:, g:g + 1])
                    last.then_inc(evac, 1)
                    act.wait_ge(proj, i * 4 + 4 + 4)
                    for h in range(2):
                        src = m.bank[3][:, :].rearrange("p (a h d) -> p a h d", h=2, d=HD)[:, :, h, :]
                        last = act.activation(Vbd[:, :, h, :], src, ACT.Copy, scale=hmask[:, h:h + 1])
                    last.then_inc(evac, 1)
                    for tt in range(TPB):
                        n = i * TPB + tt
                        act.wait_ge(shifted, n + 1)
                        act.activation(S[:, tt % 2, :, :], S[:, tt % 2, :, :], ACT.Exp).then_inc(exped, 1)
                        for h in range(2):
                            act.wait_ge(turned, 2 * n + h + 1)
                            act.activation(PT[:, 4 * h:4 * h + 4, :].rearrange("p a b -> p (a b)"), m.bank[6 + h][:, :],
                                           ACT.Copy).then_inc(pt_ready, 1)
                        act.wait_ge(ao_turned, n + 1)
                        act.activation(aoT[:, :, :].rearrange("p a b -> p (a b)"), m.bank[1][:, 0:KC * P],
                                       ACT.Copy).then_inc(aot_ready, 1)

            @block.vector
            def _(dve):
                dve.wait_ge(loaded, 16 * NLOAD)
                dve.tensor_scalar(neg[:, :, :], mask8[:, :, :], 1.0, FLT_MAX, ALU.subtract, ALU.mult).then_inc(prep, 1)
                for k in range(KC):
                    for c in range(C):
                        slot = 2 * (c % 2) + c // 2
                        dve.tensor_copy(Wq[:, k, slot, :, :], WqR[:, k, :, c, :]).then_inc(prep, 1)
                dve.sem_inc(biased, 2)
                dve.sem_inc(added, 1)

                def front(c, n, tt):
                    s = S[:, tt % 2, :, :]
                    dve.wait_ge(scores, n + 1)
                    dve.wait_ge(bias_ready, n + 1)
                    for h in range(2):
                        sl = slice(h * NH // 2, (h + 1) * NH // 2)
                        dve.scalar_tensor_tensor(s[:, sl, :].rearrange("p a b -> p (a b)"), m.bank[4 + h][:, :], HD ** -0.5,
                                                 bias[:, tt % 2, sl, :].rearrange("p a b -> p (a b)"), ALU.mult,
                                                 ALU.add).then_inc(*((biased, 1) if h else (chain_s, 1)))
                    c.n += 1
                    dve.wait_ge(biased, n + 3)
                    c.do(dve.tensor_reduce(mx[:, :], s, AX, ALU.max))
                    dve.tensor_tensor(s, s, mx[:, :].unsqueeze(2).broadcast_to((P, NH, SEQ)),
                                      ALU.subtract).then_inc(shifted, 1)

                STEPS = TPB * 4
                with dve.Fori(0, NBLK) as i:
                    c = Chain(dve, chain_s)
                    c.enter(i, STEPS)
                    front(c, i * TPB, 0)
                    for tt in range(TPB):
                        n = i * TPB + tt
                        dve.wait_ge(exped, n + 1)
                        c.do(dve.tensor_reduce(tot[:, :], S[:, tt % 2, :, :], AX, ALU.add))
                        c.do(dve.reciprocal(rtot[:, :], tot[:, :]))
                        dve.wait_ge(mixed, n + 1)
                        dve.tensor_tensor(ao[:, :, :, :].rearrange("p g c d -> p c g d"),
                                          m.bank[0][:, 0:D].rearrange("p (c g d) -> p c g d", c=C, g=G),
                                          rtot[:, :].rearrange("p (c g o) -> p c g o", c=C, o=1)
                                          .broadcast_to((P, C, G, HD)), ALU.mult).then_inc(ao_ready, 1)
                        if tt < TPB - 1:
                            front(c, n + 1, tt + 1)
                        dve.wait_ge(outp, n + 1)
                        dve.tensor_tensor(m.X[:, n, :], m.bank[3][:, 0:D], m.X[:, n, :], ALU.add).then_inc(added, 1)
                    assert c.n == STEPS, c.n

            @block.tensor
            def _(pe):
                pe.wait_ge(prep, 1 + KC * C)
                pe.sem_inc(proj, 4)

                def score(i, n, tt):
                    m.wait_apart(pe, biased, n + 2)
                    for b in range(2):
                        for c in range(C):
                            half = slice(64 * (c // 2), 64 * (c // 2) + 64)
                            tok = slice(tt * P + b * SEQ, tt * P + (b + 1) * SEQ)
                            mm = pe.matmul(m.bank[4 + c // 2][b * SEQ:(b + 1) * SEQ, (c % 2) * 256:(c % 2) * 256 + 256],
                                           QT[half, c % 2, tok],
                                           Kbd[half, 2 * tt + b, :, :].rearrange("p g k -> p (g k)"),
                                           start=True, stop=True)
                    mm.then_inc(scores, 1)

                with pe.Fori(0, NBLK) as i:
                    for c in range(2):
                        for k in range(KC):
                            mm = pe.matmul(m.bank[c][:, :], Wq[:, k, 2 * c:2 * c + 2, :, :].rearrange("p c g d -> p (c g d)"),
                                           m.xnT[:, k, ds(i * BLK, BLK)], start=(k == 0), stop=(k == KC - 1))
                        mm.then_inc(proj, 1)
                    for k in range(KC):
                        mm = pe.matmul(m.bank[2][:, :], Wk[:, k, :, :].rearrange("p a b -> p (a b)"),
                                       m.ctxT[:, k, ds(i * BLK, BLK)], start=(k == 0), stop=(k == KC - 1))
                    mm.then_inc(proj, 1)
                    pe.wait_ge(ctx_copied, i + 1)
                    pe.wait_ge(added, i * TPB + 1)
                    for b in range(BPB):
                        for half in range(2):
                            for k in range(KC):
                                mm = pe.matmul(m.bank[3][half * 64:half * 64 + 64, b * GD:(b + 1) * GD],
                                               ctxS[:, k, b * SEQ:(b + 1) * SEQ], Wv[:, k, :],
                                               start=(k == 0), stop=(k == KC - 1))
                    mm.then_inc(proj, 1)
                    pe.wait_ge(evac, i * 4 + 4)
                    score(i, i * TPB, 0)
                    for tt in range(TPB):
                        n = i * TPB + tt
                        if tt < TPB - 1:
                            score(i, n + 1, tt + 1)
                        pe.wait_ge(exped, n + 1)
                        for pr in range(2 * C):
                            mm = pe.transpose(m.bank[6 + pr // 4][:, (pr % 4) * P:(pr % 4 + 1) * P],
                                              S[:, tt % 2, 2 * pr:2 * pr + 2, :].rearrange("p a b -> p (a b)"),
                                              m.ident[:, :])
                            if pr % 4 == 3:
                                mm.then_inc(turned, 1)
                        pe.wait_ge(pt_ready, 2 * n + 2)
                        for b in range(2):
                            for pr in range(2 * C):
                                mm = pe.matmul(m.bank[0][b * SEQ:(b + 1) * SEQ, pr * 32:pr * 32 + 32],
                                               PT[:, pr, b * SEQ:(b + 1) * SEQ],
                                               Vbd[:, (2 * tt + b) * 2 + pr % 2, :, :].rearrange("p a b -> p (a b)"),
                                               start=True, stop=True)
                        mm.then_inc(mixed, 1)
                        pe.wait_ge(ao_ready, n + 1)
                        for k in range(KC):
                            mm = pe.transpose(m.bank[1][:, k * P:(k + 1) * P],
                                              ao[:, 2 * k:2 * k + 2, :, :].rearrange("p g c d -> p (g c d)"), m.ident[:, :])
                        mm.then_inc(ao_turned, 1)
                        pe.wait_ge(aot_ready, n + 1)
                        pe.wait_ge(added, n + 1)
                        for k in range(KC):
                            mm = pe.matmul(m.bank[3][:, 0:D], aoT[:, k, :], Wo[:, k, :], start=(k == 0), stop=(k == KC - 1))
                        mm.then_inc(outp, 1)


class Router:
    NE = 16

    def __init__(self, m, tag, own, top, shared, scale=1.0):
        self.m, self.top, self.ne, self.scale = m, top, self.NE + shared, scale

        def sb(n, s, dt=F32):
            return m.sb(f"{tag}_{n}", s, dt, own)
        self.route = sb("route", [P, NT, self.ne])
        self.score = sb("score", [P, NT, self.NE])
        self.iota = sb("iota", [P, self.NE])
        self.val = sb("val", [P, NT, 8])
        self.idx = sb("idx", [P, NT, 8], U32)
        self.idxf = sb("idxf", [P, NT, 8])
        self.tot = sb("tot", [P, NT])
        self.oh = sb("oh", [P, NT, self.NE])
        self.logits, self.scored, self.chain, self.done = (m.sem(f"{tag}_{n}") for n in (
            "logits", "scored", "rchain", "routed"))

    def tensor(self, pe, wa, bank):
        for t in range(NT):
            for k in range(KC):
                mm = pe.matmul(bank[:, t * self.NE:(t + 1) * self.NE], self.m.xnT[:, k, t * P:(t + 1) * P], wa[:, k, :],
                               start=(k == 0), stop=(k == KC - 1))
        mm.then_inc(self.logits, 1)

    def scalar(self, act, bank):
        act.wait_ge(self.logits, 1)
        act.activation(self.score[:, :, :].rearrange("p t e -> p (t e)"), bank[:, 0:NT * self.NE],
                       ACT.Sigmoid).then_inc(self.scored, 1)

    def vector(self, dve, bias=None):
        c = Chain(dve, self.chain)
        shape = (P, NT, self.NE)
        dve.wait_ge(self.scored, 1)
        if bias is not None:
            c.do(dve.tensor_tensor(self.score[:, :, :], self.score[:, :, :],
                                   bias.unsqueeze(1).broadcast_to(shape), ALU.add))
        c.do(dve.memset(self.route[:, :, :], self.scale))
        for t in range(NT):
            last = dve.max(self.val[:, t, :], self.score[:, t, :])
        c.do(last)
        for t in range(NT):
            last = dve.max_index(self.idx[:, t, :], self.val[:, t, :], self.score[:, t, :])
        c.do(last)
        c.do(dve.tensor_copy(self.idxf[:, :, :], self.idx[:, :, :]))
        c.do(dve.tensor_reduce(self.tot[:, :], self.val[:, :, 0:self.top], AX, ALU.add))
        c.do(dve.reciprocal(self.tot[:, :], self.tot[:, :]))
        if self.scale != 1.0:
            c.do(dve.tensor_scalar(self.tot[:, :], self.tot[:, :], self.scale, None, ALU.mult))
        c.do(dve.tensor_tensor(self.val[:, :, :], self.val[:, :, :],
                               self.tot[:, :].unsqueeze(2).broadcast_to((P, NT, 8)), ALU.mult))
        r = self.route[:, :, 0:self.NE]
        for j in range(self.top):
            out = r if j == 0 else self.oh[:, :, :]
            c.do(dve.tensor_tensor(out, self.iota[:, :].unsqueeze(1).broadcast_to(shape),
                                   self.idxf[:, :, j:j + 1].broadcast_to(shape), ALU.is_equal))
            c.do(dve.tensor_tensor(out, out, self.val[:, :, j:j + 1].broadcast_to(shape), ALU.mult))
            if j:
                c.do(dve.tensor_tensor(r, r, self.oh[:, :, :], ALU.add))
        dve.sem_inc(self.done, 1)


def experts_top2(nc, m, w):
    NE, SH, F = 16, 2, 128
    PAIRS = NE // 2
    (prepared, high, split) = (m.sem(f"c_{n}") for n in ("prepared", "high", "split"))
    (loaded, w_in0, w_in1, gate_up, gated, hready, downs, summed, routed_T, rt_ready, biased) = (
        m.sem(f"c_{n}") for n in ("loaded", "w0", "w1", "gate_up", "gelu", "h", "downs", "summed", "rT", "rTs", "b2"))
    w_in = (w_in0, w_in1)
    with ExitStack() as own:
        def sb(n, s, dt=F32):
            return m.sb("c_" + n, s, dt, own)

        wa = sb("wa", [P, KC, NE])
        Wgu = sb("Wgu", [P, 2, KC, 2, F])
        Wx = sb("Wx", [P, 2, 2, KC, 2, F], F16)
        Wd = sb("Wd", [F, 2, D])
        gb, ub = (sb(n, [F, NE + SH]) for n in ("gb", "ub"))
        b2 = sb("b2", [NE + SH, D])
        gelu = sb("gelu", [F, 2, BLK])
        h = sb("h", [F, 2, BLK])
        rT = sb("rT", [NE + SH, TPB, P])
        R = Router(m, "c", own, 2, SH, UNSPLIT)
        src_r = {"Wg": w["L0_ffn_rg"], "Wu": w["L0_ffn_rw1"], "Wd": w["L0_ffn_rw2"]}
        src_s = {"Wg": w["L0_ffn_sg"], "Wu": w["L0_ffn_sw1"], "Wd": w["L0_ffn_sw2"]}
        with nc.Block() as block:
            @block.sync
            def _(sp):
                def load(dst, src):
                    sp.dma_start(dst, src).then_inc(loaded, 16)

                def weights(src, e, slot):
                    for part, n in enumerate(("Wg", "Wu")):
                        sp.dma_start(Wgu[:, slot, :, part, :], src[n][e].rearrange("(k p) f -> p k f", p=P)).then_inc(w_in[slot], 16)
                    sp.dma_start(Wd[:, slot, :], src["Wd"][e]).then_inc(w_in[slot], 16)

                with nc.allow_non_contiguous_dma("biases to partitions"):
                    load(wa[:, :, :], w["L0_ffn_wa"].rearrange("(k p) e -> p k e", p=P))
                    load(R.iota[:, :], w["iota16"].partition_broadcast(P))
                    for dst, r, s in ((gb, "rgb", "sgb"), (ub, "rb1", "sb1")):
                        load(dst[:, 0:NE], w["L0_ffn_" + r].rearrange("e f -> f e"))
                        load(dst[:, NE:], w["L0_ffn_" + s].rearrange("e f -> f e"))
                    load(b2[0:NE, :], w["L0_ffn_rb2"])
                    load(b2[NE:, :], w["L0_ffn_sb2"])
                with sp.Fori(0, PAIRS) as i:
                    for slot in range(2):
                        sp.wait_ge(downs, i * 8 + 4 * (slot + 1))
                        weights(src_r, i * 2 + slot, slot)
                for slot in range(2):
                    sp.wait_ge(downs, PAIRS * 8 + 4 * (slot + 1))
                    weights(src_s, slot, slot)

            @block.gpsimd
            def _(pool):
                def low(e, slot):
                    m.wait_apart(pool, high, e + 1)
                    pool.tensor_tensor(Wx[:, slot, 1], Wgu[:, slot], Wx[:, slot, 0], ALU.subtract).then_inc(split, 1)

                with pool.Fori(0, PAIRS) as i:
                    for slot in range(2):
                        low(i * 2 + slot, slot)
                for slot in range(2):
                    low(NE + slot, slot)

            @block.scalar
            def _(act):
                def split_high(slot, uses):
                    m.wait_apart(act, w_in[slot], 48 * uses + 48)
                    act.activation(Wx[:, slot, 0], Wgu[:, slot], ACT.Copy, scale=SPLIT)
                    act.activation(Wgu[:, slot], Wgu[:, slot], ACT.Copy, scale=SPLIT).then_inc(high, 1)

                split_high(0, 0)
                R.scalar(act, m.bank[0])
                for q in range(NBLK):
                    act.wait_ge(routed_T, q + 1)
                    act.activation(rT[:, :, :].rearrange("p a b -> p (a b)"), m.bank[1][0:NE + SH, :],
                                   ACT.Copy).then_inc(rt_ready, 1)

                def pair(i, e0, end=False):
                    for st in range(8):
                        slot, q = divmod(st, NBLK)
                        m.wait_apart(act, gate_up, i * 8 + st + 1)
                        act.activation(gelu[:, q % 2, :], m.bank[q % 2][:, :], ACT.Gelu, scale=UNSPLIT,
                                       bias=gb[:, ds(e0 + slot, 1)]).then_inc(gated, 1)
                        if q == 1 and not (end and slot):
                            split_high(1 - slot, i + slot)

                with act.Fori(0, PAIRS) as i:
                    pair(i, i * 2)
                pair(PAIRS, NE, end=True)

            @block.vector
            def _(dve):
                dve.wait_ge(loaded, 16 * 8)
                for bias in (ub, b2):
                    dve.tensor_scalar(bias[:, :], bias[:, :], SPLIT ** 2, None, ALU.mult).then_inc(prepared, 1)
                dve.wait_ge(prepared, 2)
                R.vector(dve)
                for q in range(NBLK):
                    dve.wait_ge(biased, 2 * q + 2)
                    for half in range(2):
                        t = q * TPB + 2 * half
                        x2 = m.X[:, t:t + 2, :].rearrange("p t d -> p (t d)")
                        dve.tensor_tensor(x2, m.bank[2 + half][:, :], x2, ALU.add).then_inc(summed, 1)
                dve.sem_inc(hready, 2)

                def hidden(i, e0, st):
                    slot, q = divmod(st, NBLK)
                    dve.wait_ge(gated, i * 8 + st + 1)
                    dve.scalar_tensor_tensor(h[:, q % 2, :], m.bank[2 + q % 2][:, :], ub[:, ds(e0 + slot, 1)],
                                             gelu[:, q % 2, :], ALU.add, ALU.mult).then_inc(hready, 1)

                def add(i, e0, st):
                    slot, q = divmod(st, NBLK)
                    dve.wait_ge(downs, 8 + i * 8 + st + 1)
                    for j in range(TPB):
                        t = q * TPB + j
                        last = dve.scalar_tensor_tensor(
                            m.X[:, t, :], m.bank[4 + 2 * (q % 2) + j // 2][:, (j % 2) * D:(j % 2 + 1) * D],
                            R.route[:, t, ds(e0 + slot, 1)], m.X[:, t, :], ALU.mult, ALU.add)
                    last.then_inc(summed, 1)

                def pair(i, e0):
                    hidden(i, e0, 0)
                    for st in range(8):
                        if st < 7:
                            hidden(i, e0, st + 1)
                        add(i, e0, st)

                with dve.Fori(0, PAIRS) as i:
                    pair(i, i * 2)
                pair(PAIRS, NE)

            @block.tensor
            def _(pe):
                pe.sem_inc(downs, 8)
                pe.wait_ge(loaded, 16 * 8)
                R.tensor(pe, wa, m.bank[0])
                pe.wait_ge(R.done, 1)
                for q in range(NBLK):
                    if q:
                        pe.wait_ge(summed, 2 * q)
                    for j in range(TPB):
                        mm = pe.transpose(m.bank[1][0:NE + SH, j * P:(j + 1) * P], R.route[:, q * TPB + j, :], m.ident[:, :])
                    mm.then_inc(routed_T, 1)
                    pe.wait_ge(rt_ready, q + 1)
                    for j in range(TPB):
                        mm = pe.matmul(m.bank[2 + j // 2][:, (j % 2) * D:(j % 2 + 1) * D], rT[:, j, :], b2[:, :],
                                       start=True, stop=True)
                        if j % 2:
                            mm.then_inc(biased, 1)
                pe.wait_ge(summed, 2 * NBLK)

                def gate_and_up(i, st):
                    slot, q = divmod(st, NBLK)
                    if q == 0:
                        pe.wait_ge(split, i * 2 + slot + 1)
                    pe.wait_ge(hready, i * 8 + st + 1)
                    for part in range(2):
                        mm = split_product(pe, m.bank[2 * part + q % 2][:, :], lambda x, k: Wx[:, slot, x, k, part, :],
                                           lambda x, k: (m.xh, m.xl)[x][:, k, q * BLK:(q + 1) * BLK])
                    mm.then_inc(gate_up, 1)

                def down(i, st):
                    slot, q = divmod(st, NBLK)
                    if q == 0:
                        pe.wait_ge(w_in[slot], i * 48 + 48)
                    pe.wait_ge(hready, 2 + i * 8 + st + 1)
                    pe.wait_ge(summed, 2 * NBLK - 2 + i * 8 + st + 1)
                    for j in range(TPB):
                        mm = pe.matmul(m.bank[4 + 2 * (q % 2) + j // 2][:, (j % 2) * D:(j % 2 + 1) * D],
                                       h[:, q % 2, j * P:(j + 1) * P], Wd[:, slot, :], start=True, stop=True)
                    mm.then_inc(downs, 1)

                def pair(i):
                    gate_and_up(i, 0)
                    for st in range(8):
                        if st < 7:
                            gate_and_up(i, st + 1)
                        down(i, st)

                with pe.Fori(0, PAIRS) as i:
                    pair(i)
                pair(PAIRS)


def lightning_attention(nc, m, w):
    NH, HD = 16, 128
    Q, K, V, GT = range(4)
    PAIRS = NH // 2
    SPH = NBLK
    SPP = 2 * SPH
    TURN = 2
    (loaded, prep, decays, wload, wturned, wt_ready, proj, evac, scored, masked, mixed, ocopied, squared, yready, outs,
     summed, ssq, sd_ready, chain_s, wt_high, wo_ready) = (m.sem(f"d_{n}") for n in (
        "loaded", "prep", "decays", "wload", "wturned", "wt_ready", "proj", "evac", "scored", "masked", "mixed",
        "ocopied", "squared", "y", "outs", "summed", "ssq", "sd", "chain", "wt_high", "wo"))
    with ExitStack() as own:
        def sb(n, s, dt=F32):
            return m.sb("d_" + n, s, dt, own)

        Wn = sb("Wn", [P, 4, D])
        Won = sb("Won", [P, KC, HD])
        WT = sb("WT", [P, 2, 2, KC, 4, HD], F16)
        WoT = sb("WoT", [HD, 2, D])
        nw = sb("nw", [HD, NH])
        slope = sb("slope", [P, NH])
        rel = sb("rel", [P, P])
        tri = sb("tri", [P, P])
        decay = sb("decay", [P, NH, P])
        qT, kT, gt, vS, oS = (sb(n, [P, 2, BLK]) for n in ("qT", "kT", "gt", "vS", "oS"))
        A = sb("A", [P, TPB, P])
        y = sb("y", [P, BLK])
        sq = sb("sq", [P, BLK])
        SQ = sb("SQ", [P, TOK])
        ACC = sb("ACC", [P, NT, D])
        ones = sb("ones", [P, 1])
        eps = sb("eps", [P, 1])
        sd = sb("sd", [P, NT])
        rstd = sb("rstd", [P, NT])
        NPREP = 6
        with nc.Block() as block:
            @block.sync
            def _(sp):
                def load(dst, src):
                    sp.dma_start(dst, src).then_inc(loaded, 16)

                with nc.allow_non_contiguous_dma("norm_w to partitions"):
                    load(nw[:, :], w["L1_attn_norm_w"].rearrange("(h d) -> d h", d=HD))
                load(slope[:, :], w["L1_attn_slope_rate"].rearrange("h a b -> (h a b)").partition_broadcast(P))
                load(rel[:, :], w["rel"])
                load(tri[:, :], w["tri"])
                with sp.Fori(0, NH) as h:
                    sp.wait_ge(wturned, h + 1)
                    sp.dma_start(Wn[:, 0:3, :], w["L1_attn_w_qkv"][ds(h * 3 * HD, 3 * HD), :]
                                 .rearrange("(m o) f -> o m f", o=HD)).then_inc(wload, 16)
                    sp.dma_start(Wn[:, 3, :], w["L1_attn_w_gate"][ds(h * HD, HD), :]).then_inc(wload, 16)
                    sp.dma_start(Won[:, :, :], w["L1_attn_w_out"][:, ds(h * HD, HD)]
                                 .rearrange("(k p) o -> p k o", p=P)).then_inc(wload, 16)

            @block.gpsimd
            def _(pool):
                pool.memset(SQ[:, :], 0.0).then_inc(squared, 4)
                with pool.Fori(0, NH) as h:
                    for q in range(SPH):
                        s = h * SPH + q
                        pool.wait_ge(ocopied, s + 2)
                        pool.wait_ge(squared, 2 * s + 4)
                        o = oS[:, q % 2, :]
                        pool.tensor_tensor(sq[:, :], o, o, ALU.mult).then_inc(squared, 1)
                        pool.wait_ge(squared, 2 * s + 5)
                        acc = SQ[:, q * BLK:(q + 1) * BLK]
                        pool.tensor_tensor(acc, acc, sq[:, :], ALU.add).then_inc(squared, 1)

            @block.scalar
            def _(act):
                act.wait_ge(prep, NPREP)
                for h in range(NH):
                    act.activation(decay[:, h, :], rel[:, :], ACT.Exp, scale=slope[:, h:h + 1]).then_inc(decays, 1)
                act.sem_inc(evac, 4)
                act.sem_inc(ocopied, 1)

                def turn(h, slot):
                    m.wait_apart(act, wturned, h + 2)
                    for k in range(KC):
                        act.activation(WT[:, slot, 0, k, :, :].rearrange("p a b -> p (a b)"), m.bank[6 + k][:, :],
                                       ACT.Copy, scale=SPLIT).then_inc(wt_high, 1)
                    act.activation(WoT[:, slot, :], m.bank[4][:, 0:D], ACT.Copy,
                                   scale=nw[:, ds(h, 1)]).then_inc(wo_ready, 1)

                def qkg(s, q, turn_next=None):
                    for n, dst in enumerate((qT, kT, gt)):
                        if n == 2 and turn_next:
                            turn(*turn_next)
                        act.wait_ge(proj, 4 * s + n + 1)
                        if n == 2:
                            ins = act.activation(dst[:, q % 2, :], m.bank[n][:, :], ACT.Tanh, scale=0.5 * UNSPLIT)
                        else:
                            ins = act.activation(dst[:, q % 2, :], m.bank[n][:, :], ACT.Silu, scale=UNSPLIT)
                        ins.then_inc(evac, 1)

                def values(s, q):
                    act.wait_ge(proj, 4 * s + 4)
                    act.activation(vS[:, q % 2, :], m.bank[3][:, :], ACT.Silu, scale=UNSPLIT).then_inc(evac, 1)

                def pair(i, last):
                    for st in range(SPP):
                        u, q = divmod(st, SPH)
                        s, h = i * SPP + st, i * 2 + u
                        end = last and st == SPP - 1
                        if not end:
                            qkg(s + 1, q + 1, (h + 1, 1 - u) if q == TURN and not (last and u == 1) else None)
                        act.wait_ge(squared, 2 * s + 2)
                        act.wait_ge(mixed, s + 1)
                        act.activation(oS[:, q % 2, :], m.bank[5][:, :], ACT.Copy).then_inc(ocopied, 1)
                        if not end:
                            values(s + 1, q + 1)

                turn(0, 0)
                qkg(0, 0)
                values(0, 0)
                with act.Fori(0, PAIRS - 1) as i:
                    pair(i, False)
                pair(PAIRS - 1, True)
                act.wait_ge(ssq, 1)
                act.activation(sd[:, :], m.bank[0][:, 0:NT], ACT.Sqrt, scale=1.0 / (NH * HD),
                               bias=eps[:, :]).then_inc(sd_ready, 1)

            @block.vector
            def _(dve):
                dve.memset(ACC[:, :, :], 0.0).then_inc(prep, 1)
                dve.memset(ones[:, :], 1.0).then_inc(prep, 1)
                dve.memset(eps[:, :], 1e-6).then_inc(prep, 1)
                dve.wait_ge(loaded, 16 * 4)
                dve.tensor_scalar(nw[:, :], nw[:, :], 0.5, None, ALU.mult).then_inc(prep, 1)
                dve.tensor_scalar(slope[:, :], slope[:, :], -1.0, None, ALU.mult).then_inc(prep, 2)
                dve.wait_ge(decays, NH)
                dve.tensor_tensor(decay[:, :, :], decay[:, :, :], tri[:, :].unsqueeze(1).broadcast_to((P, NH, P)),
                                  ALU.mult).then_inc(prep, 1)
                dve.wait_ge(prep, NPREP + 1)
                dve.sem_inc(masked, 1)
                dve.sem_inc(summed, 1)

                def turned_low(h):
                    dve.wait_ge(wt_high, KC * h + KC)
                    for k in range(KC):
                        high, low = (WT[:, ds(h % 2, 1), x, k, :, :].rearrange("p s a b -> p (s a b)") for x in range(2))
                        last = dve.scalar_tensor_tensor(low, m.bank[6 + k][:, :], SPLIT, high, ALU.mult, ALU.subtract)
                    last.then_inc(wt_ready, 1)

                def head(h, end):
                    for q in range(SPH):
                        s = h * SPH + q
                        if q == TURN and not end:
                            turned_low(h + 1)
                        dve.wait_ge(scored, s + 1)
                        dve.tensor_tensor(A[:, :, :], m.bank[4][:, :].rearrange("p (a b) -> p a b", a=TPB),
                                          decay[:, ds(h, 1), :].broadcast_to((P, TPB, P)), ALU.mult).then_inc(masked, 1)
                        dve.wait_ge(ocopied, s + 2)
                        dve.wait_ge(evac, 4 + 4 * s + 3)
                        dve.scalar_tensor_tensor(y[:, :], gt[:, q % 2, :], 1.0, oS[:, q % 2, :], ALU.add,
                                                 ALU.mult).then_inc(yready, 1)
                        dve.wait_ge(outs, s + 1)
                        for half in range(2):
                            t = q * TPB + 2 * half
                            a2 = ACC[:, t:t + 2, :].rearrange("p t d -> p (t d)")
                            last = dve.tensor_tensor(a2, m.bank[6 + half][:, :], a2, ALU.add)
                        last.then_inc(summed, 1)

                turned_low(0)
                with dve.Fori(0, NH - 1) as h:
                    head(h, False)
                head(NH - 1, True)
                dve.wait_ge(sd_ready, 1)
                dve.reciprocal(rstd[:, :], sd[:, :]).then_inc(chain_s, 1)
                dve.wait_ge(chain_s, 1)
                dve.wait_ge(summed, 1 + NH * SPH)
                for t in range(NT):
                    dve.scalar_tensor_tensor(m.X[:, t, :], ACC[:, t, :], rstd[:, t:t + 1], m.X[:, t, :], ALU.mult, ALU.add)

            @block.tensor
            def _(pe):
                pe.sem_inc(wturned, 1)
                pe.wait_ge(prep, NPREP)

                def turn(h):
                    pe.wait_ge(wload, 48 * h + 48)
                    for k in range(KC):
                        for n in range(4):
                            pe.transpose(m.bank[6 + k][:, n * HD:(n + 1) * HD], Wn[:, n, k * P:(k + 1) * P], m.ident[:, :])
                    for k in range(KC):
                        mm = pe.transpose(m.bank[4][:, k * P:(k + 1) * P], Won[:, k, :], m.ident[:, :])
                    mm.then_inc(wturned, 1)

                def wide(s, q, slot, n):
                    b = {Q: 0, K: 1, GT: 2}[n]
                    pe.wait_ge(evac, 4 * s + b + 1)
                    split_product(pe, m.bank[b][:, :], lambda x, k: WT[:, slot, x, k, n, :],
                                  lambda x, k: (m.xh, m.xl)[x][:, k, q * BLK:(q + 1) * BLK]).then_inc(proj, 1)

                def values(s, q, slot):
                    pe.wait_ge(evac, 4 * s + 4)
                    for j in range(TPB):
                        t = q * TPB + j
                        mm = split_product(pe, m.bank[3][:, j * HD:(j + 1) * HD],
                                           lambda x, k: (m.xh, m.xl)[x][:, k, t * P:(t + 1) * P],
                                           lambda x, k: WT[:, slot, x, k, V, :])
                    mm.then_inc(proj, 1)

                def output(s, slot, turned_since, h):
                    pe.wait_ge(yready, s + 1)
                    pe.wait_ge(summed, s + 1)
                    if turned_since:
                        pe.wait_ge(wt_ready, h + 2)
                    for j in range(TPB):
                        mm = pe.matmul(m.bank[6 + j // 2][:, (j % 2) * D:(j % 2 + 1) * D], y[:, j * P:(j + 1) * P],
                                       WoT[:, slot, :], start=True, stop=True)
                    mm.then_inc(outs, 1)

                def pair(i, first, last):
                    for st in range(SPP):
                        u, q = divmod(st, SPH)
                        s, h = i * SPP + st, i * 2 + u
                        end = last and st == SPP - 1
                        nslot, nq = ((st + 1) // SPH) % 2, (q + 1) % SPH
                        turns = q == TURN and not (last and u == 1)

                        def score():
                            pe.wait_ge(evac, 4 + 4 * s + 2)
                            pe.wait_ge(masked, s + 1)
                            if turns:
                                pe.wait_ge(wo_ready, h + 2)
                            for j in range(TPB):
                                tok = slice(j * P, (j + 1) * P)
                                mm = pe.matmul(m.bank[4][:, tok], kT[:, q % 2, tok], qT[:, q % 2, tok], start=True, stop=True)
                            mm.then_inc(scored, 1)

                        def mix():
                            pe.wait_ge(masked, s + 2)
                            pe.wait_ge(evac, 4 + 4 * s + 4)
                            pe.wait_ge(ocopied, s + 1)
                            for j in range(TPB):
                                tok = slice(j * P, (j + 1) * P)
                                mm = pe.matmul(m.bank[5][:, tok], vS[:, q % 2, tok], A[:, j, :], start=True, stop=True)
                            mm.then_inc(mixed, 1)

                        if not end:
                            wide(s + 1, nq, nslot, Q)
                        if not (first and st == 0):
                            output(s - 1, (st - 1) % SPP // SPH, (q - 1) % SPH == TURN and not (last and u == 1), h)
                        if not end:
                            wide(s + 1, nq, nslot, K)
                        if turns:
                            pe.wait_ge(summed, s + 1)
                            pe.wait_ge(masked, s + 1)
                            turn(h + 1)
                            wide(s + 1, nq, nslot, GT)
                            score()
                            values(s + 1, nq, nslot)
                            mix()
                        else:
                            score()
                            if not end:
                                wide(s + 1, nq, nslot, GT)
                            mix()
                            if not end:
                                values(s + 1, nq, nslot)

                turn(0)
                pe.wait_ge(wt_ready, 1)
                pe.wait_ge(wo_ready, 1)
                wide(0, 0, 0, Q)
                wide(0, 0, 0, K)
                wide(0, 0, 0, GT)
                values(0, 0, 0)
                pair(0, True, False)
                with pe.Fori(1, PAIRS - 1) as i:
                    pair(i, False, False)
                pair(PAIRS - 1, False, True)
                output(NH * SPH - 1, 1, False, NH - 1)
                pe.wait_ge(squared, 4 + 2 * NH * SPH)
                for t in range(NT):
                    mm = pe.matmul(m.bank[0][:, t:t + 1], SQ[:, t * P:(t + 1) * P], ones[:, :], start=True, stop=True)
                mm.then_inc(ssq, 1)


def quantised_attention(nc, m, w):
    H, HD = 16, 16
    PR = H // 2
    U16 = mybir.dt.uint16
    KT = TOK // P
    HALF = TOK // 2
    LN255 = float(np.log(255.0))
    names = "loaded prep copied proj taken packed turned stored".split()
    loaded, prep, copied, proj, taken, packed, turned, stored = (m.sem(f"e_{n}") for n in names)
    chain_s, vmaxed, vall, v_ready = (m.sem(f"e_{n}") for n in ("chain", "vmax", "vall", "v"))
    q_here, scored, biased, exped, tturned, evac0, evac1, mixed, normed, chain2 = (m.sem(f"e_{n}") for n in (
        "q_here", "scored", "biased", "exped", "tturned", "evac0", "evac1", "mixed", "normed", "chain2"))
    xb, o_ready, o_turned, ot_ready, outp, added, chain3 = (m.sem(f"e_{n}") for n in (
        "xb", "o", "o_turned", "oT", "outp", "added", "chain3"))
    with ExitStack() as own:
        def sb(n, s, dt=F32, ctx=own):
            return m.sb("e_" + n, s, dt, ctx)

        QT = sb("QT", [P, NT * PR, P], BF16)
        KTt = sb("KT", [P, PR, TOK], BF16)
        Vi = sb("Vi", [P, KT, H, HD], BF16)
        sq = sb("sq", [P, NT * H])
        nsq = sb("nsq", [P, NT * H])
        sv = sb("sv", [P, D])
        identb = sb("identb", [P, P], BF16)
        bp = sb("bp", [P, D])
        Wp = sb("Wp", [P, KC, D])
        with ExitStack() as first:
            def sb1(n, s, dt=F32):
                return m.sb("e_" + n, s, dt, first)

            Wq = sb1("Wq", [P, KC, D])
            Wkv = sb1("Wkv", [P, KC, 2, D])
            bias = sb1("bias", [P, 3, D])
            xs, cs = sb1("xs", [P, KC, BLK]), sb1("cs", [P, KC, BLK])
            V32 = sb1("V32", [P, NT, D])
            z = sb1("z", [P, 2, H, HD])
            am, s_, rs = (sb1(n, [P, 2, H]) for n in ("am", "s", "rs"))
            k32, r32 = sb1("k32", [P, H, HD]), sb1("r32", [P, H, HD])
            Tq, Tk = (sb1(n, [P, 2, H, 4, HD], BF16) for n in ("Tq", "Tk"))
            vm, vma, rv = (sb1(n, [P, D]) for n in ("vm", "vma", "rv"))
            with nc.Block() as block:
                @block.sync
                def _(sp):
                    def load(dst, src):
                        sp.dma_start(dst, src).then_inc(loaded, 16)
                    load(Wq[:, :, :], w["L1_xattn_Wq"].rearrange("(k p) n -> p k n", p=P))
                    load(Wkv[:, :, :, :].rearrange("p k a n -> p k (a n)"), w["L1_xattn_Wkv"].rearrange("(k p) n -> p k n", p=P))
                    load(Wp[:, :, :], w["L1_xattn_Wp"].rearrange("(k p) n -> p k n", p=P))
                    load(bias[:, 0, :], w["L1_xattn_bq"].partition_broadcast(P))
                    load(bias[:, 1:3, :].rearrange("p a n -> p (a n)"), w["L1_xattn_bkv"].partition_broadcast(P))
                    load(bp[:, :], w["L1_xattn_bp"].partition_broadcast(P))

                @block.gpsimd
                def _(pool):
                    pool.wait_ge(vmaxed, 1)
                    pool.partition_all_reduce(vma[:, :], vm[:, :], P, bass.bass_isa.ReduceOp.max).then_inc(vall, 1)
                    pool.wait_ge(loaded, 16 * 6)
                    pool.tensor_tensor(m.X[:, :, :], m.X[:, :, :], bp[:, :].unsqueeze(1).broadcast_to((P, NT, D)),
                                       ALU.add).then_inc(xb, 1)

                @block.scalar
                def _(act):
                    act.sem_inc(stored, 2)
                    with act.Fori(0, NBLK) as i:
                        act.wait_ge(proj, i * TPB + 1)
                        act.activation(xs[:, :, :], m.xnT[:, :, ds(i * BLK, BLK)], ACT.Copy).then_inc(copied, 1)
                        act.activation(cs[:, :, :], m.ctxT[:, :, ds(i * BLK, BLK)], ACT.Copy).then_inc(copied, 1)
                        for tt in range(TPB):
                            t = i * TPB + tt
                            m.wait_apart(act, turned, t + 3)
                            b = 4 + 2 * (tt % 2)
                            act.activation(QT[:, ds(t * PR, PR), :].rearrange("p a b -> p (a b)"),
                                           m.bank[b].bitcast(BF16), ACT.Copy)
                            act.activation(KTt[:, :, ds(t * P, P)], m.bank[b + 1].bitcast(BF16)
                                           .rearrange("p (a b) -> p a b", a=PR), ACT.Copy).then_inc(stored, 1)

                @block.vector
                def _(dve):
                    dve.tensor_copy(identb[:, :], m.ident[:, :]).then_inc(prep, 1)
                    dve.memset(Tq[:, :, :, :, :].rearrange("p a b c d -> p (a b c d)"), 0.0).then_inc(prep, 1)
                    dve.memset(Tk[:, :, :, :, :].rearrange("p a b c d -> p (a b c d)"), 0.0).then_inc(prep, 1)
                    dve.wait_ge(loaded, 16 * 6)
                    dve.tensor_scalar(bias[:, 0, :], bias[:, 0, :], HD ** -0.5, None, ALU.mult).then_inc(prep, 1)
                    dve.wait_ge(prep, 4)
                    dve.sem_inc(taken, 2)
                    STEPS = 10
                    with dve.Fori(0, NBLK) as i:
                        c = Chain(dve, chain_s)
                        c.enter(i, STEPS * TPB)
                        for tt in range(TPB):
                            t = i * TPB + tt
                            sl = tt % 2
                            dve.wait_ge(proj, t + 2)
                            A, B = m.bank[sl], m.bank[2 + sl]
                            for n, sc in ((0, HD ** -0.5), (1, 1.0)):
                                last = dve.scalar_tensor_tensor(z[:, n, :, :].rearrange("p h d -> p (h d)"),
                                                                A[:, n * D:(n + 1) * D], sc, bias[:, n, :], ALU.mult, ALU.add)
                            c.do(last)
                            dve.tensor_tensor(V32[:, t, :], B[:, 0:D], bias[:, 2, :], ALU.add).then_inc(taken, 1)
                            zf = z[:, :, :, :].rearrange("p a h d -> p (a h) d")
                            amf, sf, rf = (x[:, :, :].rearrange("p a h -> p (a h)") for x in (am, s_, rs))
                            c.do(dve.tensor_reduce(amf, zf, AX, ALU.max, apply_absolute_value=True))
                            c.do(dve.tensor_scalar(sf, amf, 1.0 / 127.0, 1e-8, ALU.mult, ALU.max))
                            dve.tensor_copy(sq[:, ds(t * H, H)], s_[:, 0, :])
                            c.do(dve.reciprocal(rf, sf))
                            c.do(dve.tensor_tensor(zf, zf, rf.unsqueeze(2).broadcast_to((P, 2 * H, HD)), ALU.mult))
                            dve.wait_ge(turned, t + 1)
                            for cp in range(3):
                                last = dve.tensor_scalar(Tq[:, sl, :, cp, :], z[:, 0, :, :], MAGIC, MAGIC, ALU.add, ALU.subtract)
                            c.do(dve.tensor_scalar(k32[:, :, :], z[:, 1, :, :], MAGIC, MAGIC, ALU.add, ALU.subtract))
                            c.do(dve.tensor_tensor(k32[:, :, :], k32[:, :, :],
                                                   s_[:, 1, :].unsqueeze(2).broadcast_to((P, H, HD)), ALU.mult))
                            c.do(dve.tensor_copy(Tk[:, sl, :, 0, :], k32[:, :, :]))
                            c.do(dve.tensor_tensor(r32[:, :, :], k32[:, :, :], Tk[:, sl, :, 0, :], ALU.subtract))
                            c.do(dve.tensor_copy(Tk[:, sl, :, 1, :], r32[:, :, :]))
                            dve.tensor_tensor(Tk[:, sl, :, 2, :], r32[:, :, :], Tk[:, sl, :, 1, :],
                                              ALU.subtract).then_inc(packed, 1)
                        assert c.n == STEPS * TPB, c.n
                    c = Chain(dve, chain2)
                    dve.wait_ge(taken, 2 + NT)
                    dve.tensor_reduce(vm[:, :], V32[:, :, :].rearrange("p t c -> p c t"), AX, ALU.max,
                                      apply_absolute_value=True).then_inc(vmaxed, 1)
                    c.do(dve.tensor_scalar(nsq[:, :], sq[:, :], -1.0, None, ALU.mult))
                    dve.wait_ge(vall, 1)
                    c.do(dve.tensor_scalar(sv[:, :], vma[:, :], 1.0 / 127.0, 1e-8, ALU.mult, ALU.max))
                    c.do(dve.reciprocal(rv[:, :], sv[:, :]))
                    c.do(dve.tensor_tensor(V32[:, :, :], V32[:, :, :], rv[:, :].unsqueeze(1).broadcast_to((P, NT, D)), ALU.mult))
                    c.do(dve.tensor_scalar(Vi[:, :, :, :].rearrange("p t h d -> p (t h d)"),
                                           V32[:, :, :].rearrange("p t c -> p (t c)"), MAGIC, MAGIC, ALU.add, ALU.subtract))

                @block.tensor
                def _(pe):
                    pe.sem_inc(proj, 1)
                    pe.sem_inc(turned, 2)
                    pe.wait_ge(prep, 4)

                    def project(i, tt):
                        t = i * TPB + tt
                        sl = tt % 2
                        tok = slice(tt * P, (tt + 1) * P)
                        pe.wait_ge(taken, t + 1)
                        for out, src, W in ((m.bank[sl][:, 0:D], xs, lambda k: Wq[:, k, :]),
                                            (m.bank[sl][:, D:], cs, lambda k: Wkv[:, k, 0, :]),
                                            (m.bank[2 + sl][:, 0:D], cs, lambda k: Wkv[:, k, 1, :])):
                            for k in range(KC):
                                mm = pe.matmul(out, src[:, k, tok], W(k), start=(k == 0), stop=(k == KC - 1))
                        mm.then_inc(proj, 1)

                    with pe.Fori(0, NBLK) as i:
                        pe.wait_ge(copied, 2 * i + 2)
                        project(i, 0)
                        for tt in range(TPB):
                            t = i * TPB + tt
                            sl = tt % 2
                            if tt < TPB - 1:
                                project(i, tt + 1)
                            pe.wait_ge(packed, t + 1)
                            pe.wait_ge(stored, t + 1)
                            for src, b in ((Tq, 4 + 2 * sl), (Tk, 5 + 2 * sl)):
                                for pr in range(PR):
                                    mm = pe.transpose(m.bank[b].bitcast(BF16)[:, pr * P:(pr + 1) * P],
                                                      src[:, sl, 2 * pr:2 * pr + 2, :, :].rearrange("p h c d -> p (h c d)"),
                                                      identb[:, :])
                            mm.then_inc(turned, 1)

        N = NT * H
        Qs = sb("Qs", [P, 4, P], BF16)
        e16 = sb("e16", [P, 2, TOK], U16)
        PT = sb("PT", [P, 2, KT // 2, P], BF16)
        mx = sb("mx", [P, 2, 5])
        ebias = sb("ebias", [P, 2])
        esum = sb("esum", [P, 4, N])
        Osb = sb("Osb", [P, NT, D])
        RING = 5
        SC = 4 * 8
        turn_bank, out_bank = (m.bank[5].bitcast(BF16), m.bank[6].bitcast(BF16)), m.bank[7]

        def ring(j, b):
            return m.bank[(4 * j + b) % RING]

        def loop(eng, step):
            def tile(t):
                for j in range(H):
                    step(t * H + j, j, t)
            tile(0)
            with eng.Fori(1, NT - 1) as i:
                tile(i)
            tile(NT - 1)

        def first(n):
            return isinstance(n, int) and n == 0

        def last(n):
            return isinstance(n, int) and n == N - 1

        with nc.Block() as block:
            @block.gpsimd
            def _(pool):
                with pool.Fori(0, NT) as i:
                    for jp in range(PR):
                        pair = i * PR + jp
                        m.wait_apart(pool, scored, 8 * pair + 8)
                        pool.tensor_copy(Qs[:, jp % 4, :], QT[:, ds(pair, 1), :].rearrange("p a b -> p (a b)")).then_inc(q_here, 1)

            @block.tensor
            def _(pe):
                pe.sem_inc(scored, SC)

                def score(n, j, *quarters):
                    rows = slice(64 * (j % 2), 64 * (j % 2) + 48)
                    for b in quarters:
                        m.wait_apart(pe, exped, 4 * n + b + (2 if j == 0 and not first(n) else 1))
                        if b == 0 and j % 2 == 0:
                            m.wait_apart(pe, q_here, (n // 2) + 1)
                        pe.matmul(ring(j, b), Qs[rows, j // 2 % 4, :], KTt[rows, j // 2, b * BLK:(b + 1) * BLK],
                                  start=True, stop=True).then_inc(scored, 1)

                def turn(n, j, hf):
                    m.wait_apart(pe, exped, RING + 4 * n + 2 * hf + 2)
                    for k in range(KT // 2):
                        col = hf * HALF + k * P
                        mm = pe.transpose(turn_bank[hf][:, k * P:(k + 1) * P], e16[:, j % 2, col:col + P].bitcast(BF16), identb[:, :])
                    mm.then_inc(tturned, 1)

                def mix(n, j, t, hf):
                    m.wait_apart(pe, (evac0, evac1)[hf], n + 2)
                    if j == 0 and hf == 0:
                        m.wait_apart(pe, normed, t + 1)
                    for k in range(KT // 2):
                        kt = hf * (KT // 2) + k
                        mm = pe.matmul(out_bank[:, j * HD:(j + 1) * HD], PT[:, hf, k, :], Vi[:, kt, j, :],
                                       start=(kt == 0), stop=(kt == KT - 1))
                    if hf and j == H - 1:
                        mm.then_inc(mixed, 1)

                score(0, 0, 0, 1, 2, 3)

                def step(n, j, t):
                    nj = (j + 1) % H
                    if not last(n):
                        score(n + 1, nj, 0)
                    if not first(n):
                        mix(n - 1, (j - 1) % H, t, 0)
                    if not last(n):
                        score(n + 1, nj, 1, 2, 3)
                    turn(n, j, 0)
                    if not first(n):
                        mix(n - 1, (j - 1) % H, t, 1)
                    turn(n, j, 1)
                loop(pe, step)
                mix(N - 1, H - 1, NT - 1, 0)
                mix(N - 1, H - 1, NT - 1, 1)

            @block.vector
            def _(dve):
                dve.sem_inc(normed, 1)
                dve.sem_inc(evac0, 1)

                def maxima(n, j, c):
                    for b in range(4):
                        dve.wait_ge(scored, SC + 4 * n + b + 1)
                        red = dve.tensor_reduce(mx[:, j % 2, b:b + 1], ring(j, b), AX, ALU.max)
                    c.do(red)
                    c.do(dve.tensor_reduce(mx[:, j % 2, 4:5], mx[:, j % 2, 0:4], AX, ALU.max))
                    dve.tensor_scalar(ebias[:, j % 2:j % 2 + 1], mx[:, j % 2, 4:5], nsq[:, ds(n, 1)], LN255,
                                      ALU.mult, ALU.add).then_inc(biased, 1)

                def take(n):
                    dve.wait_ge(tturned, 2 * n + 1)
                    dve.tensor_copy(PT[:, 0, :, :].rearrange("p a b -> p (a b)"), turn_bank[0].bitcast(U16)).then_inc(evac0, 1)

                def output(t):
                    dve.wait_ge(mixed, t + 1)
                    dve.tensor_copy(Osb[:, ds(t, 1), :].rearrange("p a b -> p (a b)"), out_bank[:, 0:D]).then_inc(normed, 1)

                def step(n, j, t):
                    if not last(n):
                        c = Chain(dve, chain3)
                        c.base = 2 * n + 2
                        maxima(n + 1, (j + 1) % H, c)
                    take(n)
                    if j == 0 and not first(n):
                        output(t - 1)
                maxima(0, 0, Chain(dve, chain3))
                loop(dve, step)
                output(NT - 1)

            @block.scalar
            def _(act):
                act.sem_inc(exped, RING)
                act.sem_inc(evac1, 1)

                def exp(n, j, b):
                    act.activation(e16[:, j % 2, b * BLK:(b + 1) * BLK], ring(j, b), ACT.Exp, bias=ebias[:, j % 2:j % 2 + 1],
                                   scale=sq[:, ds(n, 1)], accum_out=esum[:, b, ds(n, 1)]).then_inc(exped, 1)

                def take(n):
                    act.wait_ge(tturned, 2 * n + 2)
                    act.activation(PT[:, 1, :, :].rearrange("p a b -> p (a b)"), turn_bank[1].bitcast(U16), ACT.Copy).then_inc(evac1, 1)

                def step(n, j, t):
                    m.wait_apart(act, biased, n + 1)
                    for b in range(4):
                        exp(n, j, b)
                        if b == 2 and not first(n):
                            take(n - 1)
                loop(act, step)
                take(N - 1)

        rsum = sb("rsum", [P, N])
        on = sb("on", [P, TPB, H, HD])
        onT = sb("onT", [P, KC, BLK])
        with nc.Block() as block:
            @block.vector
            def _(dve):
                c = Chain(dve, o_ready)
                c.do(dve.tensor_reduce(rsum[:, :], esum[:, :, :].rearrange("p b n -> p n b"), AX, ALU.add))
                c.do(dve.reciprocal(rsum[:, :], rsum[:, :]))
                dve.sem_inc(outp, 1)
                with dve.Fori(0, NBLK) as i:
                    nn = TPB * H
                    dve.wait_ge(o_turned, KC * i + 1)
                    of = on[:, :, :, :].rearrange("p t h d -> p (t h) d")
                    dve.tensor_tensor(on[:, :, :, :].rearrange("p t h d -> p t (h d)"),
                                      Osb[:, ds(i * TPB, TPB), :],
                                      sv[:, :].unsqueeze(1).broadcast_to((P, TPB, D)), ALU.mult).then_inc(o_ready, 1)
                    dve.wait_ge(o_ready, 2 + 2 * i + 1)
                    dve.tensor_tensor(of, of, rsum[:, ds(i * nn, nn)].unsqueeze(2).broadcast_to((P, nn, HD)),
                                      ALU.mult).then_inc(o_ready, 1)
                    for half in range(2):
                        dve.wait_ge(outp, i * 2 + half + 2)
                        x2 = m.X[:, ds(i * TPB + 2 * half, 2), :].rearrange("p t d -> p (t d)")
                        dve.tensor_tensor(x2, m.bank[2 + half], x2, ALU.add).then_inc(added, 1)

            @block.scalar
            def _(act):
                with act.Fori(0, NBLK) as i:
                    for k in range(KC):
                        act.wait_ge(o_turned, KC * i + k + 2)
                        act.activation(onT[:, k, :], m.bank[k], ACT.Copy).then_inc(ot_ready, 1)

            @block.tensor
            def _(pe):
                pe.sem_inc(o_turned, 1)
                with pe.Fori(0, NBLK) as i:
                    pe.wait_ge(o_ready, 2 + 2 * i + 2)
                    for k in range(KC):
                        for j in range(TPB):
                            mm = pe.transpose(m.bank[k][:, j * P:(j + 1) * P],
                                              on[:, j, k * H // 2:(k + 1) * H // 2, :].rearrange("p h d -> p (h d)"), m.ident[:, :])
                        mm.then_inc(o_turned, 1)
                    pe.wait_ge(ot_ready, KC * i + KC)
                    for j in range(TPB):
                        for k in range(KC):
                            mm = pe.matmul(m.bank[2 + j // 2][:, (j % 2) * D:(j % 2 + 1) * D], onT[:, k, j * P:(j + 1) * P],
                                           Wp[:, k, :], start=(k == 0), stop=(k == KC - 1))
                        if j % 2:
                            mm.then_inc(outp, 1)


def experts_top4(nc, m, w):
    NE, F, FB = 16, 176, 48
    PAIRS = NE // 2
    ROWS = (P, FB)
    UPPER = slice(64, 64 + FB)
    names = "loaded gate_w wa w0 w1 padded scaled high split up copied product h downs summed"
    (loaded, gate_turned, wa_ready, w_in0, w_in1, padded, scaled, high, split, up, copied, product, hready, downs, summed) = (
        m.sem(f"f_{n}") for n in names.split())
    w_in = (w_in0, w_in1)
    with ExitStack() as own:
        def sb(n, s, dt=F32):
            return m.sb("f_" + n, s, dt, own)

        gw, wa, gb = sb("gw", [NE, D]), sb("wa", [P, KC, NE]), sb("gb", [P, NE])
        W13 = sb("W13", [P, 2, KC, 2, F])
        WA = sb("WA", [P, 2, 2, KC, 2, P], F16)
        WB = sb("WB", [P, 2, 2, KC, 2, 64], F16)
        W2 = sb("W2", [P, 2, 2, D])
        h1, pr, h = (sb(n, [P, 2, 2, BLK]) for n in ("h1", "pr", "h"))
        R = Router(m, "f", own, 4, 1)
        with nc.Block() as block:
            @block.sync
            def _(sp):
                def load(dst, src):
                    sp.dma_start(dst, src).then_inc(loaded, 16)

                def weights(w1, w3, w2, slot):
                    for n, src in enumerate((w1, w3)):
                        sp.dma_start(W13[:, slot, :, n, :], src.rearrange("(k p) f -> p k f", p=P)).then_inc(w_in[slot], 16)
                    sp.dma_start(W2[:, slot, 0, :], w2[0:P, :]).then_inc(w_in[slot], 16)
                    sp.dma_start(W2[0:FB, slot, 1, :], w2[P:F, :]).then_inc(w_in[slot], 16)

                load(gw[:, :], w["L1_ffn_gate_w"])
                load(gb[:, :], w["L1_ffn_gate_b"].partition_broadcast(P))
                load(R.iota[:, :], w["iota16"].partition_broadcast(P))
                w1, w3, w2 = (w[f"L1_ffn_w{n}_routed"] for n in (1, 3, 2))
                with sp.Fori(0, PAIRS) as i:
                    for slot in range(2):
                        e = i * 2 + slot
                        sp.wait_ge(downs, i * 8 + 4 * (slot + 1))
                        weights(w1[e], w3[e], w2[e], slot)
                sp.wait_ge(downs, PAIRS * 8 + 4)
                weights(*(w[f"L1_ffn_w{n}_shared"] for n in (1, 3, 2)), 0)

            def parts(slot, x):
                return ((WA[:, slot, x], W13[:, slot, :, :, 0:P]), (WB[:, slot, x, :, :, 0:FB], W13[:, slot, :, :, P:F]))

            @block.gpsimd
            def _(pool):
                pool.memset(WB[:, :, :, :, :, :], 0.0).then_inc(padded, 1)

                def low(e, slot):
                    m.wait_apart(pool, high, e + 1)
                    for (lo, src), (hi, _) in zip(parts(slot, 1), parts(slot, 0)):
                        last = pool.tensor_tensor(lo, src, hi, ALU.subtract)
                    last.then_inc(split, 1)

                pool.wait_ge(padded, 1)
                with pool.Fori(0, PAIRS) as i:
                    for slot in range(2):
                        low(i * 2 + slot, slot)
                low(NE, 0)

            @block.scalar
            def _(act):
                def split_high(slot, uses):
                    act.wait_ge(w_in[slot], 64 * uses + 64)
                    act.activation(W13[:, slot], W13[:, slot], ACT.Copy, scale=SPLIT).then_inc(scaled, 1)
                    m.wait_apart(act, scaled, 2 * uses + slot + 1)
                    for hi, src in parts(slot, 0):
                        last = act.activation(hi, src, ACT.Copy)
                    last.then_inc(high, 1)

                act.wait_ge(padded, 1)
                split_high(0, 0)
                act.wait_ge(gate_turned, 1)
                act.activation(wa[:, :, :].rearrange("p k e -> p (k e)"), m.bank[1][:, 0:KC * NE], ACT.Copy).then_inc(wa_ready, 1)
                R.scalar(act, m.bank[0])

                def steps(i, n, first, second):
                    for st in range(n):
                        slot, q = divmod(st, NBLK)
                        act.wait_ge(up, i * 8 + st + 1)
                        act.activation(h1[:, q % 2, 0, :], m.bank[0][:, :], first, scale=UNSPLIT)
                        act.activation(h1[UPPER, q % 2, 1, :], m.bank[2][0:FB, :], first, scale=UNSPLIT).then_inc(copied, 1)
                        act.wait_ge(product, i * 8 + st + 2)
                        act.activation(h[:, q % 2, 0, :], pr[:, q % 2, 0, :], second, scale=UNSPLIT)
                        act.activation(h[0:FB, q % 2, 1, :], pr[UPPER, q % 2, 1, :], second, scale=UNSPLIT).then_inc(hready, 1)
                        if q == 1 and n == 8:
                            split_high(1 - slot, i + slot)

                with act.Fori(0, PAIRS) as i:
                    steps(i, 8, ACT.Copy, ACT.Silu)
                steps(PAIRS, 4, ACT.Silu, ACT.Copy)

            @block.vector
            def _(dve):
                dve.wait_ge(loaded, 16 * 3)
                R.vector(dve, gb[:, :])
                dve.sem_inc(product, 1)
                dve.sem_inc(summed, 2)

                def multiply(i, st):
                    dve.wait_ge(copied, i * 8 + st + 1)
                    dve.tensor_tensor(pr[:, st % 2, 0, :], m.bank[1][:, :], h1[:, st % 2, 0, :], ALU.mult)
                    dve.tensor_tensor(pr[UPPER, st % 2, 1, :], m.bank[2][UPPER, :], h1[UPPER, st % 2, 1, :],
                                      ALU.mult).then_inc(product, 1)

                def add(i, e, st):
                    q = st % NBLK
                    dve.wait_ge(downs, 8 + i * 8 + st + 1)
                    for j in range(TPB):
                        t = q * TPB + j
                        last = dve.scalar_tensor_tensor(
                            m.X[:, t, :], m.bank[4 + 2 * (q % 2) + j // 2][:, (j % 2) * D:(j % 2 + 1) * D],
                            R.route[:, t, ds(e, 1)], m.X[:, t, :], ALU.mult, ALU.add)
                    last.then_inc(summed, 1)

                def steps(i, n, e0):
                    multiply(i, 0)
                    for st in range(n):
                        if st < n - 1:
                            multiply(i, st + 1)
                        add(i, e0 + st // NBLK, st)

                with dve.Fori(0, PAIRS) as i:
                    steps(i, 8, i * 2)
                steps(PAIRS, 4, NE)

            @block.tensor
            def _(pe):
                pe.sem_inc(downs, 8)
                pe.wait_ge(loaded, 16 * 3)
                for k in range(KC):
                    mm = pe.transpose(m.bank[1][:, k * NE:(k + 1) * NE], gw[:, k * P:(k + 1) * P], m.ident[0:NE, 0:NE])
                mm.then_inc(gate_turned, 1)
                pe.wait_ge(wa_ready, 1)
                R.tensor(pe, wa, m.bank[0])
                pe.wait_ge(R.done, 1)

                def hidden(i, st):
                    slot, q = divmod(st, NBLK)
                    if q == 0:
                        pe.wait_ge(split, i * 2 + slot + 1)
                    pe.wait_ge(product, i * 8 + st + 1)
                    tok = slice(q * BLK, (q + 1) * BLK)
                    for bank, W in ((0, lambda x, k: WA[:, slot, x, k, 0, :]), (1, lambda x, k: WA[:, slot, x, k, 1, :]),
                                    (2, lambda x, k: WB[:, slot, x, k, :, :].rearrange("p a b -> p (a b)"))):
                        mm = split_product(pe, m.bank[bank][:, :], W, lambda x, k: (m.xh, m.xl)[x][:, k, tok])
                    mm.then_inc(up, 1)

                def down(i, st):
                    slot, q = divmod(st, NBLK)
                    if q == 0:
                        pe.wait_ge(w_in[slot], i * 64 + 64)
                    pe.wait_ge(hready, i * 8 + st + 1)
                    pe.wait_ge(summed, i * 8 + st + 1)
                    for j in range(TPB):
                        for part, r in enumerate(ROWS):
                            mm = pe.matmul(m.bank[4 + 2 * (q % 2) + j // 2][:, (j % 2) * D:(j % 2 + 1) * D],
                                           h[0:r, q % 2, part, j * P:(j + 1) * P], W2[0:r, slot, part, :],
                                           start=(part == 0), stop=(part == 1))
                    mm.then_inc(downs, 1)

                def steps(i, n):
                    hidden(i, 0)
                    for st in range(n):
                        if st < n - 1:
                            hidden(i, st + 1)
                        down(i, st)

                with pe.Fori(0, PAIRS) as i:
                    steps(i, 8)
                steps(PAIRS, 4)


def constants():
    J, M, HU = 32, 96, 3
    inv_freq = (1.0 / 10000.0 ** (np.arange(0, 64, 2, dtype=np.float32) / np.float32(64))).astype(np.float32)
    col = np.tile(inv_freq, HU)
    head = np.arange(M) // J
    slopes = (np.float32(2.0 ** -0.5) ** np.arange(1, 17, dtype=np.float32)).reshape(4, 4).T
    q, k = np.arange(P) % SEQ, np.arange(SEQ)
    rel = (k[None, :] - q[:, None]).astype(np.float32)
    row = np.arange(P)
    ahead = ((row[None, :] - row[:, None])).astype(np.float32)
    same = (row[None, :] // SEQ == row[:, None] // SEQ) & (ahead >= 0)
    return {
        "rel": np.where(same, ahead, 0).astype(np.float32),
        "tri": same.astype(np.float32),
        "alibi": (slopes.reshape(1, 16, 1) * rel[:, None, :]).astype(np.float32).reshape(P, 16 * SEQ),
        "gmask": ((row[:, None] % 64) // 16 == np.arange(4)).astype(np.float32),
        "hmask": (row[:, None] // 64 == np.arange(2)).astype(np.float32),
        "iota16": np.arange(16, dtype=np.float32),
        "ident": np.eye(P, dtype=np.float32),
        "freq": np.stack([col, -col], 1).astype(np.float32),
        "mean_w": ((head[:, None] == head[None, :]) / np.float32(64 * 4)).astype(np.float32),
    }


def build(nc, w, out):
    with ExitStack() as ctx:
        m = Mem(nc, ctx)
        x_ready, stored = m.sem("x_ready"), m.sem("stored")
        load_inputs(nc, m, w["x"], w["ctx_2048"], w["ident"], x_ready)
        layernorm(nc, m)
        own = {k[len("L0_attn_"):]: v for k, v in w.items() if k.startswith("L0_attn_")}
        rotary_recurrence(nc, m, {**own, "freq": w["freq"], "mean_w": w["mean_w"]})
        layernorm(nc, m)
        gqa_cross_attention(nc, m, w)
        layernorm(nc, m, add_to_x=True, split=True)
        experts_top2(nc, m, w)
        layernorm(nc, m, split=True)
        lightning_attention(nc, m, w)
        layernorm(nc, m)
        quantised_attention(nc, m, w)
        layernorm(nc, m, split=True)
        experts_top4(nc, m, w)
        with nc.Block() as block:
            @block.sync
            def _(sp):
                sp.dma_start(out.rearrange("(t p) d -> p t d", p=P), m.X[:, :, :]).then_inc(stored, 16)
                sp.wait_ge(stored, 16)


def kernel(**inputs):
    import concourse.bacc as bacc
    from concourse.bass_utils import run_bass_kernel_spmd

    nc = bacc.Bacc("TRN2", target_bir_lowering=False, num_devices=1)
    arrays = {k: np.ascontiguousarray(v) for k, v in inputs.items()}
    for name in ("x", "ctx_2048"):
        arrays[name] = arrays[name].reshape(TOK, D)
    arrays.update(constants())
    arrays["mask_BxS2_bf1"] = arrays["mask_BxS2_bf1"].view(np.uint8)
    aps = {k: nc.dram_tensor("in_" + k, a.shape, mybir.dt.from_np(a.dtype), kind="ExternalInput").ap()
           for k, a in arrays.items()}
    out = nc.dram_tensor("out_0", (TOK, D), F32, kind="ExternalOutput").ap()
    build(nc, aps, out)
    r = run_bass_kernel_spmd(nc, [{"in_" + k: a for k, a in arrays.items()}], core_ids=[0])
    return r.results[0]["out_0"].reshape(BATCH, SEQ, D)
```

```python
from contextlib import ExitStack

import numpy as np
import concourse.bass as bass
from concourse import mybir

F32 = mybir.dt.float32
BF16 = mybir.dt.bfloat16
F16 = mybir.dt.float16
U8 = mybir.dt.uint8
U32 = mybir.dt.uint32
ALU = mybir.AluOpType
ACT = mybir.ActivationFunctionType
AX = mybir.AxisListType.X
ds = bass.ds

BATCH, SEQ, D = 32, 64, 256
TOK = BATCH * SEQ
P = 128
NT = TOK // P
KC = D // P
BLK = 512
NBLK = TOK // BLK
TPB = BLK // P
BPB = BLK // SEQ
MAGIC = 12582912.0
SPLIT = 1024.0
UNSPLIT = SPLIT ** -2
FLT_MAX = 3.4028234663852886e38


class Mem:

    def __init__(self, nc, ctx):
        self.nc, self.ctx = nc, ctx
        self.X = self.sb("X", [P, NT, D])
        self.xnT = self.sb("xnT", [P, KC, TOK])
        self.xh, self.xl = (self.sb(n, [P, KC, TOK], F16) for n in ("xh", "xl"))
        self.ctxT = self.sb("ctxT", [P, KC, TOK])
        self.ident = self.sb("ident", [P, P])
        self.psum = ctx.enter_context(nc.psum_tensor("psum", [P, 8, 512], F32))
        self.bank = [self.psum[:, i, :] for i in range(8)]

        self.apart = self.sem("apart")
        self.norms = 0
        self.norm_sems = [self.sem(f"ln_{n}") for n in "stats moments sd rstd xn turned bank_free high".split()]
        self.splits = 0

    def wait_apart(self, eng, sem, value):
        eng.wait_ge(sem, value)
        eng.sem_inc(self.apart, 1)

    def sb(self, name, shape, dt=F32, ctx=None):
        return (ctx or self.ctx).enter_context(self.nc.sbuf_tensor(name, shape, dt))

    def sem(self, name):
        return self.ctx.enter_context(self.nc.semaphore(name))


class Chain:

    def __init__(self, eng, sem, apart=None):
        self.eng, self.sem, self.n, self.base, self.apart = eng, sem, 0, 0, apart

    def enter(self, i, per):
        self.base = i * per

    def do(self, ins):
        self.n += 1
        ins.then_inc(self.sem, 1)
        if self.apart:
            self.apart.wait_apart(self.eng, self.sem, self.base + self.n)
        else:
            self.eng.wait_ge(self.sem, self.base + self.n)


def split_product(pe, out, lhsT, rhs, chunks=KC):
    terms = [(a, b, k) for a, b in ((0, 0), (0, 1), (1, 0)) for k in range(chunks)]
    for n, (a, b, k) in enumerate(terms):
        mm = pe.matmul(out, lhsT(a, k), rhs(b, k), start=(n == 0), stop=(n == len(terms) - 1))
    return mm


def load_inputs(nc, m, x, ctx_tokens, c_ident, x_ready):
    tile_in, turned, bank_free = (m.sem(n) for n in ("ld_ctx", "ld_turned", "ld_bank_free"))
    ready = m.sem("ld_consts")
    with ExitStack() as own:
        C = m.sb("ctx_rows", [P, NT, D], ctx=own)
        with nc.Block() as block:
            @block.sync
            def _(sp):
                sp.dma_start(m.ident[:, :], c_ident).then_inc(ready, 16)
                sp.dma_start(C[:, :, :], ctx_tokens.rearrange("(t p) d -> p t d", p=P)).then_inc(tile_in, 16)
                sp.dma_start(m.X[:, :, :], x.rearrange("(t p) d -> p t d", p=P)).then_inc(x_ready, 16)

            @block.tensor
            def _(pe):
                pe.wait_ge(ready, 16)
                pe.wait_ge(tile_in, 16)
                for g in range(NBLK * KC):
                    b, c = divmod(g, KC)
                    if g >= 4:
                        pe.wait_ge(bank_free, g - 3)
                    for j in range(TPB):
                        last = pe.transpose(m.bank[g % 4][:, j * P:(j + 1) * P],
                                            C[:, b * TPB + j, c * P:(c + 1) * P], m.ident[:, :])
                    last.then_inc(turned, 1)

            @block.scalar
            def _(act):
                for g in range(NBLK * KC):
                    b, c = divmod(g, KC)
                    act.wait_ge(turned, g + 1)
                    act.activation(m.ctxT[:, c, b * BLK:(b + 1) * BLK], m.bank[g % 4][:, :],
                                   ACT.Copy).then_inc(bank_free, 1)
            @block.vector
            def _(dve):
                dve.wait_ge(x_ready, 16)


def layernorm(nc, m, preload, add_to_x=False, split=False):
    stats_done, moments_done, sd_done, rstd_done, xn_ready, turned, bank_free, high = m.norm_sems
    r = m.norms
    m.norms += 1
    highs = m.splits * NBLK
    m.splits += int(split)
    tag, tiles, turns = f"ln{r}", r * NT, r * NBLK
    with ExitStack() as own:
        stats = m.sb(f"{tag}_stats", [P, NT, 6], ctx=own)
        mom = m.sb(f"{tag}_mom", [P, NT, 2], ctx=own)
        sd = m.sb(f"{tag}_sd", [P, NT], ctx=own)
        rstd = m.sb(f"{tag}_rstd", [P, NT], ctx=own)
        eps = m.sb(f"{tag}_eps", [P, 1], ctx=own)
        xn = m.sb(f"{tag}_xn", [P, 2, TPB, D], ctx=own)
        with nc.Block() as block:
            @block.sync
            def _(sp):
                preload(sp)

            @block.vector
            def _(dve):
                dve.memset(eps[:, :], 1e-5).then_inc(moments_done, 1)
                for t in range(NT):
                    dve.bn_stats(stats[:, t, :], m.X[:, t, :]).then_inc(stats_done, 1)
                dve.wait_ge(stats_done, tiles + NT)
                for t in range(NT):
                    dve.bn_aggr(mom[:, t, :], stats[:, t, :]).then_inc(moments_done, 1)
                dve.wait_ge(sd_done, r + 1)
                dve.reciprocal(rstd[:, :], sd[:, :]).then_inc(rstd_done, 1)
                dve.wait_ge(rstd_done, r + 1)

                def low(b):
                    dve.wait_ge(high, highs + b + 1)
                    tok = slice(b * BLK, (b + 1) * BLK)
                    pair = 2 * (b % 2)
                    dve.scalar_tensor_tensor(m.xl[:, :, tok], m.psum[:, pair:pair + 2, :], SPLIT, m.xh[:, :, tok],
                                             ALU.mult, ALU.subtract).then_inc(bank_free, 1)

                for b in range(NBLK):
                    if b >= 2:
                        dve.wait_ge(turned, turns + b - 1)
                    for j in range(TPB):
                        t = b * TPB + j
                        dve.tensor_scalar(xn[:, b % 2, j, :], m.X[:, t, :], mom[:, t, 0:1], rstd[:, t:t + 1],
                                          ALU.subtract, ALU.mult).then_inc(xn_ready, 1)
                    if add_to_x:
                        dve.wait_ge(xn_ready, tiles + (b + 1) * TPB)
                        x4 = m.X[:, b * TPB:(b + 1) * TPB, :]
                        dve.tensor_tensor(x4, x4, xn[:, b % 2, :, :], ALU.add)
                    if split and b:
                        low(b - 1)
                if split:
                    low(NBLK - 1)

            @block.scalar
            def _(act):
                act.wait_ge(moments_done, (r + 1) * (NT + 1))
                act.activation(sd[:, :], mom[:, :, 1], ACT.Sqrt, bias=eps[:, :]).then_inc(sd_done, 1)
                for b in range(NBLK):
                    act.wait_ge(turned, turns + b + 1)
                    tok = slice(b * BLK, (b + 1) * BLK)
                    for c in range(KC):
                        bank = m.bank[2 * (b % 2) + c]
                        if split:
                            last = act.activation(m.xh[:, c, tok], bank, ACT.Copy, scale=SPLIT)
                        else:
                            last = act.activation(m.xnT[:, c, tok], bank, ACT.Copy)
                    last.then_inc(high if split else bank_free, 1)

            @block.tensor
            def _(pe):
                for b in range(NBLK):
                    pe.wait_ge(xn_ready, tiles + (b + 1) * TPB)
                    if b >= 2:
                        pe.wait_ge(bank_free, turns + b - 1)
                    for c in range(KC):
                        for j in range(TPB):
                            last = pe.transpose(m.bank[2 * (b % 2) + c][:, j * P:(j + 1) * P],
                                                xn[:, b % 2, j, c * P:(c + 1) * P], m.ident[:, :])
                    last.then_inc(turned, 1)


def rotary_recurrence(nc, m, w):
    NH, HD, HU = 6, 64, 3
    J = HD // 2
    U = NH // HU
    M = HU * J
    VD = NH * HD
    K, Q, VE, VO, AL, BE, GE, GO = range(8)
    NG = 8
    CONVK = 4
    TWO_PI = 6.283185307179586
    TWO_PI_HI = 6.28125
    TWO_PI_LO = TWO_PI - TWO_PI_HI
    PI_IN = 3.1415925
    loaded, prep, proj, evac, chain_s = (m.sem(f"a_{n}") for n in ("loaded", "prep", "proj", "evac", "chain"))
    angle, sincos, scanned, squares, meansq, rms_ready, gated, outp, added = (m.sem(f"a_{n}") for n in (
        "angle", "sincos", "scanned", "squares", "meansq", "rms", "gated", "outp", "added"))
    logs = m.sem("a_logs")
    with ExitStack() as own:
        def sb(n, s, dt=F32):
            return m.sb("a_" + n, s, dt, own)

        Wq, Wk, Wv, Wg = (sb(n, [P, KC, VD]) for n in ("Wq", "Wk", "Wv", "Wg"))
        Wab = sb("Wab", [P, KC, 2, NH])
        WabX = sb("WabX", [P, KC, 2, NH, J])
        Wo = sb("Wo", [M, U, 2, D])
        cw = sb("cw", [M, U, 4, CONVK])
        cwr = sb("cwr", [M, U, 2, CONVK])
        freq = sb("freq", [M, 2])
        rw = sb("rw", [M, 2])
        half_pi = sb("half_pi", [M, 1])
        eps = sb("eps", [M, 1])
        mean_w = sb("mean_w", [M, M])
        pad = sb("pad", [M, U, 4, BPB, SEQ + CONVK - 1])
        tab = sb("tab", [M, U, 2, BLK])
        gs = sb("gs", [M, U, 2, BLK])
        ang, n1 = (sb(n, [M, BLK]) for n in ("ang", "n1"))
        absang = sb("absang", [M, U, BLK])
        sc = sb("sc", [M, U, 2, BLK])
        v = sb("v", [M, 2, BLK])
        u = sb("u", [M, 2, BLK])
        t4 = sb("t4", [M, 4, BLK])
        al = sb("al", [M, BPB, SEQ])
        o = sb("o", [M, U, 2, BLK])
        sq = sb("sq", [M, U, 2, BLK])
        rms = sb("rms", [M, U, BLK])
        og = sb("og", [M, U, 2, BLK])

        def wcols(g, unit, c):
            if g in (AL, BE):
                return WabX[:, c, g - AL, unit * HU:(unit + 1) * HU, :].rearrange("p h j -> p (h j)")
            W, odd = {K: (Wk, 0), Q: (Wq, 0), VE: (Wv, 0), VO: (Wv, 1), GE: (Wg, 0), GO: (Wg, 1)}[g]
            return W[:, c, unit * HU * HD:(unit + 1) * HU * HD].rearrange("p (n two) -> p n two", two=2)[:, :, odd]

        NLOAD = 4 + 2 + 2 * U + U * 4 + 1 + 2 * HU + 1
        def preload(sp):
            with nc.allow_non_contiguous_dma("small, strided weights"):
                for W, src in ((Wk, w["Wk"]), (Wq, w["Wq"]), (Wv, w["Wv"]), (Wg, w["Wg"])):
                    sp.dma_start(W[:, :, :], src.rearrange("(c p) n -> p c n", p=P)).then_inc(loaded, 16)
                for n, src in enumerate((w["Wa"], w["Wb"])):
                    sp.dma_start(Wab[:, :, n, :], src.rearrange("(c p) n -> p c n", p=P)).then_inc(loaded, 16)
                for unit in range(U):
                    rows = slice(unit * HU * HD, (unit + 1) * HU * HD)
                    for odd in range(2):
                        src = w["Wo"][rows, :].rearrange("(n two) d -> n two d", two=2)[:, odd, :]
                        sp.dma_start(Wo[:, unit, odd, :], src).then_inc(loaded, 16)
                    for n, (src, odd) in enumerate((("conv_k", 0), ("conv_q", 0), ("conv_v", 0), ("conv_v", 1))):
                        s = w[src][rows, :].rearrange("(n two) d -> n two d", two=2)[:, odd, :]
                        sp.dma_start(cw[:, unit, n, :], s).then_inc(loaded, 16)
                sp.dma_start(freq[:, :], w["freq"]).then_inc(loaded, 16)
                sp.dma_start(mean_w[:, :], w["mean_w"]).then_inc(loaded, 16)
                for h in range(HU):
                    for odd in range(2):
                        s = w["rms_w"].rearrange("(j two) -> j two", two=2)[:, odd:odd + 1]
                        sp.dma_start(rw[h * J:(h + 1) * J, odd:odd + 1], s).then_inc(loaded, 16)

        layernorm(nc, m, preload)
        with nc.Block() as block:
            @block.vector
            def _(dve):
                dve.memset(pad[:, :, :, :, 0:CONVK - 1].rearrange("p a b c d -> p (a b) c d"), 0.0).then_inc(prep, 1)
                dve.memset(half_pi[:, :], TWO_PI / 4).then_inc(prep, 1)
                dve.memset(eps[:, :], 1e-5).then_inc(prep, 1)
                dve.wait_ge(loaded, 16 * NLOAD)
                dve.tensor_copy(WabX[:, :, :, :, :].rearrange("p c w h j -> p (c w h) j"),
                                Wab[:, :, :, :].rearrange("p c w (h o) -> p (c w h) o", o=1)
                                .broadcast_to((P, KC * 2 * NH, J))).then_inc(prep, 1)
                for n in range(2):
                    dve.tensor_scalar(cwr[:, :, n, :], cw[:, :, n, :], freq[:, n:n + 1], None, ALU.mult).then_inc(prep, 1)
                dve.tensor_scalar(rw[:, :], rw[:, :], 0.5, None, ALU.mult).then_inc(prep, 1)
                dve.wait_ge(prep, 7)
                dve.sem_inc(gated, 3)

                def conv(c, unit, jobs, first=True):
                    for j in range(CONVK):
                        for n, out, wt in jobs:
                            src = pad[:, unit, n, :, j:j + SEQ]
                            dst = out.rearrange("p (b t) -> p b t", b=BPB)
                            if first and j == 0:
                                ins = dve.tensor_scalar(dst, src, wt[:, j:j + 1], None, ALU.mult)
                            else:
                                ins = dve.scalar_tensor_tensor(dst, src, wt[:, j:j + 1], dst, ALU.mult, ALU.add)
                        c.do(ins)

                FRONT, STEPS = 12, 22

                def front(c, k, unit):
                    dve.wait_ge(evac, k * NG + K + 1 + 4)
                    conv(c, unit, ((0, ang[:, :], cwr[:, unit, 0, :]),))
                    dve.wait_ge(evac, k * NG + Q + 1 + 4)
                    conv(c, unit, ((1, ang[:, :], cwr[:, unit, 1, :]),), first=False)
                    c.do(dve.tensor_scalar(n1[:, :], ang[:, :], 1 / TWO_PI, MAGIC, ALU.mult, ALU.add))
                    c.do(dve.tensor_scalar(n1[:, :], n1[:, :], MAGIC, None, ALU.subtract))
                    c.do(dve.scalar_tensor_tensor(ang[:, :], n1[:, :], -TWO_PI_HI, ang[:, :], ALU.mult, ALU.add))
                    c.do(dve.scalar_tensor_tensor(ang[:, :], n1[:, :], -TWO_PI_LO, ang[:, :], ALU.mult, ALU.add))
                    dve.tensor_scalar(absang[:, unit, :], ang[:, :], PI_IN, -PI_IN, ALU.min, ALU.max).then_inc(angle, 1)

                def middle(c, k, unit):
                    dve.wait_ge(evac, k * NG + VO + 1 + 4)
                    conv(c, unit, [(2 + odd, v[:, odd, :], cw[:, unit, 2 + odd, :]) for odd in range(2)])
                    dve.wait_ge(sincos, 2 * (k + 1))
                    s_, c_ = sc[:, unit, 0, :], sc[:, unit, 1, :]
                    ve, vo = v[:, 0, :], v[:, 1, :]
                    dve.tensor_tensor(t4[:, 0, :], ve, c_, ALU.mult)
                    dve.tensor_tensor(t4[:, 1, :], vo, s_, ALU.mult)
                    dve.tensor_tensor(t4[:, 2, :], vo, c_, ALU.mult)
                    c.do(dve.tensor_tensor(t4[:, 3, :], ve, s_, ALU.mult))
                    dve.tensor_tensor(u[:, 0, :], t4[:, 0, :], t4[:, 1, :], ALU.subtract)
                    c.do(dve.tensor_tensor(u[:, 1, :], t4[:, 2, :], t4[:, 3, :], ALU.add))
                    dve.wait_ge(evac, k * NG + BE + 1 + 4)
                    tb = tab[:, unit, 1, :]
                    dve.scalar_tensor_tensor(u[:, 0, :], tb, 1.0, u[:, 0, :], ALU.add, ALU.mult)
                    c.do(dve.scalar_tensor_tensor(u[:, 1, :], tb, 1.0, u[:, 1, :], ALU.add, ALU.mult))
                    alf = al[:, :, :].rearrange("p b t -> p (b t)")
                    c.do(dve.tensor_scalar(alf, tab[:, unit, 0, :], 0.5, 0.5, ALU.mult, ALU.add))
                    c.do(dve.memset(al[:, :, 0:1], 0.0))
                    for par in range(2):
                        dve.tensor_tensor_scan(o[:, unit, par, :], alf, u[:, par, :], 0.0,
                                               ALU.mult, ALU.add).then_inc(scanned, 1)

                def back(c, i, k, unit):
                    dve.wait_ge(rms_ready, k + 2)
                    dve.wait_ge(evac, k * NG + GO + 1 + 4)
                    dve.wait_ge(outp, i * 2 + 1)
                    for par in range(2):
                        last = dve.scalar_tensor_tensor(t4[:, par, :], o[:, unit, par, :], rw[:, par:par + 1],
                                                        rms[:, unit, :], ALU.mult, ALU.mult)
                    c.do(last)
                    for par in range(2):
                        dve.tensor_tensor(og[:, unit, par, :], t4[:, par, :], gs[:, unit, par, :],
                                          ALU.mult).then_inc(gated, 1)

                def add(i):
                    for half in range(2):
                        dve.wait_ge(outp, i * 2 + half + 2)
                        t = i * TPB + 2 * half
                        x2 = m.X[:, ds(t, 2), :].rearrange("p t d -> p (t d)")
                        dve.tensor_tensor(x2, m.bank[5 + half][:, :], x2, ALU.add).then_inc(added, 1)

                def units(i, first, last):
                    c = Chain(dve, chain_s)
                    c.base = i * (STEPS * U) + FRONT
                    for unit in range(U):
                        k = i * U + unit
                        middle(c, k, unit)
                        if unit == 0 and not first:
                            add(i - 1)
                        if not (last and unit == U - 1):
                            front(c, k + 1, (unit + 1) % U)
                        back(c, i, k, unit)
                    assert c.n == STEPS * U - (FRONT if last else 0), c.n

                front(Chain(dve, chain_s), 0, 0)
                units(0, True, False)
                with dve.Fori(1, NBLK - 1) as i:
                    units(i, False, False)
                units(NBLK - 1, False, True)
                add(NBLK - 1)

            @block.scalar
            def _(act):
                act.sem_inc(evac, 4)
                act.sem_inc(rms_ready, 1)
                act.wait_ge(prep, 6)

                def evacuate(k, unit):
                    for g in range(NG):
                        act.wait_ge(proj, k * NG + g + 1)
                        if g == GE:
                            act.wait_ge(gated, k * 2 + 1)
                        src = m.bank[g % 4][0:M, :]
                        if g in (K, Q, VE, VO):
                            ins = act.activation(pad[:, unit, g, :, CONVK - 1:],
                                                 src.rearrange("p (b t) -> p b t", b=BPB), ACT.Copy)
                        elif g in (AL, BE):
                            ins = act.activation(tab[:, unit, g - AL, :], src, ACT.Tanh, scale=0.5)
                        else:
                            ins = act.activation(gs[:, unit, g - GE, :], src, ACT.Silu)
                        ins.then_inc(evac, 1)

                def units(i, last):
                    for unit in range(U):
                        k = i * U + unit
                        act.wait_ge(angle, k + 1)
                        act.activation(sc[:, unit, 0, :], absang[:, unit, :], ACT.Sin).then_inc(sincos, 1)
                        act.activation(rms[:, unit, :], absang[:, unit, :], ACT.Abs).then_inc(squares, 1)
                        act.wait_ge(squares, k * 3 + 1)
                        act.activation(sc[:, unit, 1, :], rms[:, unit, :], ACT.Sin, scale=-1.0,
                                       bias=half_pi[:, :]).then_inc(sincos, 1)
                        if not (last and unit == U - 1):
                            evacuate(k + 1, (unit + 1) % U)
                        act.wait_ge(scanned, 2 * (k + 1))
                        for par in range(2):
                            act.activation(sq[:, unit, par, :], o[:, unit, par, :], ACT.Square).then_inc(squares, 1)
                        act.wait_ge(meansq, k + 1)
                        act.wait_ge(sincos, 2 * (k + 1))
                        act.activation(rms[:, unit, :], m.bank[4][0:M, :], ACT.Ln, bias=eps[:, :]).then_inc(logs, 1)
                        act.wait_ge(logs, k + 1)
                        act.activation(rms[:, unit, :], rms[:, unit, :], ACT.Exp, scale=-0.5).then_inc(rms_ready, 1)

                evacuate(0, 0)
                with act.Fori(0, NBLK - 1) as i:
                    units(i, False)
                units(NBLK - 1, True)

            @block.tensor
            def _(pe):
                pe.wait_ge(prep, 6)
                pe.sem_inc(outp, 1)

                def project(i, k, unit):
                    for g in range(NG):
                        pe.wait_ge(evac, k * NG + g + 1)
                        for c in range(KC):
                            mm = pe.matmul(m.bank[g % 4][0:M, :], wcols(g, unit, c),
                                           m.xnT[:, c, ds(i * BLK, BLK)], start=(c == 0), stop=(c == KC - 1))
                        mm.then_inc(proj, 1)

                def output(i):
                    pe.wait_ge(gated, 3 + (i + 1) * U * 2)
                    for half in range(2):
                        for j in range(2):
                            tok = slice((2 * half + j) * P, (2 * half + j + 1) * P)
                            for n in range(2 * U):
                                mm = pe.matmul(m.bank[5 + half][:, j * D:(j + 1) * D], og[:, n // 2, n % 2, tok],
                                               Wo[:, n // 2, n % 2, :], start=(n == 0), stop=(n == 2 * U - 1))
                        mm.then_inc(outp, 1)

                def units(i, first, last):
                    for unit in range(U):
                        k = i * U + unit
                        if not (last and unit == U - 1):
                            project(i + (unit + 1) // U, k + 1, (unit + 1) % U)
                        if unit == 0 and not first:
                            output(i - 1)
                        for par in range(2):
                            pe.wait_ge(squares, k * 3 + 2 + par)
                            if par == 0:
                                pe.wait_ge(rms_ready, k + 1)
                            mm = pe.matmul(m.bank[4][0:M, :], mean_w[:, :], sq[:, unit, par, :],
                                           start=(par == 0), stop=(par == 1))
                        mm.then_inc(meansq, 1)

                project(0, 0, 0)
                units(0, True, False)
                with pe.Fori(1, NBLK - 1) as i:
                    units(i, False, False)
                units(NBLK - 1, False, True)
                output(NBLK - 1)


def gqa_cross_attention(nc, m, w):
    G, C, HD = 4, 4, 16
    NH = G * C
    GD = G * HD
    loaded, prep, ctx_copied, proj, evac = (m.sem(f"b_{n}") for n in ("loaded", "prep", "ctx", "proj", "evac"))
    bias_ready, scores, biased, shifted, exped = (m.sem(f"b_{n}") for n in ("bias", "scores", "biased", "shifted", "exped"))
    turned, pt_ready, mixed, ao_ready, ao_turned, aot_ready, outp, added, chain_s = (m.sem(f"b_{n}") for n in (
        "turned", "pt", "mixed", "ao", "ao_turned", "aot", "outp", "added", "chain"))
    with ExitStack() as own:
        def sb(n, s, dt=F32):
            return m.sb("b_" + n, s, dt, own)

        WqR = sb("WqR", [P, KC, G, C, HD])
        Wq = sb("Wq", [P, KC, C, G, HD])
        Wk = sb("Wk", [P, KC, 2, GD])
        Wv = sb("Wv", [P, KC, GD])
        Wo = sb("Wo", [P, KC, D])
        alibi = sb("alibi", [P, NH, SEQ])
        gmask = sb("gmask", [P, G])
        hmask = sb("hmask", [P, 2])
        mask8 = sb("mask8", [P, NT, SEQ], U8)
        neg = sb("neg", [P, NT, SEQ])
        ctxS = sb("ctxS", [P, KC, BLK])
        QT = sb("QT", [P, 2, BLK])
        Kbd = sb("Kbd", [P, BPB, G, SEQ])
        Vbd = sb("Vbd", [P, BPB * 2, 2, HD])
        bias = sb("bias", [P, 2, NH, SEQ])
        S = sb("S", [P, 2, NH, SEQ])
        mx, tot, rtot = (sb(n, [P, NH]) for n in ("mx", "tot", "rtot"))
        PT = sb("PT", [P, 2 * C, P])
        ao = sb("ao", [P, G, C, HD])
        aoT = sb("aoT", [P, KC, P])
        NLOAD = 1 + 2 + 1 + 1 + 3 + 2
        def preload(sp):
            def load(dst, src):
                sp.dma_start(dst, src).then_inc(loaded, 16)
            with nc.allow_non_contiguous_dma("small weights, mask rows"):
                load(WqR[:, :, :, :, :].rearrange("p k g c d -> p k (g c d)"),
                     w["L0_xattn_Wq"].rearrange("(k p) n -> p k n", p=P))
                for half in range(2):
                    load(Wk[:, :, half, :], w["L0_xattn_Wk"].rearrange("(k p) n -> p k n", p=P))
                load(Wv[:, :, :], w["L0_xattn_Wv"].rearrange("(k p) n -> p k n", p=P))
                load(Wo[:, :, :], w["L0_xattn_Wo"].rearrange("(k p) n -> p k n", p=P))
                load(alibi[:, :, :].rearrange("p h k -> p (h k)"), w["alibi"])
                load(gmask[:, :], w["gmask"])
                load(hmask[:, :], w["hmask"])
                for b in range(2):
                    src = w["mask_BxS2_bf1"].rearrange("(t b) k -> b t k", b=2)[b]
                    load(mask8[b * SEQ:(b + 1) * SEQ, :, :], src.partition_broadcast(SEQ))

        layernorm(nc, m, preload)
        with nc.Block() as block:
            @block.gpsimd
            def _(pool):
                pool.wait_ge(prep, 1 + KC * C)
                with pool.Fori(0, NBLK) as i:
                    pool.wait_ge(proj, i * 4 + 4)
                    pool.tensor_copy(ctxS[:, :, :], m.ctxT[:, :, ds(i * BLK, BLK)]).then_inc(ctx_copied, 1)
                    for tt in range(TPB):
                        n = i * TPB + tt
                        pool.wait_ge(biased, n + 1)
                        pool.tensor_tensor(bias[:, tt % 2, :, :], alibi[:, :, :],
                                           neg[:, ds(n, 1), :].broadcast_to((P, NH, SEQ)), ALU.add).then_inc(bias_ready, 1)

            @block.scalar
            def _(act):
                act.wait_ge(prep, 1 + KC * C)
                with act.Fori(0, NBLK) as i:
                    for c in range(2):
                        act.wait_ge(proj, i * 4 + 4 + c + 1)
                        act.activation(QT[:, c, :], m.bank[c][:, :], ACT.Copy).then_inc(evac, 1)
                    act.wait_ge(proj, i * 4 + 4 + 3)
                    for g in range(G):
                        last = act.activation(Kbd[:, :, g, :], m.bank[2][:, :].rearrange("p (b k) -> p b k", k=SEQ),
                                              ACT.Copy, scale=gmask[:, g:g + 1])
                    last.then_inc(evac, 1)
                    act.wait_ge(proj, i * 4 + 4 + 4)
                    for h in range(2):
                        src = m.bank[3][:, :].rearrange("p (a h d) -> p a h d", h=2, d=HD)[:, :, h, :]
                        last = act.activation(Vbd[:, :, h, :], src, ACT.Copy, scale=hmask[:, h:h + 1])
                    last.then_inc(evac, 1)

                    def ao_copy(n):
                        act.wait_ge(ao_turned, n + 1)
                        act.activation(aoT[:, :, :].rearrange("p a b -> p (a b)"), m.bank[1][:, 0:KC * P],
                                       ACT.Copy).then_inc(aot_ready, 1)

                    for tt in range(TPB):
                        n = i * TPB + tt
                        act.wait_ge(shifted, n + 1)
                        act.activation(S[:, tt % 2, :, :], S[:, tt % 2, :, :], ACT.Exp).then_inc(exped, 1)
                        for h in range(2):
                            act.wait_ge(turned, 2 * n + h + 1)
                            act.activation(PT[:, 4 * h:4 * h + 4, :].rearrange("p a b -> p (a b)"), m.bank[6 + h][:, :],
                                           ACT.Copy).then_inc(pt_ready, 1)
                        if tt:
                            ao_copy(n - 1)
                    ao_copy(i * TPB + TPB - 1)

            @block.vector
            def _(dve):
                dve.wait_ge(loaded, 16 * NLOAD)
                dve.tensor_scalar(neg[:, :, :], mask8[:, :, :], 1.0, FLT_MAX, ALU.subtract, ALU.mult).then_inc(prep, 1)
                for k in range(KC):
                    for c in range(C):
                        slot = 2 * (c % 2) + c // 2
                        dve.tensor_copy(Wq[:, k, slot, :, :], WqR[:, k, :, c, :]).then_inc(prep, 1)
                dve.sem_inc(biased, 2)
                dve.sem_inc(added, 1)

                def front(c, n, tt):
                    s = S[:, tt % 2, :, :]
                    dve.wait_ge(scores, n + 1)
                    dve.wait_ge(bias_ready, n + 1)
                    for h in range(2):
                        sl = slice(h * NH // 2, (h + 1) * NH // 2)
                        dve.scalar_tensor_tensor(s[:, sl, :].rearrange("p a b -> p (a b)"), m.bank[4 + h][:, :], HD ** -0.5,
                                                 bias[:, tt % 2, sl, :].rearrange("p a b -> p (a b)"), ALU.mult,
                                                 ALU.add).then_inc(*((biased, 1) if h else (chain_s, 1)))
                    c.n += 1
                    dve.wait_ge(biased, n + 3)
                    c.do(dve.tensor_reduce(mx[:, :], s, AX, ALU.max))
                    dve.tensor_tensor(s, s, mx[:, :].unsqueeze(2).broadcast_to((P, NH, SEQ)),
                                      ALU.subtract).then_inc(shifted, 1)

                def add(n):
                    dve.wait_ge(outp, n + 1)
                    dve.tensor_tensor(m.X[:, n, :], m.bank[3][:, 0:D], m.X[:, n, :], ALU.add).then_inc(added, 1)

                STEPS = TPB * 4
                with dve.Fori(0, NBLK) as i:
                    c = Chain(dve, chain_s)
                    c.enter(i, STEPS)
                    front(c, i * TPB, 0)
                    for tt in range(TPB):
                        n = i * TPB + tt
                        dve.wait_ge(exped, n + 1)
                        c.do(dve.tensor_reduce(tot[:, :], S[:, tt % 2, :, :], AX, ALU.add))
                        c.do(dve.reciprocal(rtot[:, :], tot[:, :]))
                        if tt < TPB - 1:
                            front(c, n + 1, tt + 1)
                        dve.wait_ge(mixed, n + 1)
                        dve.tensor_tensor(ao[:, :, :, :].rearrange("p g c d -> p c g d"),
                                          m.bank[0][:, 0:D].rearrange("p (c g d) -> p c g d", c=C, g=G),
                                          rtot[:, :].rearrange("p (c g o) -> p c g o", c=C, o=1)
                                          .broadcast_to((P, C, G, HD)), ALU.mult).then_inc(ao_ready, 1)
                        if tt:
                            add(n - 1)
                    add(i * TPB + TPB - 1)
                    assert c.n == STEPS, c.n

            @block.tensor
            def _(pe):
                pe.wait_ge(prep, 1 + KC * C)
                pe.sem_inc(proj, 4)

                def score(i, n, tt):
                    m.wait_apart(pe, biased, n + 2)
                    for b in range(2):
                        for c in range(C):
                            half = slice(64 * (c // 2), 64 * (c // 2) + 64)
                            tok = slice(tt * P + b * SEQ, tt * P + (b + 1) * SEQ)
                            mm = pe.matmul(m.bank[4 + c // 2][b * SEQ:(b + 1) * SEQ, (c % 2) * 256:(c % 2) * 256 + 256],
                                           QT[half, c % 2, tok],
                                           Kbd[half, 2 * tt + b, :, :].rearrange("p g k -> p (g k)"),
                                           start=True, stop=True)
                    mm.then_inc(scores, 1)

                def turn_out(n):
                    pe.wait_ge(ao_ready, n + 1)
                    for k in range(KC):
                        mm = pe.transpose(m.bank[1][:, k * P:(k + 1) * P],
                                          ao[:, 2 * k:2 * k + 2, :, :].rearrange("p g c d -> p (g c d)"), m.ident[:, :])
                    mm.then_inc(ao_turned, 1)

                def output(n):
                    pe.wait_ge(aot_ready, n + 1)
                    pe.wait_ge(added, n + 1)
                    for k in range(KC):
                        mm = pe.matmul(m.bank[3][:, 0:D], aoT[:, k, :], Wo[:, k, :], start=(k == 0), stop=(k == KC - 1))
                    mm.then_inc(outp, 1)

                with pe.Fori(0, NBLK) as i:
                    for c in range(2):
                        for k in range(KC):
                            mm = pe.matmul(m.bank[c][:, :], Wq[:, k, 2 * c:2 * c + 2, :, :].rearrange("p c g d -> p (c g d)"),
                                           m.xnT[:, k, ds(i * BLK, BLK)], start=(k == 0), stop=(k == KC - 1))
                        mm.then_inc(proj, 1)
                    for k in range(KC):
                        mm = pe.matmul(m.bank[2][:, :], Wk[:, k, :, :].rearrange("p a b -> p (a b)"),
                                       m.ctxT[:, k, ds(i * BLK, BLK)], start=(k == 0), stop=(k == KC - 1))
                    mm.then_inc(proj, 1)
                    pe.wait_ge(ctx_copied, i + 1)
                    pe.wait_ge(added, i * TPB + 1)
                    for b in range(BPB):
                        for half in range(2):
                            for k in range(KC):
                                mm = pe.matmul(m.bank[3][half * 64:half * 64 + 64, b * GD:(b + 1) * GD],
                                               ctxS[:, k, b * SEQ:(b + 1) * SEQ], Wv[:, k, :],
                                               start=(k == 0), stop=(k == KC - 1))
                    mm.then_inc(proj, 1)
                    pe.wait_ge(evac, i * 4 + 4)
                    score(i, i * TPB, 0)
                    for tt in range(TPB):
                        n = i * TPB + tt
                        if tt < TPB - 1:
                            score(i, n + 1, tt + 1)
                        pe.wait_ge(exped, n + 1)
                        for pr in range(2 * C):
                            mm = pe.transpose(m.bank[6 + pr // 4][:, (pr % 4) * P:(pr % 4 + 1) * P],
                                              S[:, tt % 2, 2 * pr:2 * pr + 2, :].rearrange("p a b -> p (a b)"),
                                              m.ident[:, :])
                            if pr % 4 == 3:
                                mm.then_inc(turned, 1)
                        if tt:
                            turn_out(n - 1)
                        pe.wait_ge(pt_ready, 2 * n + 2)
                        for b in range(2):
                            for pr in range(2 * C):
                                mm = pe.matmul(m.bank[0][b * SEQ:(b + 1) * SEQ, pr * 32:pr * 32 + 32],
                                               PT[:, pr, b * SEQ:(b + 1) * SEQ],
                                               Vbd[:, (2 * tt + b) * 2 + pr % 2, :, :].rearrange("p a b -> p (a b)"),
                                               start=True, stop=True)
                        mm.then_inc(mixed, 1)
                        if tt:
                            output(n - 1)
                    turn_out(i * TPB + TPB - 1)
                    output(i * TPB + TPB - 1)


class Router:
    NE = 16

    def __init__(self, m, tag, own, top, shared, scale=1.0):
        self.m, self.top, self.ne, self.scale = m, top, self.NE + shared, scale

        def sb(n, s, dt=F32):
            return m.sb(f"{tag}_{n}", s, dt, own)
        self.route = sb("route", [P, NT, self.ne])
        self.score = sb("score", [P, NT, self.NE])
        self.iota = sb("iota", [P, self.NE])
        self.val = sb("val", [P, NT, 8])
        self.idx = sb("idx", [P, NT, 8], U32)
        self.idxf = sb("idxf", [P, NT, 8])
        self.tot = sb("tot", [P, NT])
        self.oh = sb("oh", [P, NT, self.NE])
        self.wa = sb("wa", [P, KC, self.NE])
        self.wa16 = sb("wa16", [P, 2, KC, self.NE], F16)
        self.logits, self.scored, self.chain, self.done, self.high, self.low = (m.sem(f"{tag}_{n}") for n in (
            "logits", "scored", "rchain", "routed", "wa_high", "wa_low"))

    def tensor(self, pe, bank):
        pe.wait_ge(self.low, 1)
        for t in range(NT):
            mm = split_product(pe, bank[:, t * self.NE:(t + 1) * self.NE],
                               lambda x, k: (self.m.xh, self.m.xl)[x][:, k, t * P:(t + 1) * P],
                               lambda x, k: self.wa16[:, x, k, :])
        mm.then_inc(self.logits, 1)

    def scalar(self, act, bank, wa):
        act.activation(self.wa16[:, 0, :, :].rearrange("p k e -> p (k e)"), wa, ACT.Copy, scale=SPLIT).then_inc(self.high, 1)
        act.wait_ge(self.logits, 1)
        act.activation(self.score[:, :, :].rearrange("p t e -> p (t e)"), bank[:, 0:NT * self.NE],
                       ACT.Sigmoid, scale=UNSPLIT).then_inc(self.scored, 1)

    def vector(self, dve, bias=None):
        c = Chain(dve, self.chain)
        shape = (P, NT, self.NE)
        dve.wait_ge(self.high, 1)
        dve.scalar_tensor_tensor(self.wa16[:, 1, :, :], self.wa[:, :, :], SPLIT, self.wa16[:, 0, :, :],
                                 ALU.mult, ALU.subtract).then_inc(self.low, 1)
        dve.wait_ge(self.scored, 1)
        if bias is not None:
            c.do(dve.tensor_tensor(self.score[:, :, :], self.score[:, :, :],
                                   bias.unsqueeze(1).broadcast_to(shape), ALU.add))
        c.do(dve.memset(self.route[:, :, :], self.scale))
        for t in range(NT):
            last = dve.max(self.val[:, t, :], self.score[:, t, :])
        c.do(last)
        for t in range(NT):
            last = dve.max_index(self.idx[:, t, :], self.val[:, t, :], self.score[:, t, :])
        c.do(last)
        c.do(dve.tensor_copy(self.idxf[:, :, :], self.idx[:, :, :]))
        c.do(dve.tensor_reduce(self.tot[:, :], self.val[:, :, 0:self.top], AX, ALU.add))
        c.do(dve.reciprocal(self.tot[:, :], self.tot[:, :]))
        if self.scale != 1.0:
            c.do(dve.tensor_scalar(self.tot[:, :], self.tot[:, :], self.scale, None, ALU.mult))
        c.do(dve.tensor_tensor(self.val[:, :, :], self.val[:, :, :],
                               self.tot[:, :].unsqueeze(2).broadcast_to((P, NT, 8)), ALU.mult))
        r = self.route[:, :, 0:self.NE]
        for j in range(self.top):
            out = r if j == 0 else self.oh[:, :, :]
            c.do(dve.tensor_tensor(out, self.iota[:, :].unsqueeze(1).broadcast_to(shape),
                                   self.idxf[:, :, j:j + 1].broadcast_to(shape), ALU.is_equal))
            c.do(dve.tensor_tensor(out, out, self.val[:, :, j:j + 1].broadcast_to(shape), ALU.mult))
            if j:
                c.do(dve.tensor_tensor(r, r, self.oh[:, :, :], ALU.add))
        dve.sem_inc(self.done, 1)


def experts_top2(nc, m, w):
    NE, SH, F = 16, 2, 128
    PAIRS = NE // 2
    HS = 256.0
    prepared, high, split, scaled, hhigh, hlow = (m.sem(f"c_{n}") for n in (
        "prepared", "high", "split", "scaled", "hhigh", "hlow"))
    (loaded, w_in0, w_in1, gate_up, gated, hready, downs, summed, routed_T, rt_ready, biased) = (
        m.sem(f"c_{n}") for n in ("loaded", "w0", "w1", "gate_up", "gelu", "h", "downs", "summed", "rT", "rTs", "b2"))
    w_in = (w_in0, w_in1)
    with ExitStack() as own:
        def sb(n, s, dt=F32):
            return m.sb("c_" + n, s, dt, own)

        Wgu = sb("Wgu", [P, 2, KC, 2, F])
        Wx = sb("Wx", [P, 2, 2, KC, 2, F], F16)
        Wd = sb("Wd", [F, 2, D])
        WdH, WdL = (sb(n, [F, 2, D], F16) for n in ("WdH", "WdL"))
        hh, hl = (sb(n, [F, 2, BLK], F16) for n in ("hh", "hl"))
        gb, ub = (sb(n, [F, NE + SH]) for n in ("gb", "ub"))
        b2 = sb("b2", [NE + SH, D])
        gelu = sb("gelu", [F, 2, BLK])
        h = sb("h", [F, 2, BLK])
        rT = sb("rT", [NE + SH, 2, TPB, P])
        R = Router(m, "c", own, 2, SH, 1.0 / (HS * SPLIT))
        src_r = {"Wg": w["L0_ffn_rg"], "Wu": w["L0_ffn_rw1"], "Wd": w["L0_ffn_rw2"]}
        src_s = {"Wg": w["L0_ffn_sg"], "Wu": w["L0_ffn_sw1"], "Wd": w["L0_ffn_sw2"]}
        def bias_bank(q):
            return 2 + 2 * (q % 3)

        def weights(sp, src, e, slot):
            for part, n in enumerate(("Wg", "Wu")):
                sp.dma_start(Wgu[:, slot, :, part, :], src[n][e].rearrange("(k p) f -> p k f", p=P)).then_inc(w_in[slot], 16)
            sp.dma_start(Wd[:, slot, :], src["Wd"][e]).then_inc(w_in[slot], 16)

        def preload(sp):
            def load(dst, src):
                sp.dma_start(dst, src).then_inc(loaded, 16)

            with nc.allow_non_contiguous_dma("biases to partitions"):
                load(R.wa[:, :, :], w["L0_ffn_wa"].rearrange("(k p) e -> p k e", p=P))
                load(R.iota[:, :], w["iota16"].partition_broadcast(P))
                weights(sp, src_r, 0, 0)
                for dst, r, s in ((gb, "rgb", "sgb"), (ub, "rb1", "sb1")):
                    load(dst[:, 0:NE], w["L0_ffn_" + r].rearrange("e f -> f e"))
                    load(dst[:, NE:], w["L0_ffn_" + s].rearrange("e f -> f e"))
                load(b2[0:NE, :], w["L0_ffn_rb2"])
                load(b2[NE:, :], w["L0_ffn_sb2"])
                weights(sp, src_r, 1, 1)

        layernorm(nc, m, preload, add_to_x=True, split=True)
        with nc.Block() as block:
            @block.sync
            def _(sp):
                with sp.Fori(1, PAIRS) as i:
                    for slot in range(2):
                        sp.wait_ge(downs, i * 8 + 4 * (slot + 1))
                        weights(sp, src_r, i * 2 + slot, slot)
                for slot in range(2):
                    sp.wait_ge(downs, PAIRS * 8 + 4 * (slot + 1))
                    weights(sp, src_s, slot, slot)

            @block.gpsimd
            def _(pool):
                def low(e, slot):
                    m.wait_apart(pool, high, e + 1)
                    pool.tensor_tensor(Wx[:, slot, 1], Wgu[:, slot], Wx[:, slot, 0], ALU.subtract)
                    pool.tensor_tensor(WdL[:, slot], Wd[:, slot], WdH[:, slot], ALU.subtract).then_inc(split, 1)

                with pool.Fori(0, PAIRS) as i:
                    for slot in range(2):
                        low(i * 2 + slot, slot)
                for slot in range(2):
                    low(NE + slot, slot)

            @block.scalar
            def _(act):
                def split_high(slot, uses):
                    m.wait_apart(act, w_in[slot], 48 * uses + 48)
                    act.activation(Wgu[:, slot], Wgu[:, slot], ACT.Copy, scale=SPLIT)
                    act.activation(Wd[:, slot], Wd[:, slot], ACT.Copy, scale=SPLIT).then_inc(scaled, 1)
                    m.wait_apart(act, scaled, 2 * uses + slot + 1)
                    act.activation(Wx[:, slot, 0], Wgu[:, slot], ACT.Copy)
                    act.activation(WdH[:, slot], Wd[:, slot], ACT.Copy).then_inc(high, 1)

                split_high(0, 0)
                act.wait_ge(loaded, 16 * 8)
                R.scalar(act, m.bank[0], R.wa[:, :, :].rearrange("p k e -> p (k e)"))
                for q in range(NBLK):
                    act.wait_ge(routed_T, q + 1)
                    act.activation(rT[:, q % 2, :, :].rearrange("p a b -> p (a b)"), m.bank[q % 2][0:NE + SH, :],
                                   ACT.Copy).then_inc(rt_ready, 1)

                def hidden_high(s, sl):
                    m.wait_apart(act, hready, s + 3)
                    act.activation(hh[:, sl, :], h[:, sl, :], ACT.Copy, scale=HS * UNSPLIT).then_inc(hhigh, 1)

                def pair(i, e0, end=False):
                    for st in range(8):
                        slot, q = divmod(st, NBLK)
                        m.wait_apart(act, gate_up, i * 8 + st + 1)
                        act.activation(gelu[:, q % 2, :], m.bank[q % 2][:, :], ACT.Gelu, scale=UNSPLIT,
                                       bias=gb[:, ds(e0 + slot, 1)]).then_inc(gated, 1)
                        hidden_high(i * 8 + st, q % 2)
                        if q == 1 and not (end and slot):
                            split_high(1 - slot, i + slot)


                with act.Fori(0, PAIRS) as i:
                    pair(i, i * 2)
                pair(PAIRS, NE, end=True)

            @block.vector
            def _(dve):
                dve.wait_ge(loaded, 16 * 8)
                for bias, scale in ((ub, SPLIT ** 2), (b2, HS * SPLIT)):
                    dve.tensor_scalar(bias[:, :], bias[:, :], scale, None, ALU.mult).then_inc(prepared, 1)
                dve.wait_ge(prepared, 2)
                R.vector(dve)
                for q in range(NBLK):
                    for half in range(2):
                        dve.wait_ge(biased, 2 * q + half + 1)
                        t = q * TPB + 2 * half
                        x2 = m.X[:, t:t + 2, :].rearrange("p t d -> p (t d)")
                        dve.tensor_tensor(x2, m.bank[bias_bank(q) + half][:, :], x2, ALU.add).then_inc(summed, 1)
                dve.sem_inc(hready, 2)

                def hidden(i, e0, st):
                    slot, q = divmod(st, NBLK)
                    dve.wait_ge(gated, i * 8 + st + 1)
                    dve.scalar_tensor_tensor(h[:, q % 2, :], m.bank[2 + q % 2][:, :], ub[:, ds(e0 + slot, 1)],
                                             gelu[:, q % 2, :], ALU.add, ALU.mult).then_inc(hready, 1)

                def add(i, e0, st):
                    slot, q = divmod(st, NBLK)
                    dve.wait_ge(downs, 8 + i * 8 + st + 1)
                    for j in range(TPB):
                        t = q * TPB + j
                        last = dve.scalar_tensor_tensor(
                            m.X[:, t, :], m.bank[4 + 2 * (q % 2) + j // 2][:, (j % 2) * D:(j % 2 + 1) * D],
                            R.route[:, t, ds(e0 + slot, 1)], m.X[:, t, :], ALU.mult, ALU.add)
                    last.then_inc(summed, 1)

                def low(i, st):
                    dve.wait_ge(hhigh, i * 8 + st + 1)
                    dve.scalar_tensor_tensor(hl[:, st % 2, :], h[:, st % 2, :], HS * UNSPLIT, hh[:, st % 2, :],
                                             ALU.mult, ALU.subtract).then_inc(hlow, 1)

                def pair(i, e0, end=False):
                    for st in range(8):
                        low(i, st)
                        if not (end and st == 7):
                            hidden(i, e0, st + 1)
                        add(i, e0, st)

                hidden(0, 0, 0)
                with dve.Fori(0, PAIRS) as i:
                    pair(i, i * 2)
                pair(PAIRS, NE, end=True)

            @block.tensor
            def _(pe):
                pe.sem_inc(downs, 8)
                pe.wait_ge(loaded, 16 * 8)
                R.tensor(pe, m.bank[0])
                pe.wait_ge(R.done, 1)

                def turn_routes(q):
                    if q >= 2:
                        pe.wait_ge(rt_ready, q - 1)
                    for j in range(TPB):
                        mm = pe.transpose(m.bank[q % 2][0:NE + SH, j * P:(j + 1) * P], R.route[:, q * TPB + j, :], m.ident[:, :])
                    mm.then_inc(routed_T, 1)

                def route_biases(q):
                    pe.wait_ge(rt_ready, q + 1)
                    if q == 3:
                        pe.wait_ge(summed, 2)
                    for j in range(TPB):
                        mm = pe.matmul(m.bank[bias_bank(q) + j // 2][:, (j % 2) * D:(j % 2 + 1) * D], rT[:, q % 2, j, :],
                                       b2[:, :], start=True, stop=True)
                        if j % 2:
                            mm.then_inc(biased, 1)

                for q in range(NBLK):
                    turn_routes(q)
                    if q:
                        route_biases(q - 1)
                route_biases(NBLK - 1)
                pe.wait_ge(summed, 2 * NBLK)

                def gate_and_up(i, st):
                    slot, q = st // NBLK % 2, st % NBLK
                    if q == 0:
                        pe.wait_ge(split, i * 2 + st // NBLK + 1)
                    pe.wait_ge(hready, i * 8 + st + 1)
                    for part in range(2):
                        mm = split_product(pe, m.bank[2 * part + q % 2][:, :], lambda x, k: Wx[:, slot, x, k, part, :],
                                           lambda x, k: (m.xh, m.xl)[x][:, k, q * BLK:(q + 1) * BLK])
                    mm.then_inc(gate_up, 1)

                def down(i, st):
                    slot, q = divmod(st, NBLK)
                    pe.wait_ge(hlow, i * 8 + st + 1)
                    pe.wait_ge(summed, 2 * NBLK - 2 + i * 8 + st + 1)
                    for j in range(TPB):
                        tok = slice(j * P, (j + 1) * P)
                        mm = split_product(pe, m.bank[4 + 2 * (q % 2) + j // 2][:, (j % 2) * D:(j % 2 + 1) * D],
                                           lambda x, k: (hh, hl)[x][:, q % 2, tok], lambda x, k: (WdH, WdL)[x][:, slot, :],
                                           chunks=1)
                    mm.then_inc(downs, 1)

                def pair(i, end=False):
                    for st in range(8):
                        if not (end and st == 7):
                            gate_and_up(i, st + 1)
                        down(i, st)

                gate_and_up(0, 0)
                with pe.Fori(0, PAIRS) as i:
                    pair(i)
                pair(PAIRS, end=True)


def lightning_attention(nc, m, w):
    NH, HD = 16, 128
    Q, K, V, GT = range(4)
    PAIRS = NH // 2
    SPH = NBLK
    SPP = 2 * SPH
    TURN = 2
    (loaded, prep, decays, wload, wturned, wt_ready, proj, evac, scored, masked, mixed, ocopied, squared, yready, outs,
     summed, ssq, sd_ready, chain_s, wt_high, wo_ready) = (m.sem(f"d_{n}") for n in (
        "loaded", "prep", "decays", "wload", "wturned", "wt_ready", "proj", "evac", "scored", "masked", "mixed",
        "ocopied", "squared", "y", "outs", "summed", "ssq", "sd", "chain", "wt_high", "wo"))
    acc_zero = m.sem("d_acc_zero")
    with ExitStack() as own:
        def sb(n, s, dt=F32):
            return m.sb("d_" + n, s, dt, own)

        Wn = sb("Wn", [P, 4, D])
        Won = sb("Won", [P, KC, HD])
        WT = sb("WT", [P, 2, 2, KC, 4, HD], F16)
        WoT = sb("WoT", [HD, 2, D])
        nw = sb("nw", [HD, NH])
        slope = sb("slope", [P, NH])
        rel = sb("rel", [P, P])
        tri = sb("tri", [P, P])
        decay = sb("decay", [P, NH, P])
        qT, kT, gt, vS, oS = (sb(n, [P, 2, BLK]) for n in ("qT", "kT", "gt", "vS", "oS"))
        A = sb("A", [P, TPB, P])
        y = sb("y", [P, BLK])
        sq = sb("sq", [P, BLK])
        SQ = sb("SQ", [P, TOK])
        ACC = sb("ACC", [P, NT, D])
        ones = sb("ones", [P, 1])
        eps = sb("eps", [P, 1])
        sd = sb("sd", [P, NT])
        rstd = sb("rstd", [P, NT])
        NPREP = 4
        def weights(sp, h):
            sp.dma_start(Wn[:, 0:3, :], w["L1_attn_w_qkv"][ds(h * 3 * HD, 3 * HD), :]
                         .rearrange("(m o) f -> o m f", o=HD)).then_inc(wload, 16)
            sp.dma_start(Wn[:, 3, :], w["L1_attn_w_gate"][ds(h * HD, HD), :]).then_inc(wload, 16)
            sp.dma_start(Won[:, :, :], w["L1_attn_w_out"][:, ds(h * HD, HD)]
                         .rearrange("(k p) o -> p k o", p=P)).then_inc(wload, 16)

        def preload(sp):
            def load(dst, src):
                sp.dma_start(dst, src).then_inc(loaded, 16)

            weights(sp, 0)
            load(slope[:, :], w["L1_attn_slope_rate"].rearrange("h a b -> (h a b)").partition_broadcast(P))
            load(rel[:, :], w["rel"])
            load(tri[:, :], w["tri"])
            with nc.allow_non_contiguous_dma("norm_w to partitions"):
                load(nw[:, :], w["L1_attn_norm_w"].rearrange("(h d) -> d h", d=HD))

        layernorm(nc, m, preload, split=True)
        with nc.Block() as block:
            @block.sync
            def _(sp):
                with sp.Fori(1, NH) as h:
                    sp.wait_ge(wturned, h)
                    weights(sp, h)

            @block.gpsimd
            def _(pool):
                pool.memset(SQ[:, :], 0.0).then_inc(squared, 4)
                pool.memset(ACC[:, :, :], 0.0).then_inc(acc_zero, 1)
                with pool.Fori(0, NH) as h:
                    for q in range(SPH):
                        s = h * SPH + q
                        pool.wait_ge(ocopied, s + 2)
                        pool.wait_ge(squared, 2 * s + 4)
                        o = oS[:, q % 2, :]
                        pool.tensor_tensor(sq[:, :], o, o, ALU.mult).then_inc(squared, 1)
                        pool.wait_ge(squared, 2 * s + 5)
                        acc = SQ[:, q * BLK:(q + 1) * BLK]
                        pool.tensor_tensor(acc, acc, sq[:, :], ALU.add).then_inc(squared, 1)

            @block.scalar
            def _(act):
                act.wait_ge(prep, NPREP)
                act.sem_inc(evac, 4)
                act.sem_inc(ocopied, 1)

                def turn(h, slot):
                    m.wait_apart(act, wturned, h + 1)
                    for k in range(KC):
                        act.activation(WT[:, slot, 0, k, :, :].rearrange("p a b -> p (a b)"), m.bank[6 + k][:, :],
                                       ACT.Copy, scale=SPLIT).then_inc(wt_high, 1)
                    act.activation(WoT[:, slot, :], m.bank[4][:, 0:D], ACT.Copy,
                                   scale=nw[:, ds(h, 1)]).then_inc(wo_ready, 1)

                def qkg(s, q, turn_next=None):
                    for n, dst in enumerate((qT, kT, gt)):
                        if n == 2 and turn_next:
                            turn(*turn_next)
                        act.wait_ge(proj, 4 * s + n + 1)
                        if n == 2:
                            ins = act.activation(dst[:, q % 2, :], m.bank[n][:, :], ACT.Tanh, scale=0.5 * UNSPLIT)
                        else:
                            ins = act.activation(dst[:, q % 2, :], m.bank[n][:, :], ACT.Silu, scale=UNSPLIT)
                        ins.then_inc(evac, 1)

                def values(s, q):
                    act.wait_ge(proj, 4 * s + 4)
                    act.activation(vS[:, q % 2, :], m.bank[3][:, :], ACT.Silu, scale=UNSPLIT).then_inc(evac, 1)

                def pair(i, last):
                    for st in range(SPP):
                        u, q = divmod(st, SPH)
                        s, h = i * SPP + st, i * 2 + u
                        end = last and st == SPP - 1
                        if not end:
                            qkg(s + 1, q + 1, (h + 1, 1 - u) if q == TURN and not (last and u == 1) else None)
                        act.wait_ge(squared, 2 * s + 2)
                        act.wait_ge(mixed, s + 1)
                        act.activation(oS[:, q % 2, :], m.bank[5][:, :], ACT.Copy).then_inc(ocopied, 1)
                        if not end:
                            values(s + 1, q + 1)

                turn(0, 0)
                for h in range(NH):
                    act.activation(decay[:, h, :], rel[:, :], ACT.Exp, scale=slope[:, h:h + 1]).then_inc(decays, 1)
                qkg(0, 0)
                values(0, 0)
                with act.Fori(0, PAIRS - 1) as i:
                    pair(i, False)
                pair(PAIRS - 1, True)
                act.wait_ge(ssq, 1)
                act.activation(sd[:, :], m.bank[0][:, 0:NT], ACT.Sqrt, scale=1.0 / (NH * HD),
                               bias=eps[:, :]).then_inc(sd_ready, 1)

            @block.vector
            def _(dve):
                dve.memset(ones[:, :], 1.0).then_inc(prep, 1)
                dve.memset(eps[:, :], 1e-6).then_inc(prep, 1)
                dve.wait_ge(loaded, 16 * 4)
                dve.tensor_scalar(nw[:, :], nw[:, :], 0.5, None, ALU.mult).then_inc(prep, 1)
                dve.tensor_scalar(slope[:, :], slope[:, :], -1.0, None, ALU.mult).then_inc(prep, 1)
                dve.sem_inc(masked, 1)
                dve.sem_inc(summed, 1)

                def turned_low(h):
                    dve.wait_ge(wt_high, KC * h + KC)
                    for k in range(KC):
                        high, low = (WT[:, ds(h % 2, 1), x, k, :, :].rearrange("p s a b -> p (s a b)") for x in range(2))
                        last = dve.scalar_tensor_tensor(low, m.bank[6 + k][:, :], SPLIT, high, ALU.mult, ALU.subtract)
                    last.then_inc(wt_ready, 1)

                def head(h, end):
                    for q in range(SPH):
                        s = h * SPH + q
                        if q == TURN and not end:
                            turned_low(h + 1)
                        dve.wait_ge(scored, s + 1)
                        dve.tensor_tensor(A[:, :, :], m.bank[4][:, :].rearrange("p (a b) -> p a b", a=TPB),
                                          decay[:, ds(h, 1), :].broadcast_to((P, TPB, P)), ALU.mult).then_inc(masked, 1)
                        dve.wait_ge(ocopied, s + 2)
                        dve.wait_ge(evac, 4 + 4 * s + 3)
                        dve.scalar_tensor_tensor(y[:, :], gt[:, q % 2, :], 1.0, oS[:, q % 2, :], ALU.add,
                                                 ALU.mult).then_inc(yready, 1)
                        dve.wait_ge(outs, s + 1)
                        for half in range(2):
                            t = q * TPB + 2 * half
                            a2 = ACC[:, t:t + 2, :].rearrange("p t d -> p (t d)")
                            last = dve.tensor_tensor(a2, m.bank[6 + half][:, :], a2, ALU.add)
                        last.then_inc(summed, 1)

                turned_low(0)
                dve.wait_ge(decays, NH)
                dve.tensor_tensor(decay[:, :, :], decay[:, :, :], tri[:, :].unsqueeze(1).broadcast_to((P, NH, P)),
                                  ALU.mult).then_inc(prep, 1)
                dve.wait_ge(prep, NPREP + 1)
                dve.wait_ge(acc_zero, 1)
                with dve.Fori(0, NH - 1) as h:
                    head(h, False)
                head(NH - 1, True)
                dve.wait_ge(sd_ready, 1)
                dve.reciprocal(rstd[:, :], sd[:, :]).then_inc(chain_s, 1)
                dve.wait_ge(chain_s, 1)
                dve.wait_ge(summed, 1 + NH * SPH)
                for t in range(NT):
                    dve.scalar_tensor_tensor(m.X[:, t, :], ACC[:, t, :], rstd[:, t:t + 1], m.X[:, t, :], ALU.mult, ALU.add)

            @block.tensor
            def _(pe):

                def turn(h):
                    pe.wait_ge(wload, 48 * h + 48)
                    for k in range(KC):
                        for n in range(4):
                            pe.transpose(m.bank[6 + k][:, n * HD:(n + 1) * HD], Wn[:, n, k * P:(k + 1) * P], m.ident[:, :])
                    for k in range(KC):
                        mm = pe.transpose(m.bank[4][:, k * P:(k + 1) * P], Won[:, k, :], m.ident[:, :])
                    mm.then_inc(wturned, 1)

                def wide(s, q, slot, n):
                    b = {Q: 0, K: 1, GT: 2}[n]
                    pe.wait_ge(evac, 4 * s + b + 1)
                    split_product(pe, m.bank[b][:, :], lambda x, k: WT[:, slot, x, k, n, :],
                                  lambda x, k: (m.xh, m.xl)[x][:, k, q * BLK:(q + 1) * BLK]).then_inc(proj, 1)

                def values(s, q, slot):
                    pe.wait_ge(evac, 4 * s + 4)
                    for j in range(TPB):
                        t = q * TPB + j
                        mm = split_product(pe, m.bank[3][:, j * HD:(j + 1) * HD],
                                           lambda x, k: (m.xh, m.xl)[x][:, k, t * P:(t + 1) * P],
                                           lambda x, k: WT[:, slot, x, k, V, :])
                    mm.then_inc(proj, 1)

                def output(s, slot, turned_since, h):
                    pe.wait_ge(yready, s + 1)
                    pe.wait_ge(summed, s + 1)
                    if turned_since:
                        pe.wait_ge(wt_ready, h + 2)
                    for j in range(TPB):
                        mm = pe.matmul(m.bank[6 + j // 2][:, (j % 2) * D:(j % 2 + 1) * D], y[:, j * P:(j + 1) * P],
                                       WoT[:, slot, :], start=True, stop=True)
                    mm.then_inc(outs, 1)

                def pair(i, first, last):
                    for st in range(SPP):
                        u, q = divmod(st, SPH)
                        s, h = i * SPP + st, i * 2 + u
                        end = last and st == SPP - 1
                        nslot, nq = ((st + 1) // SPH) % 2, (q + 1) % SPH
                        turns = q == TURN and not (last and u == 1)

                        def score():
                            pe.wait_ge(evac, 4 + 4 * s + 2)
                            pe.wait_ge(masked, s + 1)
                            if turns:
                                pe.wait_ge(wo_ready, h + 2)
                            for j in range(TPB):
                                tok = slice(j * P, (j + 1) * P)
                                mm = pe.matmul(m.bank[4][:, tok], kT[:, q % 2, tok], qT[:, q % 2, tok], start=True, stop=True)
                            mm.then_inc(scored, 1)

                        def mix():
                            pe.wait_ge(masked, s + 2)
                            pe.wait_ge(evac, 4 + 4 * s + 4)
                            pe.wait_ge(ocopied, s + 1)
                            for j in range(TPB):
                                tok = slice(j * P, (j + 1) * P)
                                mm = pe.matmul(m.bank[5][:, tok], vS[:, q % 2, tok], A[:, j, :], start=True, stop=True)
                            mm.then_inc(mixed, 1)

                        if not end:
                            wide(s + 1, nq, nslot, Q)
                        if not (first and st == 0):
                            output(s - 1, (st - 1) % SPP // SPH, (q - 1) % SPH == TURN and not (last and u == 1), h)
                        if not end:
                            wide(s + 1, nq, nslot, K)
                        if turns:
                            pe.wait_ge(summed, s + 1)
                            pe.wait_ge(masked, s + 1)
                            turn(h + 1)
                            wide(s + 1, nq, nslot, GT)
                            score()
                            values(s + 1, nq, nslot)
                            mix()
                        else:
                            score()
                            if not end:
                                wide(s + 1, nq, nslot, GT)
                            mix()
                            if not end:
                                values(s + 1, nq, nslot)

                turn(0)
                pe.wait_ge(wt_ready, 1)
                pe.wait_ge(wo_ready, 1)
                wide(0, 0, 0, Q)
                wide(0, 0, 0, K)
                wide(0, 0, 0, GT)
                values(0, 0, 0)
                pair(0, True, False)
                with pe.Fori(1, PAIRS - 1) as i:
                    pair(i, False, False)
                pair(PAIRS - 1, False, True)
                output(NH * SPH - 1, 1, False, NH - 1)
                pe.wait_ge(prep, NPREP)
                pe.wait_ge(squared, 4 + 2 * NH * SPH)
                for t in range(NT):
                    mm = pe.matmul(m.bank[0][:, t:t + 1], SQ[:, t * P:(t + 1) * P], ones[:, :], start=True, stop=True)
                mm.then_inc(ssq, 1)


def quantised_attention(nc, m, w):
    H, HD = 16, 16
    PR = H // 2
    U16 = mybir.dt.uint16
    KT = TOK // P
    HALF = TOK // 2
    LN255 = float(np.log(255.0))
    names = "loaded prep copied proj taken packed turned stored".split()
    loaded, prep, copied, proj, taken, packed, turned, stored = (m.sem(f"e_{n}") for n in names)
    chain_s, vmaxed, vall = (m.sem(f"e_{n}") for n in ("chain", "vmax", "vall"))
    q_here, scored, biased, exped, tturned, taken_pt, mixed, normed, chain2 = (m.sem(f"e_{n}") for n in (
        "q_here", "scored", "biased", "exped", "tturned", "taken_pt", "mixed", "normed", "chain2"))
    xb, o_ready, o_turned, ot_ready, outp, added, chain3 = (m.sem(f"e_{n}") for n in (
        "xb", "o", "o_turned", "oT", "outp", "added", "chain3"))
    rounded, chain_k = m.sem("e_rounded"), m.sem("e_chain_k")
    with ExitStack() as own:
        def sb(n, s, dt=F32, ctx=own):
            return m.sb("e_" + n, s, dt, ctx)

        QT = sb("QT", [P, NT * PR, P], BF16)
        KTt = sb("KT", [P, PR, TOK], BF16)
        Vi = sb("Vi", [P, KT, H, HD], BF16)
        sq = sb("sq", [P, NT * H])
        nsq = sb("nsq", [P, NT * H])
        sv = sb("sv", [P, D])
        identb = sb("identb", [P, P], BF16)
        bp = sb("bp", [P, D])
        Wp = sb("Wp", [P, KC, D])
        with ExitStack() as first:
            def sb1(n, s, dt=F32):
                return m.sb("e_" + n, s, dt, first)

            Wq = sb1("Wq", [P, KC, D])
            Wkv = sb1("Wkv", [P, KC, 2, D])
            bias = sb1("bias", [P, 3, D])
            xs, cs = (sb1(n, [P, 2, KC, BLK]) for n in ("xs", "cs"))
            V32 = sb1("V32", [P, NT, D])
            z = sb1("z", [P, 2, H, HD])
            am, rs = (sb1(n, [P, 2, H]) for n in ("am", "rs"))
            s_ = sb1("s", [P, 2, 2, H])
            k32, r32 = sb1("k32", [P, 2, H, HD]), sb1("r32", [P, H, HD])
            Tq, Tk = (sb1(n, [P, 2, H, 4, HD], BF16) for n in ("Tq", "Tk"))
            vm = sb1("vm", [P, D])
            def preload(sp):
                def load(dst, src):
                    sp.dma_start(dst, src).then_inc(loaded, 16)
                load(Wq[:, :, :], w["L1_xattn_Wq"].rearrange("(k p) n -> p k n", p=P))
                load(Wkv[:, :, :, :].rearrange("p k a n -> p k (a n)"), w["L1_xattn_Wkv"].rearrange("(k p) n -> p k n", p=P))
                load(Wp[:, :, :], w["L1_xattn_Wp"].rearrange("(k p) n -> p k n", p=P))
                load(bias[:, 0, :], w["L1_xattn_bq"].partition_broadcast(P))
                load(bias[:, 1:3, :].rearrange("p a n -> p (a n)"), w["L1_xattn_bkv"].partition_broadcast(P))
                load(bp[:, :], w["L1_xattn_bp"].partition_broadcast(P))

            layernorm(nc, m, preload)
            with nc.Block() as block:
                @block.gpsimd
                def _(pool):
                    with pool.Fori(0, NBLK) as i:
                        c = Chain(pool, chain_k, m)
                        c.enter(i, 4 * TPB)
                        for tt in range(TPB):
                            sl = tt % 2
                            k = k32[:, sl, :, :]
                            m.wait_apart(pool, rounded, i * TPB + tt + 1)
                            c.do(pool.tensor_tensor(k, k, s_[:, sl, 1, :].unsqueeze(2).broadcast_to((P, H, HD)), ALU.mult))
                            c.do(pool.tensor_copy(Tk[:, sl, :, 0, :], k))
                            c.do(pool.tensor_tensor(r32[:, :, :], k, Tk[:, sl, :, 0, :], ALU.subtract))
                            c.do(pool.tensor_copy(Tk[:, sl, :, 1, :], r32[:, :, :]))
                            pool.tensor_tensor(Tk[:, sl, :, 2, :], r32[:, :, :], Tk[:, sl, :, 1, :],
                                               ALU.subtract).then_inc(packed, 1)
                    pool.wait_ge(vmaxed, 1)
                    pool.partition_all_reduce(sv[:, :], vm[:, :], P, bass.bass_isa.ReduceOp.max).then_inc(vall, 1)
                    pool.tensor_tensor(m.X[:, :, :], m.X[:, :, :], bp[:, :].unsqueeze(1).broadcast_to((P, NT, D)),
                                       ALU.add).then_inc(xb, 1)

                @block.scalar
                def _(act):
                    act.sem_inc(stored, 2)

                    def copies(b, slot):
                        act.activation(xs[:, slot, :, :], m.xnT[:, :, ds(b * BLK, BLK)], ACT.Copy).then_inc(copied, 1)
                        act.activation(cs[:, slot, :, :], m.ctxT[:, :, ds(b * BLK, BLK)], ACT.Copy).then_inc(copied, 1)

                    copies(0, 0)
                    with act.Fori(0, NBLK // 2) as i:
                        for tt in range(2 * TPB):
                            if tt % TPB == 0:
                                b = i * 2 + tt // TPB
                                act.wait_ge(proj, b * TPB + 1)
                                copies((b + 1) % NBLK, (tt // TPB + 1) % 2)
                            t = i * 2 * TPB + tt
                            m.wait_apart(act, turned, t + 3)
                            b = 4 + 2 * (tt % 2)
                            act.activation(QT[:, ds(t * PR, PR), :].rearrange("p a b -> p (a b)"),
                                           m.bank[b].bitcast(BF16), ACT.Copy)
                            act.activation(KTt[:, :, ds(t * P, P)], m.bank[b + 1].bitcast(BF16)
                                           .rearrange("p (a b) -> p a b", a=PR), ACT.Copy).then_inc(stored, 1)

                @block.vector
                def _(dve):
                    dve.tensor_copy(identb[:, :], m.ident[:, :]).then_inc(prep, 1)
                    dve.memset(Tq[:, :, :, :, :].rearrange("p a b c d -> p (a b c d)"), 0.0).then_inc(prep, 1)
                    dve.memset(Tk[:, :, :, :, :].rearrange("p a b c d -> p (a b c d)"), 0.0).then_inc(prep, 1)
                    dve.wait_ge(loaded, 16 * 6)
                    dve.tensor_scalar(bias[:, 0, :], bias[:, 0, :], HD ** -0.5, None, ALU.mult).then_inc(prep, 1)
                    dve.wait_ge(prep, 4)
                    dve.sem_inc(taken, 2)
                    STEPS = 5
                    with dve.Fori(0, NBLK) as i:
                        c = Chain(dve, chain_s)
                        c.enter(i, STEPS * TPB)
                        for tt in range(TPB):
                            t = i * TPB + tt
                            sl = tt % 2
                            dve.wait_ge(proj, t + 2)
                            A, B = m.bank[sl], m.bank[2 + sl]
                            for n, sc in ((0, HD ** -0.5), (1, 1.0)):
                                last = dve.scalar_tensor_tensor(z[:, n, :, :].rearrange("p h d -> p (h d)"),
                                                                A[:, n * D:(n + 1) * D], sc, bias[:, n, :], ALU.mult, ALU.add)
                            c.do(last)
                            dve.tensor_tensor(V32[:, t, :], B[:, 0:D], bias[:, 2, :], ALU.add).then_inc(taken, 1)
                            zf = z[:, :, :, :].rearrange("p a h d -> p (a h) d")
                            amf, sf, rf = (x.rearrange("p a h -> p (a h)") for x in (am[:, :, :], s_[:, sl, :, :], rs[:, :, :]))
                            c.do(dve.tensor_reduce(amf, zf, AX, ALU.max, apply_absolute_value=True))
                            dve.wait_ge(turned, t + 1)
                            c.do(dve.tensor_scalar(sf, amf, 1.0 / 127.0, 1e-8, ALU.mult, ALU.max))
                            dve.tensor_copy(sq[:, ds(t * H, H)], s_[:, sl, 0, :])
                            c.do(dve.reciprocal(rf, sf))
                            c.do(dve.tensor_tensor(zf, zf, rf.unsqueeze(2).broadcast_to((P, 2 * H, HD)), ALU.mult))
                            for cp in range(3):
                                dve.tensor_scalar(Tq[:, sl, :, cp, :], z[:, 0, :, :], MAGIC, MAGIC, ALU.add, ALU.subtract)
                            dve.tensor_scalar(k32[:, sl, :, :], z[:, 1, :, :], MAGIC, MAGIC, ALU.add,
                                              ALU.subtract).then_inc(rounded, 1)
                            dve.wait_ge(rounded, t + 1)
                        assert c.n == STEPS * TPB, c.n
                    c = Chain(dve, chain2)
                    dve.wait_ge(taken, 2 + NT)
                    dve.tensor_reduce(vm[:, :], V32[:, :, :].rearrange("p t c -> p c t"), AX, ALU.max,
                                      apply_absolute_value=True).then_inc(vmaxed, 1)
                    c.do(dve.tensor_scalar(nsq[:, :], sq[:, :], -1.0, None, ALU.mult))
                    dve.wait_ge(vall, 1)
                    c.do(dve.tensor_scalar(sv[:, :], sv[:, :], 1.0 / 127.0, 1e-8, ALU.mult, ALU.max))
                    c.do(dve.reciprocal(vm[:, :], sv[:, :]))
                    c.do(dve.tensor_tensor(V32[:, :, :], V32[:, :, :], vm[:, :].unsqueeze(1).broadcast_to((P, NT, D)), ALU.mult))
                    c.do(dve.tensor_scalar(Vi[:, :, :, :].rearrange("p t h d -> p (t h d)"),
                                           V32[:, :, :].rearrange("p t c -> p (t c)"), MAGIC, MAGIC, ALU.add, ALU.subtract))

                @block.tensor
                def _(pe):
                    pe.sem_inc(proj, 1)
                    pe.sem_inc(turned, 2)
                    pe.wait_ge(prep, 4)

                    def project(i, tt):
                        t = i * 2 * TPB + tt
                        sl, blk = tt % 2, tt // TPB
                        tok = slice(tt % TPB * P, (tt % TPB + 1) * P)
                        if tt % TPB == 0:
                            pe.wait_ge(copied, 2 * (i * 2 + blk) + 2)
                        pe.wait_ge(taken, t + 1)
                        for out, src, W in ((m.bank[sl][:, 0:D], xs, lambda k: Wq[:, k, :]),
                                            (m.bank[sl][:, D:], cs, lambda k: Wkv[:, k, 0, :]),
                                            (m.bank[2 + sl][:, 0:D], cs, lambda k: Wkv[:, k, 1, :])):
                            for k in range(KC):
                                mm = pe.matmul(out, src[:, blk, k, tok], W(k), start=(k == 0), stop=(k == KC - 1))
                        mm.then_inc(proj, 1)

                    with pe.Fori(0, NBLK // 2) as i:
                        project(i, 0)
                        for tt in range(2 * TPB):
                            t = i * 2 * TPB + tt
                            sl = tt % 2
                            if tt < 2 * TPB - 1:
                                project(i, tt + 1)
                            pe.wait_ge(packed, t + 1)
                            pe.wait_ge(stored, t + 1)
                            for src, b in ((Tq, 4 + 2 * sl), (Tk, 5 + 2 * sl)):
                                for pr in range(PR):
                                    mm = pe.transpose(m.bank[b].bitcast(BF16)[:, pr * P:(pr + 1) * P],
                                                      src[:, sl, 2 * pr:2 * pr + 2, :, :].rearrange("p h c d -> p (h c d)"),
                                                      identb[:, :])
                            mm.then_inc(turned, 1)

        N = NT * H
        Qs = sb("Qs", [P, 4, P], BF16)
        e16 = sb("e16", [P, 2, TOK], U16)
        PT = sb("PT", [P, 2, KT // 2, P], BF16)
        mx = sb("mx", [P, 2, 5])
        ebias = sb("ebias", [P, 2])
        esum = sb("esum", [P, 4, N])
        Osb = sb("Osb", [P, NT, D])
        RING = 6
        SC = 4 * 8
        turn_bank, out_bank = m.bank[RING].bitcast(BF16), m.bank[RING + 1]

        def ring(j, b):
            return m.bank[(4 * j + b) % RING]

        def loop(eng, step):
            def tile(t):
                for j in range(H):
                    step(t * H + j, j, t)
            tile(0)
            with eng.Fori(1, NT - 1) as i:
                tile(i)
            tile(NT - 1)

        def first(n):
            return isinstance(n, int) and n == 0

        def beyond(n):
            return isinstance(n, int) and n >= N

        with nc.Block() as block:
            @block.gpsimd
            def _(pool):
                with pool.Fori(0, NT) as i:
                    for jp in range(PR):
                        pair = i * PR + jp
                        m.wait_apart(pool, scored, 8 * pair + 8)
                        pool.tensor_copy(Qs[:, jp % 4, :],
                                         QT[:, ds(pair, 1), :].rearrange("p a b -> p (a b)")).then_inc(q_here, 1)

            @block.tensor
            def _(pe):
                pe.sem_inc(scored, SC)

                def score(n, j, *quarters):
                    if beyond(n):
                        return
                    j %= H
                    rows = slice(64 * (j % 2), 64 * (j % 2) + 48)
                    for b in quarters:
                        tile_start = j == 0 and not first(n)
                        m.wait_apart(pe, exped, 4 * n + b + (RING - 3 if tile_start else 1))
                        if b == 0 and j % 2 == 0:
                            m.wait_apart(pe, q_here, (n // 2) + 1)
                        pe.matmul(ring(j, b), Qs[rows, j // 2 % 4, :], KTt[rows, j // 2, b * BLK:(b + 1) * BLK],
                                  start=True, stop=True).then_inc(scored, 1)

                def turn(n, j, hf):
                    m.wait_apart(pe, exped, RING + 4 * n + 2 * hf + 2)
                    m.wait_apart(pe, taken_pt, 2 * n + hf + 1)
                    for k in range(KT // 2):
                        col = hf * HALF + k * P
                        mm = pe.transpose(turn_bank[:, k * P:(k + 1) * P], e16[:, j % 2, col:col + P].bitcast(BF16), identb[:, :])
                    mm.then_inc(tturned, 1)

                def mix(n, j, t, hf):
                    m.wait_apart(pe, taken_pt, 2 * n + hf + 2)
                    if j == 0 and hf == 0:
                        m.wait_apart(pe, normed, t + 1)
                    for k in range(KT // 2):
                        kt = hf * (KT // 2) + k
                        mm = pe.matmul(out_bank[:, j * HD:(j + 1) * HD], PT[:, hf, k, :], Vi[:, kt, j, :],
                                       start=(kt == 0), stop=(kt == KT - 1))
                    if hf and j == H - 1:
                        mm.then_inc(mixed, 1)

                score(0, 0, 0, 1, 2, 3)
                score(1, 1, 0, 1)

                def step(n, j, t):
                    score(n + 1, j + 1, 2, 3)
                    turn(n, j, 0)
                    if not first(n):
                        mix(n - 1, (j - 1) % H, t, 1)
                    score(n + 2, j + 2, 0, 1)
                    turn(n, j, 1)
                    mix(n, j, t, 0)
                loop(pe, step)
                mix(N - 1, H - 1, NT - 1, 1)

            @block.vector
            def _(dve):
                dve.sem_inc(normed, 1)
                dve.sem_inc(taken_pt, 1)

                def maxima(n, j, *quarters):
                    if beyond(n):
                        return
                    j %= H
                    for b in quarters:
                        dve.wait_ge(scored, SC + 4 * n + b + 1)
                        red = dve.tensor_reduce(mx[:, j % 2, b:b + 1], ring(j, b), AX, ALU.max)
                    if b == 3:
                        c = Chain(dve, chain3)
                        c.base = 2 * n
                        c.do(red)
                        c.do(dve.tensor_reduce(mx[:, j % 2, 4:5], mx[:, j % 2, 0:4], AX, ALU.max))
                        dve.tensor_scalar(ebias[:, j % 2:j % 2 + 1], mx[:, j % 2, 4:5], nsq[:, ds(n, 1)], LN255,
                                          ALU.mult, ALU.add).then_inc(biased, 1)

                def take(n, hf):
                    dve.wait_ge(tturned, 2 * n + hf + 1)
                    dve.tensor_copy(PT[:, hf, :, :].rearrange("p a b -> p (a b)"),
                                    turn_bank.bitcast(U16)).then_inc(taken_pt, 1)

                def output(t):
                    dve.wait_ge(mixed, t + 1)
                    dve.tensor_copy(Osb[:, ds(t, 1), :].rearrange("p a b -> p (a b)"), out_bank[:, 0:D]).then_inc(normed, 1)

                def step(n, j, t):
                    maxima(n + 1, j + 1, 2, 3)
                    take(n, 0)
                    maxima(n + 2, j + 2, 0, 1)
                    if j == 0 and not first(n):
                        output(t - 1)
                    take(n, 1)
                maxima(0, 0, 0, 1, 2, 3)
                maxima(1, 1, 0, 1)
                loop(dve, step)
                output(NT - 1)

            @block.scalar
            def _(act):
                act.sem_inc(exped, RING)

                def step(n, j, t):
                    m.wait_apart(act, biased, n + 1)
                    for b in range(4):
                        act.activation(e16[:, j % 2, b * BLK:(b + 1) * BLK], ring(j, b), ACT.Exp, bias=ebias[:, j % 2:j % 2 + 1],
                                       scale=sq[:, ds(n, 1)], accum_out=esum[:, b, ds(n, 1)]).then_inc(exped, 1)
                loop(act, step)

        rsum = sb("rsum", [P, N])
        on = sb("on", [P, TPB, H, HD])
        onT = sb("onT", [P, KC, BLK])
        with nc.Block() as block:
            @block.vector
            def _(dve):
                c = Chain(dve, o_ready)
                c.do(dve.tensor_reduce(rsum[:, :], esum[:, :, :].rearrange("p b n -> p n b"), AX, ALU.add))
                c.do(dve.reciprocal(rsum[:, :], rsum[:, :]))
                dve.sem_inc(outp, 1)
                with dve.Fori(0, NBLK) as i:
                    nn = TPB * H
                    dve.wait_ge(o_turned, KC * i + 1)
                    of = on[:, :, :, :].rearrange("p t h d -> p (t h) d")
                    dve.tensor_tensor(on[:, :, :, :].rearrange("p t h d -> p t (h d)"),
                                      Osb[:, ds(i * TPB, TPB), :],
                                      sv[:, :].unsqueeze(1).broadcast_to((P, TPB, D)), ALU.mult).then_inc(o_ready, 1)
                    dve.wait_ge(o_ready, 2 + 2 * i + 1)
                    dve.tensor_tensor(of, of, rsum[:, ds(i * nn, nn)].unsqueeze(2).broadcast_to((P, nn, HD)),
                                      ALU.mult).then_inc(o_ready, 1)
                    for half in range(2):
                        dve.wait_ge(outp, i * 2 + half + 2)
                        x2 = m.X[:, ds(i * TPB + 2 * half, 2), :].rearrange("p t d -> p (t d)")
                        dve.tensor_tensor(x2, m.bank[2 + half], x2, ALU.add).then_inc(added, 1)

            @block.scalar
            def _(act):
                with act.Fori(0, NBLK) as i:
                    for k in range(KC):
                        act.wait_ge(o_turned, KC * i + k + 2)
                        act.activation(onT[:, k, :], m.bank[k], ACT.Copy).then_inc(ot_ready, 1)

            @block.tensor
            def _(pe):
                pe.sem_inc(o_turned, 1)
                with pe.Fori(0, NBLK) as i:
                    pe.wait_ge(o_ready, 2 + 2 * i + 2)
                    for k in range(KC):
                        for j in range(TPB):
                            mm = pe.transpose(m.bank[k][:, j * P:(j + 1) * P],
                                              on[:, j, k * H // 2:(k + 1) * H // 2, :].rearrange("p h d -> p (h d)"), m.ident[:, :])
                        mm.then_inc(o_turned, 1)
                    pe.wait_ge(ot_ready, KC * i + KC)
                    for j in range(TPB):
                        for k in range(KC):
                            mm = pe.matmul(m.bank[2 + j // 2][:, (j % 2) * D:(j % 2 + 1) * D], onT[:, k, j * P:(j + 1) * P],
                                           Wp[:, k, :], start=(k == 0), stop=(k == KC - 1))
                        if j % 2:
                            mm.then_inc(outp, 1)


def experts_top4(nc, m, w, out):
    NE, F, FB = 16, 176, 48
    PAIRS = NE // 2
    UPPER = slice(64, 64 + FB)
    HS = 256.0
    names = "loaded gate_w w0 w1 padded scaled high split up copied product h hh hready downs summed"
    (loaded, gate_turned, w_in0, w_in1, padded, scaled, high, split, up, copied, product, hmade, hhigh, hready,
     downs, summed) = (
        m.sem(f"f_{n}") for n in names.split())
    w_in = (w_in0, w_in1)
    stored = m.sem("f_stored")
    with ExitStack() as own:
        def sb(n, s, dt=F32):
            return m.sb("f_" + n, s, dt, own)

        gw, gb = sb("gw", [NE, D]), sb("gb", [P, NE])
        W13 = sb("W13", [P, 2, KC, 2, F])
        WA = sb("WA", [P, 2, 2, KC, 2, P], F16)
        WB = sb("WB", [P, 2, 2, KC, 2, 64], F16)
        W2 = sb("W2", [P, 2, 2, D])
        W2H, W2L = (sb(n, [P, 2, 2, D], F16) for n in ("W2H", "W2L"))
        h1, pr, h = (sb(n, [P, 2, 2, BLK]) for n in ("h1", "pr", "h"))
        hh = sb("hh", [P, 2, 2, BLK], F16)
        hl = sb("hl", [P, 2, BLK], F16)
        R = Router(m, "f", own, 4, 1, 1.0 / (HS * SPLIT))
        routed = [w[f"L1_ffn_w{n}_routed"] for n in (1, 3, 2)]

        def weights(sp, w1, w3, w2, slot):
            for n, src in enumerate((w1, w3)):
                sp.dma_start(W13[:, slot, :, n, :], src.rearrange("(k p) f -> p k f", p=P)).then_inc(w_in[slot], 16)
            sp.dma_start(W2[:, slot, 0, :], w2[0:P, :]).then_inc(w_in[slot], 16)
            for rows in (slice(0, FB), UPPER):
                sp.dma_start(W2[rows, slot, 1, :], w2[P:F, :]).then_inc(w_in[slot], 16)

        def preload(sp):
            sp.dma_start(gw[:, :], w["L1_ffn_gate_w"]).then_inc(loaded, 16)
            sp.dma_start(gb[:, :], w["L1_ffn_gate_b"].partition_broadcast(P)).then_inc(loaded, 16)
            sp.dma_start(R.iota[:, :], w["iota16"].partition_broadcast(P)).then_inc(loaded, 16)
            sp.wait_ge(padded, 1)
            for slot in range(2):
                weights(sp, *(r[slot] for r in routed), slot)

        with nc.Block() as block:
            @block.gpsimd
            def _(pool):
                pool.memset(W2[:, :, :, :], 0.0).then_inc(padded, 1)

        layernorm(nc, m, preload, split=True)
        with nc.Block() as block:
            @block.sync
            def _(sp):
                with sp.Fori(1, PAIRS) as i:
                    for slot in range(2):
                        sp.wait_ge(downs, i * 8 + 4 * (slot + 1))
                        weights(sp, *(r[i * 2 + slot] for r in routed), slot)
                sp.wait_ge(downs, PAIRS * 8 + 4)
                weights(sp, *(w[f"L1_ffn_w{n}_shared"] for n in (1, 3, 2)), 0)
                for q in range(NBLK):
                    sp.wait_ge(summed, 2 + PAIRS * 8 + q + 1)
                    sp.dma_start(out.rearrange("(t p) d -> p t d", p=P)[:, q * TPB:(q + 1) * TPB, :],
                                 m.X[:, q * TPB:(q + 1) * TPB, :]).then_inc(stored, 16)
                sp.wait_ge(stored, 16 * NBLK)

            def parts(slot, x):
                return ((WA[:, slot, x], W13[:, slot, :, :, 0:P]), (WB[:, slot, x, :, :, 0:FB], W13[:, slot, :, :, P:F]))

            @block.gpsimd
            def _(pool):
                pool.memset(WB[:, :, :, :, :, :], 0.0).then_inc(padded, 1)
                pool.memset(hh[:, :, :, :], 0.0).then_inc(padded, 1)

                def low(e, slot):
                    m.wait_apart(pool, high, e + 1)
                    for (lo, src), (hi, _) in zip(parts(slot, 1), parts(slot, 0)):
                        pool.tensor_tensor(lo, src, hi, ALU.subtract)
                    pool.tensor_tensor(W2L[:, slot], W2[:, slot], W2H[:, slot], ALU.subtract).then_inc(split, 1)

                pool.wait_ge(padded, 3)
                with pool.Fori(0, PAIRS) as i:
                    for slot in range(2):
                        low(i * 2 + slot, slot)
                low(NE, 0)

            @block.scalar
            def _(act):
                def split_high(slot, uses):
                    act.wait_ge(w_in[slot], 80 * uses + 80)
                    act.activation(W13[:, slot], W13[:, slot], ACT.Copy, scale=SPLIT)
                    act.activation(W2[:, slot], W2[:, slot], ACT.Copy, scale=SPLIT).then_inc(scaled, 1)
                    m.wait_apart(act, scaled, 2 * uses + slot + 1)
                    for hi, src in parts(slot, 0):
                        act.activation(hi, src, ACT.Copy)
                    act.activation(W2H[:, slot], W2[:, slot], ACT.Copy).then_inc(high, 1)

                act.wait_ge(padded, 3)
                split_high(0, 0)
                act.wait_ge(gate_turned, 1)
                act.activation(R.wa[:, :, :].rearrange("p k e -> p (k e)"), m.bank[1][:, 0:KC * NE], ACT.Copy)
                R.scalar(act, m.bank[3], m.bank[1][:, 0:KC * NE])

                def steps(i, n, first, second):
                    for st in range(n):
                        slot, q = divmod(st, NBLK)
                        s = 2 * (i * 8 + st)
                        act.wait_ge(up, i * 8 + st + 1)
                        act.activation(h1[:, q % 2, 0, :], m.bank[0][:, :], first, scale=UNSPLIT).then_inc(copied, 1)
                        act.activation(h1[UPPER, q % 2, 1, :], m.bank[2][0:FB, :], first, scale=UNSPLIT).then_inc(copied, 1)
                        act.wait_ge(product, s + 3)
                        act.activation(h[:, q % 2, 0, :], pr[:, q % 2, 0, :], second, scale=UNSPLIT).then_inc(hmade, 1)
                        act.wait_ge(product, s + 4)
                        act.activation(h[0:FB, q % 2, 1, :], pr[UPPER, q % 2, 1, :], second, scale=UNSPLIT).then_inc(hmade, 1)
                        for part, rows in enumerate((slice(0, P), slice(0, FB))):
                            act.wait_ge(hmade, s + part + 1)
                            act.activation(hh[rows, q % 2, part, :], h[rows, q % 2, part, :], ACT.Copy,
                                           scale=HS).then_inc(hhigh, 1)
                        if q == 1 and n == 8:
                            split_high(1 - slot, i + slot)

                with act.Fori(0, PAIRS) as i:
                    steps(i, 8, ACT.Copy, ACT.Silu)
                steps(PAIRS, 4, ACT.Silu, ACT.Copy)

            @block.vector
            def _(dve):
                dve.wait_ge(loaded, 16 * 3)
                R.vector(dve, gb[:, :])
                dve.sem_inc(product, 2)
                dve.sem_inc(summed, 2)

                def multiply(i, st):
                    s = 2 * (i * 8 + st)
                    dve.wait_ge(copied, s + 1)
                    dve.tensor_tensor(pr[:, st % 2, 0, :], m.bank[1][:, :], h1[:, st % 2, 0, :], ALU.mult).then_inc(product, 1)
                    dve.wait_ge(copied, s + 2)
                    dve.tensor_tensor(pr[UPPER, st % 2, 1, :], m.bank[2][UPPER, :], h1[UPPER, st % 2, 1, :],
                                      ALU.mult).then_inc(product, 1)

                def add(i, e, st):
                    q = st % NBLK
                    dve.wait_ge(downs, 8 + i * 8 + st + 1)
                    for j in range(TPB):
                        t = q * TPB + j
                        last = dve.scalar_tensor_tensor(
                            m.X[:, t, :], m.bank[4 + 2 * (q % 2) + j // 2][:, (j % 2) * D:(j % 2 + 1) * D],
                            R.route[:, t, ds(e, 1)], m.X[:, t, :], ALU.mult, ALU.add)
                    last.then_inc(summed, 1)

                def low(i, st):
                    s, sl = 2 * (i * 8 + st), st % 2
                    dve.wait_ge(hhigh, s + 1)
                    dve.scalar_tensor_tensor(hl[:, sl, :], h[:, sl, 0, :], HS, hh[:, sl, 0, :],
                                             ALU.mult, ALU.subtract).then_inc(hready, 1)
                    dve.wait_ge(hhigh, s + 2)
                    dve.scalar_tensor_tensor(hh[UPPER, sl, 1, :], h[0:FB, sl, 1, :], HS, hh[0:FB, sl, 1, :],
                                             ALU.mult, ALU.subtract).then_inc(hready, 1)

                def steps(i, n, e0):
                    for st in range(n):
                        low(i, st)
                        if n == 8 or st < n - 1:
                            multiply(i, st + 1)
                        add(i, e0 + st // NBLK, st)

                multiply(0, 0)
                with dve.Fori(0, PAIRS) as i:
                    steps(i, 8, i * 2)
                steps(PAIRS, 4, NE)

            @block.tensor
            def _(pe):
                pe.sem_inc(downs, 8)
                pe.wait_ge(loaded, 16 * 3)
                for k in range(KC):
                    mm = pe.transpose(m.bank[1][:, k * NE:(k + 1) * NE], gw[:, k * P:(k + 1) * P], m.ident[0:NE, 0:NE])
                mm.then_inc(gate_turned, 1)
                R.tensor(pe, m.bank[3])

                def hidden(i, st):
                    slot, q = st // NBLK % 2, st % NBLK
                    if q == 0:
                        pe.wait_ge(split, i * 2 + st // NBLK + 1)
                    pe.wait_ge(product, 2 * (i * 8 + st) + 2)
                    tok = slice(q * BLK, (q + 1) * BLK)
                    for bank, W in ((0, lambda x, k: WA[:, slot, x, k, 0, :]), (1, lambda x, k: WA[:, slot, x, k, 1, :]),
                                    (2, lambda x, k: WB[:, slot, x, k, :, :].rearrange("p a b -> p (a b)"))):
                        mm = split_product(pe, m.bank[bank][:, :], W, lambda x, k: (m.xh, m.xl)[x][:, k, tok])
                    mm.then_inc(up, 1)

                def down(i, st):
                    slot, q = divmod(st, NBLK)
                    pe.wait_ge(hready, 2 * (i * 8 + st) + 2)
                    pe.wait_ge(summed, i * 8 + st + 1)
                    for j in range(TPB):
                        tok = slice(j * P, (j + 1) * P)
                        terms = ((hh[:, q % 2, 0, tok], W2H[:, slot, 0, :]), (hh[:, q % 2, 0, tok], W2L[:, slot, 0, :]),
                                 (hl[:, q % 2, tok], W2H[:, slot, 0, :]), (hh[:, q % 2, 1, tok], W2H[:, slot, 1, :]),
                                 (hh[0:FB, q % 2, 1, tok], W2L[0:FB, slot, 1, :]))
                        for n, (a, b) in enumerate(terms):
                            mm = pe.matmul(m.bank[4 + 2 * (q % 2) + j // 2][:, (j % 2) * D:(j % 2 + 1) * D], a, b,
                                           start=(n == 0), stop=(n == len(terms) - 1))
                    mm.then_inc(downs, 1)

                def steps(i, n):
                    for st in range(n):
                        if n == 8 or st < n - 1:
                            hidden(i, st + 1)
                        down(i, st)

                hidden(0, 0)
                with pe.Fori(0, PAIRS) as i:
                    steps(i, 8)
                steps(PAIRS, 4)


def constants():
    J, M, HU = 32, 96, 3
    inv_freq = (1.0 / 10000.0 ** (np.arange(0, 64, 2, dtype=np.float32) / np.float32(64))).astype(np.float32)
    col = np.tile(inv_freq, HU)
    head = np.arange(M) // J
    slopes = (np.float32(2.0 ** -0.5) ** np.arange(1, 17, dtype=np.float32)).reshape(4, 4).T
    q, k = np.arange(P) % SEQ, np.arange(SEQ)
    rel = (k[None, :] - q[:, None]).astype(np.float32)
    row = np.arange(P)
    ahead = ((row[None, :] - row[:, None])).astype(np.float32)
    same = (row[None, :] // SEQ == row[:, None] // SEQ) & (ahead >= 0)
    return {
        "rel": np.where(same, ahead, 0).astype(np.float32),
        "tri": same.astype(np.float32),
        "alibi": (slopes.reshape(1, 16, 1) * rel[:, None, :]).astype(np.float32).reshape(P, 16 * SEQ),
        "gmask": ((row[:, None] % 64) // 16 == np.arange(4)).astype(np.float32),
        "hmask": (row[:, None] // 64 == np.arange(2)).astype(np.float32),
        "iota16": np.arange(16, dtype=np.float32),
        "ident": np.eye(P, dtype=np.float32),
        "freq": np.stack([col, -col], 1).astype(np.float32),
        "mean_w": ((head[:, None] == head[None, :]) / np.float32(64 * 4)).astype(np.float32),
    }


def build(nc, w, out):
    with ExitStack() as ctx:
        m = Mem(nc, ctx)
        x_ready = m.sem("x_ready")
        load_inputs(nc, m, w["x"], w["ctx_2048"], w["ident"], x_ready)
        own = {k[len("L0_attn_"):]: v for k, v in w.items() if k.startswith("L0_attn_")}
        rotary_recurrence(nc, m, {**own, "freq": w["freq"], "mean_w": w["mean_w"]})
        gqa_cross_attention(nc, m, w)
        experts_top2(nc, m, w)
        lightning_attention(nc, m, w)
        quantised_attention(nc, m, w)
        experts_top4(nc, m, w, out)


def kernel(**inputs):
    import concourse.bacc as bacc
    from concourse.bass_utils import run_bass_kernel_spmd

    nc = bacc.Bacc("TRN2", target_bir_lowering=False, num_devices=1)
    arrays = {k: np.ascontiguousarray(v) for k, v in inputs.items()}
    for name in ("x", "ctx_2048"):
        arrays[name] = arrays[name].reshape(TOK, D)
    arrays.update(constants())
    arrays["mask_BxS2_bf1"] = arrays["mask_BxS2_bf1"].view(np.uint8)
    aps = {k: nc.dram_tensor("in_" + k, a.shape, mybir.dt.from_np(a.dtype), kind="ExternalInput").ap()
           for k, a in arrays.items()}
    out = nc.dram_tensor("out_0", (TOK, D), F32, kind="ExternalOutput").ap()
    build(nc, aps, out)
    r = run_bass_kernel_spmd(nc, [{"in_" + k: a for k, a in arrays.items()}], core_ids=[0])
    return r.results[0]["out_0"].reshape(BATCH, SEQ, D)
```
